# Optimizing a Trainium2 kernel written in Bass

```python
import numpy as np
import jax
import jax.numpy as jnp

def _softmax(x, axis=-1):
    return jax.nn.softmax(x, axis=axis)

def _gelu(x):
    return jax.nn.gelu(x, approximate=True)

def _silu(x):
    return jax.nn.silu(x)

def _sigmoid(x):
    return jax.nn.sigmoid(x)

def _layernorm(x, axis=-1, eps=1e-05):
    m = jnp.mean(x, axis=axis, keepdims=True)
    v = jnp.var(x, axis=axis, keepdims=True)
    return (x - m) / jnp.sqrt(v + eps)

def _scatter_add(tgt, idx, src, axis=0):
    return tgt.at[idx].add(src)

def _segment_sum(src, seg, n):
    return jax.ops.segment_sum(src, seg, n)
kernel_name = 'mk_gps_d2_gnn_r32_f13a30'

def setup_inputs(seed: int=0):
    np.random.seed(seed)
    _w = jnp.asarray

    def _rec_inputs():
        import jax
        import jax.numpy as jnp
        _gk = jax.random.key(seed)
        x = -0.0002117 + 1 * jax.random.normal(jax.random.fold_in(_gk, 1), (3125, 256), jnp.float32)
        src = jax.random.randint(jax.random.fold_in(_gk, 2), (50000,), 0, 3125, jnp.int32)
        dst = jnp.minimum((3125 * jax.random.uniform(jax.random.fold_in(_gk, 3), (50000,)) ** 2.0).astype(jnp.int32), 99999)
        _o = jnp.argsort(dst, stable=True)
        src = src[_o]
        dst = dst[_o]
        edge_weight = jax.random.uniform(jax.random.fold_in(_gk, 13), (50000,), jnp.float32, 0.0, 1)
        return (x, src, dst, edge_weight)
    x, src, dst, edge_weight = _rec_inputs()

    def _L0_gnn_setup():
        import jax, jax.numpy as jnp
        import numpy as np
        N_NODES = 3125
        N_EDGES = 100000
        IN_DIM = 256
        OUT_DIM = 256
        key = jax.random.key(seed)
        k1, k2, k3, k4, k5 = jax.random.split(key, 5)
        x = jax.random.normal(k1, (N_NODES, IN_DIM), dtype=jnp.float32)
        limit = np.sqrt(6.0 / (IN_DIM + OUT_DIM)).astype(np.float32)
        weight = jax.random.uniform(k2, (IN_DIM, OUT_DIM), dtype=jnp.float32, minval=-limit, maxval=limit)
        values = jax.random.uniform(k3, (N_EDGES,), dtype=jnp.float32)
        row = jnp.sort(jax.random.randint(k4, (N_EDGES,), 0, N_NODES, dtype=jnp.int32))
        col = jax.random.randint(k5, (N_EDGES,), 0, N_NODES, dtype=jnp.int32)
        return {'x': x, 'weight': weight, 'values': values, 'row': row, 'col': col}
    _L0_gnn_all = _L0_gnn_setup()
    _L0_gnn_in = {k: v for k, v in _L0_gnn_all.items() if k in ('weight',)}
    del _L0_gnn_all

    def _L0_mix_setup():
        import jax, jax.numpy as jnp
        import numpy as np
        BN_EPS = 1e-05
        key = jax.random.key(seed)
        ks = jax.random.split(key, 4)
        B, N, D = (8, 256, 256)
        outD = 256
        s = 1.0 / np.sqrt(D)
        return {'feature': jax.random.normal(ks[0], (B, N, D), dtype=jnp.float32), 'W_qk': jax.random.normal(ks[1], (2, D, D), dtype=jnp.float32) * s, 'b_qk': jnp.zeros((2, D), dtype=jnp.float32), 'W_v': jax.random.normal(ks[2], (D, outD), dtype=jnp.float32) * s, 'b_v': jnp.zeros((outD,), dtype=jnp.float32), 'gamma': jnp.ones((D,), dtype=jnp.float32), 'beta': jnp.zeros((D,), dtype=jnp.float32)}
    _L0_mix_all = _L0_mix_setup()
    _L0_mix_in = {k: v for k, v in _L0_mix_all.items() if k in ('W_qk', 'b_qk', 'W_v', 'b_v', 'gamma', 'beta')}
    del _L0_mix_all

    def _L0_ffn_setup():
        import jax, jax.numpy as jnp
        import numpy as np
        B, K, D = (512, 16, 256)
        E = 32
        H = int(D * 0.25)
        key = jax.random.key(seed)
        ks = jax.random.split(key, 7)
        d_rs = D ** (-0.5)
        h_rs = H ** (-0.5)
        x = jax.random.normal(ks[0], (B, K, D), dtype=jnp.float32)
        router_w = jax.random.uniform(ks[1], (E, D), jnp.float32, -d_rs, d_rs)
        router_b = jax.random.uniform(ks[2], (E,), jnp.float32, -d_rs, d_rs)
        W1 = jax.random.uniform(ks[3], (E, D, H), jnp.float32, -h_rs, h_rs)
        b1 = jax.random.uniform(ks[4], (E, H), jnp.float32, -h_rs, h_rs)
        W2 = jax.random.uniform(ks[5], (E, H, D), jnp.float32, -d_rs, d_rs)
        b2 = jax.random.uniform(ks[6], (E, D), jnp.float32, -d_rs, d_rs)
        return {'x': x, 'router_w': router_w, 'router_b': router_b, 'W1': W1, 'b1': b1, 'W2': W2, 'b2': b2}
    _L0_ffn_all = _L0_ffn_setup()
    _L0_ffn_in = {k: v for k, v in _L0_ffn_all.items() if k in ('router_w', 'router_b', 'W1', 'b1', 'W2', 'b2')}
    del _L0_ffn_all

    def _L1_gnn_setup():
        import jax, jax.numpy as jnp
        import numpy as np
        N_NODES = 50000
        N_EDGES = 25000
        IN_CH = 256
        HID_CH = 256
        OUT_CH = 256
        N_LAYERS = 3
        key = jax.random.key(seed)
        ks = jax.random.split(key, 8)
        s_in = 1.0 / np.sqrt(IN_CH)
        s_h = 1.0 / np.sqrt(HID_CH)
        return {'x': jax.random.normal(ks[0], (N_NODES, IN_CH), dtype=jnp.float32), 'W_in': jax.random.normal(ks[1], (IN_CH, HID_CH), dtype=jnp.float32) * s_in, 'b_in': jnp.zeros((HID_CH,), dtype=jnp.float32), 'W_agg': jax.random.normal(ks[2], (N_LAYERS, HID_CH, HID_CH), dtype=jnp.float32) * s_h, 'W_self': jax.random.normal(ks[3], (N_LAYERS, HID_CH, HID_CH), dtype=jnp.float32) * s_h, 'b_hid': jnp.zeros((N_LAYERS, HID_CH), dtype=jnp.float32), 'W_out': jax.random.normal(ks[4], (HID_CH, OUT_CH), dtype=jnp.float32) * s_h, 'b_out': jnp.zeros((OUT_CH,), dtype=jnp.float32), 'edge_index': jax.random.randint(ks[5], (2, N_EDGES), 0, N_NODES, dtype=jnp.int64)}
    _L1_gnn_all = _L1_gnn_setup()
    _L1_gnn_in = {k: v for k, v in _L1_gnn_all.items() if k in ('W_in', 'b_in', 'W_agg', 'W_self', 'b_hid', 'W_out', 'b_out')}
    del _L1_gnn_all

    def _L1_mix_setup():
        import math
        import jax, jax.numpy as jnp
        import numpy as np
        EPS_DIV = 1e-07
        EPS_NORM = 1e-12

        def _l2_normalize(x, axis):
            n = jnp.sqrt(jnp.sum(x * x, axis=axis, keepdims=True))
            return x / jnp.maximum(n, EPS_NORM)
        key = jax.random.key(seed)
        ks = jax.random.split(key, 5)
        b, N, C = (8, 128, 256)
        x = jax.random.normal(ks[0], (b, N, C), dtype=jnp.float32)
        W_qkv = jax.random.normal(ks[1], (C, 3 * C), dtype=jnp.float32) * (1.0 / math.sqrt(C))
        b_qkv = jax.random.normal(ks[2], (3 * C,), dtype=jnp.float32) * 0.02
        W_out = jax.random.normal(ks[3], (C, C), dtype=jnp.float32) * (1.0 / math.sqrt(C))
        b_out = jax.random.normal(ks[4], (C,), dtype=jnp.float32) * 0.02
        return {'x': x, 'W_qkv': W_qkv, 'b_qkv': b_qkv, 'W_out': W_out, 'b_out': b_out}
    _L1_mix_all = _L1_mix_setup()
    _L1_mix_in = {k: v for k, v in _L1_mix_all.items() if k in ('W_qkv', 'b_qkv', 'W_out', 'b_out')}
    del _L1_mix_all

    def _L1_ffn_setup():
        import math
        import jax, jax.numpy as jnp
        import numpy as np
        CAPACITY_FACTOR = 1.25
        TOP_K = 2
        LN_EPS = 1e-05

        def _layer_norm(x, gamma, beta):
            mu = jnp.mean(x, axis=-1, keepdims=True)
            var = jnp.var(x, axis=-1, keepdims=True)
            return (x - mu) * jax.lax.rsqrt(var + LN_EPS) * gamma + beta
        key = jax.random.key(seed)
        ks = jax.random.split(key, 4)
        B, S, D, F, E = (8, 128, 256, 512, 8)
        x = jax.random.normal(ks[0], (B, S, D), dtype=jnp.float32)
        Wr = jax.random.normal(ks[1], (D, E), dtype=jnp.float32) / np.sqrt(D)
        br = jnp.zeros((E,), jnp.float32)
        W1 = jax.random.normal(ks[2], (E, D, F), dtype=jnp.float32) / np.sqrt(D)
        b1 = jnp.zeros((E, F), jnp.float32)
        W2 = jax.random.normal(ks[3], (E, F, D), dtype=jnp.float32) / np.sqrt(F)
        b2 = jnp.zeros((E, D), jnp.float32)
        gamma = jnp.ones((D,), jnp.float32)
        beta = jnp.zeros((D,), jnp.float32)
        return {'x': x, 'Wr': Wr, 'br': br, 'W1': W1, 'b1': b1, 'W2': W2, 'b2': b2, 'gamma': gamma, 'beta': beta}
    _L1_ffn_all = _L1_ffn_setup()
    _L1_ffn_in = {k: v for k, v in _L1_ffn_all.items() if k in ('Wr', 'br', 'W1', 'b1', 'W2', 'b2', 'gamma', 'beta')}
    del _L1_ffn_all
    return {'x': x, 'src': src, 'dst': dst, 'edge_weight': edge_weight, 'L0_gnn_weight': _L0_gnn_in['weight'], 'L0_mix_W_qk': _L0_mix_in['W_qk'], 'L0_mix_b_qk': _L0_mix_in['b_qk'], 'L0_mix_W_v': _L0_mix_in['W_v'], 'L0_mix_b_v': _L0_mix_in['b_v'], 'L0_mix_gamma': _L0_mix_in['gamma'], 'L0_mix_beta': _L0_mix_in['beta'], 'L0_ffn_router_w': _L0_ffn_in['router_w'], 'L0_ffn_router_b': _L0_ffn_in['router_b'], 'L0_ffn_W1': _L0_ffn_in['W1'], 'L0_ffn_b1': _L0_ffn_in['b1'], 'L0_ffn_W2': _L0_ffn_in['W2'], 'L0_ffn_b2': _L0_ffn_in['b2'], 'L1_gnn_W_in': _L1_gnn_in['W_in'], 'L1_gnn_b_in': _L1_gnn_in['b_in'], 'L1_gnn_W_agg': _L1_gnn_in['W_agg'], 'L1_gnn_W_self': _L1_gnn_in['W_self'], 'L1_gnn_b_hid': _L1_gnn_in['b_hid'], 'L1_gnn_W_out': _L1_gnn_in['W_out'], 'L1_gnn_b_out': _L1_gnn_in['b_out'], 'L1_mix_W_qkv': _L1_mix_in['W_qkv'], 'L1_mix_b_qkv': _L1_mix_in['b_qkv'], 'L1_mix_W_out': _L1_mix_in['W_out'], 'L1_mix_b_out': _L1_mix_in['b_out'], 'L1_ffn_Wr': _L1_ffn_in['Wr'], 'L1_ffn_br': _L1_ffn_in['br'], 'L1_ffn_W1': _L1_ffn_in['W1'], 'L1_ffn_b1': _L1_ffn_in['b1'], 'L1_ffn_W2': _L1_ffn_in['W2'], 'L1_ffn_b2': _L1_ffn_in['b2'], 'L1_ffn_gamma': _L1_ffn_in['gamma'], 'L1_ffn_beta': _L1_ffn_in['beta']}

def reference(x, src, dst, edge_weight, L0_gnn_weight, L0_mix_W_qk, L0_mix_b_qk, L0_mix_W_v, L0_mix_b_v, L0_mix_gamma, L0_mix_beta, L0_ffn_router_w, L0_ffn_router_b, L0_ffn_W1, L0_ffn_b1, L0_ffn_W2, L0_ffn_b2, L1_gnn_W_in, L1_gnn_b_in, L1_gnn_W_agg, L1_gnn_W_self, L1_gnn_b_hid, L1_gnn_W_out, L1_gnn_b_out, L1_mix_W_qkv, L1_mix_b_qkv, L1_mix_W_out, L1_mix_b_out, L1_ffn_Wr, L1_ffn_br, L1_ffn_W1, L1_ffn_b1, L1_ffn_W2, L1_ffn_b2, L1_ffn_gamma, L1_ffn_beta):
    import jax
    import jax.numpy as jnp

    def _L0_gnn_ref(x, weight, values, row, col):
        import jax, jax.numpy as jnp
        import numpy as np
        N_NODES = 3125
        N_EDGES = 100000
        IN_DIM = 256
        OUT_DIM = 256
        h = x @ weight
        msgs = values[:, None] * h[col]
        out = jax.ops.segment_sum(msgs, row, num_segments=N_NODES)
        return out

    def _L0_mix_ref(feature, W_qk, b_qk, W_v, b_v, gamma, beta):
        import jax, jax.numpy as jnp
        import numpy as np
        BN_EPS = 1e-05
        QK = jnp.einsum('bnd,kde->bkne', feature, W_qk) + b_qk[None, :, None, :]
        value = jnp.einsum('bnd,de->bne', feature, W_v) + b_v
        query = QK[:, 0]
        key = QK[:, 1]
        sm = jax.nn.softmax(key, axis=1)
        lam = jnp.einsum('bnd,bne->bde', sm, value)
        mean = jnp.mean(lam, axis=(0, 2), keepdims=True)
        var = jnp.var(lam, axis=(0, 2), keepdims=True)
        bn = (lam - mean) * jax.lax.rsqrt(var + BN_EPS)
        bn = bn * gamma[None, :, None] + beta[None, :, None]
        return jnp.einsum('bnd,bde->bne', query, bn)

    def _L0_ffn_ref(x, router_w, router_b, W1, b1, W2, b2):
        import jax, jax.numpy as jnp
        import numpy as np
        B, K, D = (512, 16, 256)
        E = 32
        H = int(D * 0.25)
        xf = x.reshape(-1, D)
        logits = xf @ router_w.T + router_b
        idx = jnp.argmax(logits, axis=-1)
        w1t = jnp.take(W1, idx, axis=0)
        h = jnp.einsum('nd,ndh->nh', xf, w1t) + jnp.take(b1, idx, axis=0)
        h = jax.nn.relu(h)
        w2t = jnp.take(W2, idx, axis=0)
        out = jnp.einsum('nh,nhd->nd', h, w2t) + jnp.take(b2, idx, axis=0)
        out = jax.nn.relu(out)
        return out.reshape(x.shape)

    def _L1_gnn_ref(x, W_in, b_in, W_agg, W_self, b_hid, W_out, b_out, edge_index):
        import jax, jax.numpy as jnp
        import numpy as np
        N_NODES = 50000
        N_EDGES = 25000
        IN_CH = 256
        HID_CH = 256
        OUT_CH = 256
        N_LAYERS = 3
        n = x.shape[0]
        dst = edge_index[0]
        src = edge_index[1]
        n_layers = W_agg.shape[0]
        h = x @ W_in + b_in
        deg = jax.ops.segment_sum(jnp.ones_like(dst, dtype=h.dtype), dst, num_segments=n)
        deg = jnp.maximum(deg, 1.0)[:, None]
        for l in range(n_layers):
            agg = jax.ops.segment_sum(h[src], dst, num_segments=n) / deg
            h = jax.nn.relu(agg @ W_agg[l] + h @ W_self[l] + b_hid[l])
        return h @ W_out + b_out

    def _L1_mix_ref(x, W_qkv, b_qkv, W_out, b_out):
        import math
        import jax, jax.numpy as jnp
        import numpy as np
        EPS_DIV = 1e-07
        EPS_NORM = 1e-12

        def _l2_normalize(x, axis):
            n = jnp.sqrt(jnp.sum(x * x, axis=axis, keepdims=True))
            return x / jnp.maximum(n, EPS_NORM)
        b, N, C = x.shape
        qkv = x @ W_qkv + b_qkv
        q, k, v = jnp.split(qkv, 3, axis=2)
        q = q - jnp.mean(q, axis=2, keepdims=True)
        k = k - jnp.mean(k, axis=2, keepdims=True)
        q2 = q * q
        k2 = k * k
        q2s = jnp.sum(q2, axis=2, keepdims=True)
        k2s = jnp.sum(k2, axis=2, keepdims=True)
        k2 = _l2_normalize(k2 / (k2s + EPS_DIV), axis=-2)
        q2 = _l2_normalize(q2 / (q2s + EPS_DIV), axis=-1)
        kv = jnp.einsum('bnc,bnd->bcd', k2, v)
        t2 = jnp.einsum('bnc,bcd->bnd', q2, kv) / math.sqrt(N)
        attn = v + t2
        return attn @ W_out + b_out

    def _L1_ffn_ref(x, Wr, br, W1, b1, W2, b2, gamma, beta):
        import math
        import jax, jax.numpy as jnp
        import numpy as np
        CAPACITY_FACTOR = 1.25
        TOP_K = 2
        LN_EPS = 1e-05

        def _layer_norm(x, gamma, beta):
            mu = jnp.mean(x, axis=-1, keepdims=True)
            var = jnp.var(x, axis=-1, keepdims=True)
            return (x - mu) * jax.lax.rsqrt(var + LN_EPS) * gamma + beta
        B, S, D = x.shape
        E = Wr.shape[1]
        N = B * S
        K = TOP_K
        logits = jnp.mean(x, axis=1) @ Wr + br
        routing_weights = jax.nn.softmax(logits, axis=-1)
        capacity = float(math.ceil(N * CAPACITY_FACTOR / E))
        expected_loads = routing_weights.sum(axis=0) * (N / B)
        scale = jnp.where(expected_loads > capacity, capacity / expected_loads, 1.0)
        routing_weights = jax.nn.softmax(routing_weights * scale, axis=-1)
        rw_tok = jnp.broadcast_to(routing_weights[:, None, :], (B, S, E)).reshape(N, E)
        top_w, top_i = jax.lax.top_k(rw_tok, K)
        top_w = jax.nn.softmax(top_w, axis=-1)
        xf = x.reshape(N, D)
        h = jax.nn.gelu(jnp.einsum('nd,edf->enf', xf, W1) + b1[:, None, :], approximate=False)
        y = jnp.einsum('enf,efd->end', h, W2) + b2[:, None, :]
        w_dense = jnp.zeros((N, E), x.dtype).at[jnp.arange(N)[:, None], top_i].add(top_w)
        out = jnp.einsum('ne,end->nd', w_dense, y).reshape(B, S, D)
        out = _layer_norm(out + x, gamma, beta)
        return out
    edge_index = jnp.stack([src, dst])
    xn = _layernorm(x, axis=-1)
    x = x + _L0_gnn_ref(xn, L0_gnn_weight, edge_weight, src, dst) + _L0_mix_ref(xn[None], L0_mix_W_qk, L0_mix_b_qk, L0_mix_W_v, L0_mix_b_v, L0_mix_gamma, L0_mix_beta)[0]
    x = x + _L0_ffn_ref(_layernorm(x, axis=-1)[None], L0_ffn_router_w, L0_ffn_router_b, L0_ffn_W1, L0_ffn_b1, L0_ffn_W2, L0_ffn_b2)[0]
    xn = _layernorm(x, axis=-1)
    x = x + _L1_gnn_ref(xn, L1_gnn_W_in, L1_gnn_b_in, L1_gnn_W_agg, L1_gnn_W_self, L1_gnn_b_hid, L1_gnn_W_out, L1_gnn_b_out, edge_index) + _L1_mix_ref(xn[None], L1_mix_W_qkv, L1_mix_b_qkv, L1_mix_W_out, L1_mix_b_out)[0]
    x = x + _L1_ffn_ref(_layernorm(x, axis=-1)[None], L1_ffn_Wr, L1_ffn_br, L1_ffn_W1, L1_ffn_b1, L1_ffn_W2, L1_ffn_b2, L1_ffn_gamma, L1_ffn_beta)[0]
    return x

_drawn_inputs = setup_inputs


def setup_inputs(seed=0):
    import zlib

    import numpy as np

    out = dict(_drawn_inputs(seed))
    spreads = {'L0_mix_b_qk': (0.0, 0.1),
     'L0_mix_b_v': (0.0, 0.1),
     'L0_mix_gamma': (1.0, 0.2),
     'L0_mix_beta': (0.0, 0.1),
     'L1_gnn_b_in': (0.0, 2.0),
     'L1_gnn_b_hid': (0.0, 0.8),
     'L1_gnn_b_out': (0.0, 0.8),
     'L1_ffn_br': (0.0, 0.8),
     'L1_ffn_b1': (0.0, 2.0),
     'L1_ffn_b2': (0.0, 2.0),
     'L1_ffn_gamma': (1.0, 0.6),
     'L1_ffn_beta': (0.0, 0.8)}
    factors = {'L0_ffn_router_w': 6.89,
     'L0_ffn_router_b': 8.0,
     'L0_ffn_W1': 8.0,
     'L0_ffn_b1': 8.0,
     'L0_ffn_W2': 6.59,
     'L0_ffn_b2': 43.493,
     'L1_gnn_W_in': 3.573,
     'L1_mix_b_qkv': 6.307,
     'L1_mix_b_out': 57.17,
     'L1_ffn_W1': 2.683}
    for name, (base, spread) in spreads.items():
        noise = np.random.default_rng([zlib.crc32(name.encode()), seed]).standard_normal(out[name].shape)
        drawn = base * np.exp(spread * noise) if base else spread * noise
        out[name] = jnp.asarray(drawn.astype(out[name].dtype))
    for name, factor in factors.items():
        out[name] = (out[name] * factor).astype(out[name].dtype)
    return out
```

```python
from contextlib import ExitStack

import concourse.bass as bass
from concourse import mybir

F32 = mybir.dt.float32
BF16 = mybir.dt.bfloat16
I32 = mybir.dt.int32
U32 = mybir.dt.uint32
ALU = mybir.AluOpType
ACT = mybir.ActivationFunctionType
AX = mybir.AxisListType.X

P = 128
N, D, E = 3125, 256, 50000
KD = D // P
T = -(-N // P)
TAIL = N - (T - 1) * P
NP = T * P
EC = -(-E // P)
EREST = E - (EC - 1) * P
U = 32
NT = -(-((E + T * (P - 1)) // P) // U) * U
RING = 16
MRING = 8
SLOTS = 4
AHEAD = 4
AW = D + 1
EX, H0 = 32, 64
FT = -(-((N + EX * (P - 1)) // P) // 4) * 4
EX1, H1 = 8, 512
J1 = 2 * H1 // P
EPS = 1e-5
CAPACITY = float(-(-N * 5 // (4 * EX1)))
CH = [(c * 512, min(512, N - c * 512)) for c in range(-(-N // 512))]
CHP = [(c * 512, min(512, NP - c * 512)) for c in range(-(-NP // 512))]
TG = [(0, 7), (7, 7), (14, 6), (20, 5)]


def gps_kernel(nc, x, src, dst, edge_weight, gnn0_W, mix0_Wqk, mix0_bqk, mix0_Wv, mix0_bv, mix0_gamma,
               mix0_beta, ffn0_rw, ffn0_rb, ffn0_W1, ffn0_b1, ffn0_W2, ffn0_b2, gnn1_Win, gnn1_bin,
               gnn1_Wagg, gnn1_Wself, gnn1_bhid, gnn1_Wout, gnn1_bout, mix1_Wqkv, mix1_bqkv, mix1_Wout,
               mix1_bout, ffn1_Wr, ffn1_br, ffn1_W1, ffn1_b1, ffn1_W2, ffn1_b2, ffn1_gamma, ffn1_beta, out):
    records_d = nc.dram_tensor("records_d", [P, NT, 3], F32).ap()
    rows_d = nc.dram_tensor("rows_d", [NP, D], F32).ap()
    xs_d = nc.dram_tensor("xs_d", [FT * P, D], F32).ap()
    ys_d = nc.dram_tensor("ys_d", [FT * P, D], F32).ap()

    with ExitStack() as ctx:
        def sb(name, shape, dt=F32):
            return ctx.enter_context(nc.sbuf_tensor(name, shape, dt))

        sems = {}

        def sem(name):
            if name not in sems:
                sems[name] = ctx.enter_context(nc.semaphore(name))
            return sems[name]

        x_sb = sb("x_sb", [P, T, D])
        rows = sb("rows", [P, T, D])
        xT = sb("xT", [P, KD, NP])
        hT = sb("hT", [P, KD, NP])
        vals = sb("vals", [P, T, D])
        accF = sb("accF", [P, (T + 1) * AW])
        acc = accF[:, :].rearrange("p (t w) -> p t w", w=AW)
        recs = sb("recs", [P, NT + AHEAD, 3])
        wA = sb("wA", [P, 4096])
        wB = sb("wB", [P, 2048])
        gF = sb("gF", [P, 2056])
        g = rows[:, :, :].rearrange("p t d -> p (t d)")[:, 0:RING * AW].rearrange("p (s w) -> p s w", w=AW)
        oh = sb("oh", [P, MRING, P])
        xt = sb("xt", [P, 2, KD, P])
        idx = sb("idx", [P, U], I32)
        srt = sb("srt", [P, U, 3])
        misc = sb("misc", [P, 1280])
        rowb = misc[0:1, :]
        bins = misc[32:33, 0:NT].bitcast(I32)
        iotaT = misc[32:33, NT:2 * NT]
        ident = sb("ident", [P, P])
        tri = sb("tri", [P, P])
        ones = sb("ones", [P, P])
        iota = sb("iota", [P, P])
        rowok = sb("rowok", [P, 1])
        rowid = sb("rowid", [P, 1])
        small = sb("small", [P, 768])
        stats = sb("stats", [P, T, 6])
        mv = sb("mv", [P, T, 2])
        ln = sb("ln", [P, 4, T])
        bcast = sb("bcast", [P, D])
        banks = [ctx.enter_context(nc.psum_tensor(f"bank{i}", [P, 512], F32)) for i in range(8)]

        def cols(a, n):
            return small[:, a:a + n]
        rowtot, pref, tot, cnt, endt, off = (cols(32 * i, 32) for i in range(6))
        colb = cols(192, 16)
        invdeg = cols(208, T)
        kmax, ksum, kinv = cols(240, 2), cols(242, 2), cols(244, 2)
        bnst, bnmv, bnt = cols(248, 12), cols(260, 4), cols(264, 8)
        qs, qk, q4, sq = cols(272, 2 * T), cols(322, 2 * T), cols(372, T), cols(397, T)
        posI = cols(424, 32).bitcast(I32)
        negm = cols(456, 2 * T)
        kn = cols(506, 6)
        top = cols(512, 96)
        cntI = cols(640, 32).bitcast(I32)
        eidx = cols(672, 64).bitcast(I32)

        block = ctx.enter_context(nc.Block())

        ohs = accF[:, 0:T * EC // 2 + 1].bitcast(BF16)[:, 0:T * EC].rearrange("p (b j) -> p b j", j=EC)
        o = T * EC // 2 + 2
        srcI, dstI, wE, tmpI = (accF[:, o + EC * i:o + EC * (i + 1)] for i in range(4))
        srcI, dstI, tmpI = srcI.bitcast(I32), dstI.bitcast(I32), tmpI.bitcast(I32)
        EP = EC + 1
        binF, scanF, posF, prodF, oneF = (gF[:, EP * i:EP * i + EC] for i in range(5))
        addr = gF[:, EP * 2:EP * 3]
        edge = wB[:, 0:3 * EP].rearrange("p (j c) -> p j c", c=3)

        W0V = wA[:, 0:1024].rearrange("p (k n) -> p k n", k=KD)
        Wk = wA[:, 1024:1536].rearrange("p (k n) -> p k n", k=KD)
        Wq = wA[:, 1536:2048].rearrange("p (k n) -> p k n", k=KD)
        WqT = wA[:, 2048:2560].rearrange("p (k n) -> p k n", k=KD)
        bn = wA[:, 2560:3072].rearrange("p (k n) -> p k n", k=KD)
        Mx = wA[:, 3072:3584].rearrange("p (k n) -> p k n", k=KD)
        rw = wA[0:EX, 3584:3840]
        rwT = wA[:, 3840:3904].rearrange("p (k n) -> p k n", k=KD)
        f_x = accF[:, 0:1024].rearrange("p (s n) -> p s n", s=4)
        f_w1 = accF[:, 1024:1536].rearrange("p (s k n) -> p s k n", s=4, k=KD)
        f_w2 = accF[0:H0, 1536:2560].rearrange("p (s n) -> p s n", s=4)
        f_b2 = accF[0:1, 2560:3584].rearrange("p (s n) -> p s n", s=4)
        f_b1 = accF[0:H0, 3584:3588]
        f_xT = accF[:, 3588:4100].rearrange("p (s k n) -> p s k n", s=2, k=KD)
        f_h = accF[0:H0, 4100:4356].rearrange("p (s n) -> p s n", s=2)
        f_y = accF[:, 4356:5380].rearrange("p (s n) -> p s n", s=4)
        r_oh = wB[:, 0:EX * T].rearrange("p (b t) -> p b t", t=T)
        r_sc = wB[:, 800:1600].rearrange("p (b t) -> p b t", t=T)
        r_lg = oh[:, 0:7, :].rearrange("p a b -> p (a b)")[:, 0:T * EX].rearrange("p (t b) -> p t b", b=EX)
        r_m8 = gF[:, 0:8 * T].rearrange("p (t e) -> p t e", e=8)
        r_i8 = gF[:, 8 * T:16 * T].bitcast(U32).rearrange("p (t e) -> p t e", e=8)
        r_msk = gF[:, 16 * T:16 * T + EX * T].rearrange("p (b t) -> p b t", t=T)
        r_eid = gF[:, 1400:1400 + T]
        Wio = wA[:, 0:1024].rearrange("p (w k n) -> p w k n", w=2, k=KD)
        Was = wA[:, 1024:4096].rearrange("p (l k n) -> p l k n", l=3, k=KD)
        Wqkv = wB[:, 0:1536].rearrange("p (k n) -> p k n", k=KD)
        Wo1 = wB[:, 1536:2048].rearrange("p (k n) -> p k n", k=KD)
        W1c = wA[:, 0:2 * KD * H1].rearrange("p (e k n) -> p e k n", e=2, k=KD)
        W2c = wA[:, 2048:4096].rearrange("p (j n) -> p j n", n=D)
        gel = hT[:, :, :].rearrange("p k n -> p (k n)")[:, 0:2 * J1 * 384].rearrange("p (s j n) -> p s j n", s=2, j=J1)

        def pt(ap):
            return ap.rearrange("(t p) d -> p t d", p=P)

        def kp(ap):
            return ap.rearrange("(k p) n -> p k n", p=P)

        def row(ap):
            return ap.rearrange("(a n) -> a n", a=1)

        def tw(t):
            return P if t < T - 1 else TAIL

        @block.sync
        def _(sp):
            ld = sem("edges_loaded")
            sp.wait_ge(sem("edge_pad_set"), 3)
            for tile, a in ((srcI, src), (dstI, dst), (wE, edge_weight)):
                sp.dma_start(tile[:, 0:EC - 1], a[0:(EC - 1) * P].rearrange("(p j) -> p j", p=P)).then_inc(ld, 16)
                sp.dma_start(tile[0:EREST, EC - 1:EC],
                             a[(EC - 1) * P:E].rearrange("(p j) -> p j", j=1)).then_inc(ld, 16)
            sp.wait_ge(sem("x_pad_set"), 1)
            sp.dma_start(x_sb[:, 0:T - 1, :], pt(x[0:(T - 1) * P, :])).then_inc(sem("x_loaded"), 16)
            sp.dma_start(x_sb[0:TAIL, T - 1, :], x[(T - 1) * P:N, :]).then_inc(sem("x_loaded"), 16)
            w = sem("w_block0")
            sp.dma_start(W0V[:, :, 0:D], kp(gnn0_W)).then_inc(w, 16)
            sp.dma_start(W0V[:, :, D:2 * D], kp(mix0_Wv)).then_inc(w, 16)
            sp.dma_start(Wk, kp(mix0_Wqk[1])).then_inc(w, 16)
            sp.dma_start(Wq, kp(mix0_Wqk[0])).then_inc(w, 16)
            sp.dma_start(colb[:, 0:2], mix0_bqk[1].rearrange("(k p) -> p k", p=P), allow_slow_non_contiguous=True).then_inc(w, 16)
            sp.dma_start(colb[:, 2:4], mix0_bqk[0].rearrange("(k p) -> p k", p=P), allow_slow_non_contiguous=True).then_inc(w, 16)
            sp.dma_start(colb[:, 4:6], mix0_gamma.rearrange("(k p) -> p k", p=P), allow_slow_non_contiguous=True).then_inc(w, 16)
            sp.dma_start(colb[:, 6:8], mix0_beta.rearrange("(k p) -> p k", p=P), allow_slow_non_contiguous=True).then_inc(w, 16)
            sp.dma_start(bcast[:, :], row(mix0_bv).to_broadcast([P, D])).then_inc(w, 16)
            sp.dma_start(rw, ffn0_rw).then_inc(w, 16)
            sp.dma_start(rowb[0:1, 0:EX], row(ffn0_rb)).then_inc(w, 16)
            for a, n in TG:
                sp.wait_ge(sem("rows_ready"), a + n)
                sp.dma_start(pt(rows_d)[:, a:a + n, :], rows[:, a:a + n, :]).then_inc(sem("rows_stored"), 16)
            sp.wait_ge(sem("sort_part0"), 16 * (8 * (EC // U) + EC % U))
            for q in (1, 2, 3):
                sp.wait_ge(sem(f"sort_part{q}"), 16 + 16 * 8 * (EC // U))
            sp.dma_start(recs[:, 0:NT, :], records_d).then_inc(sem("recs_loaded"), 16)
            sp.wait_ge(sem("acc_zero"), 1)
            xs_flat = xs_d.rearrange("(p a) d -> p (a d)", p=P)
            q = FT * D // 4
            for i in range(4):
                sp.dma_start(xs_flat[:, i * q:(i + 1) * q], accF[:, 0:q]).then_inc(sem(f"f_stored{i}"), 16)
            sp.wait_ge(sem("tokens_scattered"), 16 * T)
            sp.wait_ge(sem("expert_table"), 1)
            with sp.Fori(0, FT // 4) as it:
                for s in range(4):
                    sp.wait_ge(sem("f_y_done"), it * 4 + (s + 1))
                    e = sp.value_load(eidx[32:33, bass.ds(it * 4 + s, 1)], min_val=0, max_val=EX - 1)
                    f = sem(f"f_loaded{s}")
                    sp.dma_start(f_x[:, s, :], xs_d[bass.ds((it * 4 + s) * P, P), :]).then_inc(f, 16)
                    sp.dma_start(f_w1[:, s], ffn0_W1[bass.ds(e, 1)].rearrange("a (k p) n -> p (a k) n", p=P)).then_inc(f, 16)
                    sp.dma_start(f_w2[:, s, :], ffn0_W2[bass.ds(e, 1)].rearrange("a p n -> (a p) n")).then_inc(f, 16)
                    sp.dma_start(f_b1[:, s:s + 1], ffn0_b1[bass.ds(e, 1)].rearrange("a (p j) -> (a p) j", j=1)).then_inc(f, 16)
                    sp.dma_start(f_b2[:, s, :], ffn0_b2[bass.ds(e, 1)]).then_inc(f, 16)
            w = sem("w_block1")
            sp.wait_ge(sem("f_y_done"), 4 + FT)
            sp.dma_start(Wio[:, 0], kp(gnn1_Win)).then_inc(w, 16)
            sp.dma_start(Wio[:, 1], kp(gnn1_Wout)).then_inc(w, 16)
            for l in range(3):
                sp.dma_start(Was[:, l, :, 0:D], kp(gnn1_Wagg[l])).then_inc(w, 16)
                sp.dma_start(Was[:, l, :, D:2 * D], kp(gnn1_Wself[l])).then_inc(w, 16)
            sp.dma_start(colb[:, 8:10], gnn1_bin.rearrange("(k p) -> p k", p=P), allow_slow_non_contiguous=True).then_inc(w, 16)
            sp.wait_ge(sem("pos_ready"), 1)
            sp.dma_start(Wqkv, kp(mix1_Wqkv)).then_inc(w, 16)
            sp.dma_start(Wo1, kp(mix1_Wout)).then_inc(w, 16)
            sp.dma_start(rowb[0:1, 0:768], row(mix1_bqkv)).then_inc(w, 16)
            sp.dma_start(rowb[0:1, 768:1024], row(gnn1_bout)).then_inc(w, 16)
            sp.dma_start(rowb[0:1, 1024:1280], row(mix1_bout)).then_inc(w, 16)
            for l in range(3):
                if l > 0:
                    sp.wait_ge(sem("self_ready"), l)
                    sp.wait_ge(sem("agg_gathered"), l + 1)
                else:
                    sp.wait_ge(sem("v_bias_used"), 1)
                sp.dma_start(bcast[:, :], row(gnn1_bhid[l]).to_broadcast([P, D])).then_inc(sem("bhid_loaded"), 16)
                for a, n in TG:
                    sp.wait_ge(sem("rows_ready"), (l + 1) * T + a + n)
                    sp.dma_start(pt(rows_d)[:, a:a + n, :], rows[:, a:a + n, :]).then_inc(sem("rows_stored"), 16)
            sp.wait_ge(sem("lin_taken"), 7 * T)
            sp.dma_start(top[:, 64:80].rearrange("p (k e) -> p k e", e=EX1), kp(ffn1_Wr)).then_inc(sem("wr_loaded"), 16)
            sp.dma_start(rowb[0:1, 512:520], row(ffn1_br)).then_inc(sem("wr_loaded"), 16)
            sp.wait_ge(sem("experts_chosen"), 1)
            w = sem("w_ffn1")
            sp.dma_start(bcast[:, :], row(ffn1_gamma).to_broadcast([P, D])).then_inc(w, 16)
            sp.dma_start(wB[:, 0:D], row(ffn1_beta).to_broadcast([P, D])).then_inc(w, 16)
            for k in range(2):
                e = sp.value_load(eidx[0:1, k:k + 1], min_val=0, max_val=EX1 - 1)
                sp.dma_start(W1c[:, k], ffn1_W1[bass.ds(e, 1)].rearrange("a (k p) n -> p (a k) n", p=P)).then_inc(w, 16)
                sp.dma_start(W2c[:, k * J1 // 2:(k + 1) * J1 // 2, :],
                             ffn1_W2[bass.ds(e, 1)].rearrange("a (j p) n -> p (a j) n", p=P)).then_inc(w, 16)
                sp.dma_start(colb[:, k * J1 // 2:(k + 1) * J1 // 2],
                             ffn1_b1[bass.ds(e, 1)].rearrange("a (j p) -> p (a j)", p=P),
                             allow_slow_non_contiguous=True).then_inc(w, 16)
                sp.dma_start(rowb[0:1, k * D:(k + 1) * D], ffn1_b2[bass.ds(e, 1)]).then_inc(w, 16)
            for t in range(T):
                sp.wait_ge(sem("out_ready"), t + 1)
                sp.dma_start(out[t * P:t * P + tw(t), :], vals[0:tw(t), t, :]).then_inc(sem("out_stored"), 16)
            sp.wait_ge(sem("out_stored"), 16 * T)
            sp.wait_ge(sem("rows_stored"), 16 * 4 * len(TG))

        @block.gpsimd
        def _(pool):
            c = sem("consts")
            nc.gpsimd.iota(iota[:, :], pattern=[[1, P]], base=0, channel_multiplier=0,
                           allow_small_or_imprecise_dtypes=True).then_inc(c, 1)
            pool.wait_ge(c, 1)
            nc.gpsimd.iota(iotaT, pattern=[[1, NT]], base=0, channel_multiplier=0,
                           allow_small_or_imprecise_dtypes=True).then_inc(c, 1)
            pool.wait_ge(c, 2)
            nc.gpsimd.iota(rowid[:, :], pattern=[[0, 1]], base=0, channel_multiplier=1,
                           allow_small_or_imprecise_dtypes=True).then_inc(c, 1)
            nc.gpsimd.memset(ones[:, :], 1.0).then_inc(c, 1)
            nc.gpsimd.memset(ident[:, :], 0.0).then_inc(c, 1)
            pool.wait_ge(c, 5)
            nc.gpsimd.affine_select(out=ident[:, :], in_=ident[:, :], compare_op=ALU.not_equal, fill=1.0, base=0,
                                    pattern=[[-1, P]], channel_multiplier=1).then_inc(c, 1)
            nc.gpsimd.affine_select(out=tri[:, :], in_=ones[:, :], compare_op=ALU.is_gt, fill=0.0, base=0,
                                    pattern=[[1, P]], channel_multiplier=-1).then_inc(c, 1)
            nc.gpsimd.tensor_scalar(rowok[:, :], rowid[:, :], float(TAIL), None, ALU.is_lt).then_inc(c, 1)

            copied = sem("sort_copied")

            def fill(h, j):
                nc.gpsimd.tensor_copy(idx[:, 8 * h:8 * h + 8], addr[:, bass.ds(j, 8)]).then_inc(copied, 1)
                nc.gpsimd.tensor_copy(srt[:, 8 * h:8 * h + 8, :], edge[:, bass.ds(j, 8), :]).then_inc(copied, 1)

            def scatter(u, rows_n, part):
                pool.indirect_dma_start(records_d.rearrange("p t c -> (p t) c"),
                                        bass.IndirectOffsetOnAxis(ap=idx[0:rows_n, u:u + 1], axis=0),
                                        srt[0:rows_n, u, :], None).then_inc(sem(f"sort_part{part}"), 16)

            pool.wait_ge(sem("recs_empty"), 1)
            for q in (1, 2, 3):
                pool.dma_start(records_d[:, NT * (q - 1) // 3:NT * q // 3], recs[:, NT * (q - 1) // 3:NT * q // 3, :])\
                    .then_inc(sem(f"sort_part{q}"), 16)
            for q in (1, 2, 3):
                pool.wait_ge(sem(f"sort_part{q}"), 16)
            pool.wait_ge(sem("edge_slots"), 1)
            fill(0, 0)
            with pool.Fori(0, EC // U) as it:
                for q in range(4):
                    pool.wait_ge(sem(f"sort_part{(q + 1) % 4}"), it * 128 + (128 if q == 3 else 16))
                    fill((q + 1) % 4, it * U + 8 * q + 8)
                    pool.wait_ge(copied, it * 8 + (2 * q + 2))
                    pool.sem_inc(sem("sort_turn"))
                    for u in range(8 * q, 8 * q + 8):
                        scatter(u, P, q)
            pool.wait_ge(copied, 8 * (EC // U) + 2)
            for u in range(EC % U):
                scatter(u, P if u < EC % U - 1 else EREST, 0)

            def gathers(a):
                pool.wait_ge(sem("rows_stored"), 16 * len(TG) * (a + 1))
                with pool.Fori(0, NT // U) as it:
                    for q in range(U // 8):
                        pool.wait_ge(sem("gather_idx"), it * (U // 8) + (a * NT // 8 + q + 1))
                        for u in range(8 * q, 8 * q + 8):
                            if u % 4 == 0:
                                pool.wait_ge(sem("product"), it * U + (a * NT + u + 4 + U - RING))
                                pool.sem_inc(sem("gather_turn"))
                            pool.indirect_dma_start(g[:, u % RING, 0:D], None, rows_d,
                                                    bass.IndirectOffsetOnAxis(ap=idx[:, u:u + 1], axis=0))\
                                .then_inc(sem(f"gathered{u % RING}"), 16)
                pool.wait_ge(sem("product"), U + (a + 1) * NT)
                pool.sem_inc(sem("agg_gathered"))

            gathers(0)
            for s in range(4):
                pool.wait_ge(sem(f"f_stored{s}"), 16)
            pool.wait_ge(sem("pos_ready"), 1)
            for t in range(T):
                pool.indirect_dma_start(xs_d, bass.IndirectOffsetOnAxis(ap=posI[0:tw(t), t:t + 1], axis=0),
                                        rows[0:tw(t), t, :], None).then_inc(sem("tokens_scattered"), 16)
            for s in range(4):
                pool.wait_ge(sem(f"f_stored{s}"), 16 + 16 * FT // 4)
            for t in range(T):
                pool.indirect_dma_start(vals[0:tw(t), t, :], None, ys_d,
                                        bass.IndirectOffsetOnAxis(ap=posI[0:tw(t), t:t + 1], axis=0))\
                    .then_inc(sem("tokens_back"), 16)
            for a in range(1, 4):
                gathers(a)

        @block.scalar
        def _(act):
            step = [0]

            def link(ins):
                step[0] += 1
                ins.then_inc(sem("act_step"), 1)
                act.wait_ge(sem("act_step"), step[0])

            def sqrt_of(k):
                act.wait_ge(sem("var_ready"), k + 1)
                nc.scalar.sqrt(ln[:, 1, :], ln[:, 0, :]).then_inc(sem("sqrt_ready"), 1)

            def take_transposed(s, dest):
                for t in range(T):
                    act.wait_ge(sem("tr_done"), s * T + t + 1)
                    nc.scalar.copy(dest[:, :, t * P:(t + 1) * P],
                                   banks[t % 2][:, 0:2 * P].rearrange("p (k n) -> p k n", k=KD))\
                        .then_inc(sem("tr_taken"), 1)

            def take_linearT(first, chunks, dest, bias):
                for e in range(KD):
                    for c, (a, n) in enumerate(chunks):
                        i = e * len(chunks) + c
                        act.wait_ge(sem("lt_done"), first + i + 1)
                        nc.scalar.activation(dest[:, e, a:a + n], banks[2 + i % 2][:, 0:n], ACT.Identity,
                                             bias=bias[:, e:e + 1]).then_inc(sem("lt_taken"), 1)

            def indices(a):
                with act.Fori(0, NT // U) as it:
                    for q in range(U // 8):
                        act.wait_ge(sem("product"), it * U + (a * NT + 8 * q + 8))
                        nc.scalar.copy(idx[:, 8 * q:8 * q + 8], recs[:, bass.ds(it * U + 8 * q, 8), 0])\
                            .then_inc(sem("gather_idx"), 1)

            sqrt_of(0)
            take_transposed(0, xT)
            take_linearT(0, CH, hT, colb[:, 0:2])
            act.wait_ge(sem("kmax_ready"), 1)
            for k in range(KD):
                nc.scalar.activation(hT[:, k, 0:N], hT[:, k, 0:N], ACT.Exp, bias=kmax[:, k:k + 1],
                                     accum_out=ksum[:, k:k + 1]).then_inc(sem("exp_ready"), 1)
            for t in range(T):
                act.wait_ge(sem("et_done"), t + 1)
                if t >= 2:
                    act.wait_ge(sem("lam_done"), t - 1)
                nc.scalar.copy(xt[0:tw(t), t % 2].rearrange("p k n -> p (k n)"), banks[t % 2][0:tw(t), 0:D])\
                    .then_inc(sem("et_taken"), 1)
            act.wait_ge(sem("bn_var"), 1)
            nc.scalar.sqrt(bnt[:, 2:4], bnt[:, 0:2]).then_inc(sem("bn_sqrt"), 1)
            for k in range(KD):
                act.wait_ge(sem("wqT_done"), k + 1)
                nc.scalar.copy(WqT[:, k, :], banks[k][:, 0:D]).then_inc(sem("wqT_taken"), 1)
            act.wait_ge(sem("mx_done"), KD + 1)
            for k in range(KD):
                nc.scalar.copy(Mx[:, k, :], banks[2 + k][:, 0:D]).then_inc(sem("mx_taken"), 1)
            nc.scalar.copy(rowb[0:1, 256:512], banks[6][0:1, 0:D]).then_inc(sem("mx_taken"), 1)
            act.wait_ge(sem("rwT_done"), 1)
            nc.scalar.copy(rwT, banks[0][:, 0:2 * EX].rearrange("p (k n) -> p k n", k=KD)).then_inc(sem("rwT_taken"), 1)
            act.wait_ge(sem("recs_loaded"), 16)
            indices(0)
            sqrt_of(1)
            take_transposed(1, xT)
            act.sem_inc(sem("f_xt_taken"), 1)
            with act.Fori(0, FT // 4) as it:
                for s in range(4):
                    act.wait_ge(sem("f_xt_done"), it * 4 + (s + 1))
                    act.wait_ge(sem("f_h_done"), it * 4 + (s + 1))
                    nc.scalar.copy(f_xT[:, s % 2], banks[s % 2][:, 0:2 * P].rearrange("p (k n) -> p k n", k=KD))\
                        .then_inc(sem("f_xt_taken"), 1)
                    act.wait_ge(sem("f_h_done"), it * 4 + (s + 3))
                    act.wait_ge(sem("f_o_done"), it * 4 + (s + 1))
                    nc.scalar.activation(f_h[:, s % 2, :], banks[2 + s % 2][0:H0, 0:P], ACT.Relu,
                                         bias=f_b1[:, s:s + 1]).then_inc(sem("f_h_taken"), 1)
                    act.wait_ge(sem("f_y_ready"), it * 4 + (s + 1))
                    act.dma_start(ys_d[bass.ds((it * 4 + s) * P, P), :], f_y[:, s, :]).then_inc(sem(f"f_stored{s}"), 16)
            sqrt_of(2)
            take_transposed(2, xT)
            take_linearT(KD * len(CH), CHP, hT, colb[:, 8:10])
            for t in range(T):
                n = tw(t)
                act.wait_ge(sem("qk_means"), t + 1)
                nc.scalar.activation(rows[:, t, :], banks[2][:, 0:D], ACT.Square,
                                     bias=negm[:, 2 * t:2 * t + 1]).then_inc(sem("q2_ready"), 1)
                if t >= 1:
                    act.wait_ge(sem("kv_done"), t)
                link(nc.scalar.activation(oh[:, 0:2, :].rearrange("p a b -> p (a b)"), banks[2][:, D:2 * D], ACT.Square,
                                          bias=negm[:, 2 * t + 1:2 * t + 2]))
                nc.scalar.copy(oh[:, 2:4, :].rearrange("p a b -> p (a b)"), banks[3][:, 0:D]).then_inc(sem("v_ready"), 1)
                link(nc.scalar.mul(oh[:, 0:2, :].rearrange("p a b -> p (a b)"),
                                   oh[:, 0:2, :].rearrange("p a b -> p (a b)"), qk[:, 2 * t + 1:2 * t + 2]))
                nc.scalar.square(oh[:, 4:6, :].rearrange("p a b -> p (a b)"),
                                 oh[:, 0:2, :].rearrange("p a b -> p (a b)")).then_inc(sem("k2_ready"), 1)
                act.wait_ge(sem("q2_ready"), t + 1)
                nc.scalar.activation(oh[:, 6:8, :].rearrange("p a b -> p (a b)"), rows[:, t, :], ACT.Square,
                                     accum_out=q4[:, t:t + 1]).then_inc(sem("q4_ready"), 1)
                act.wait_ge(sem("vT_done"), t + 1)
                nc.scalar.copy(xt[:, 0], banks[0][:, 0:2 * P].rearrange("p (k n) -> p k n", k=KD)).then_inc(sem("vT_taken"), 1)
            act.wait_ge(sem("q4_sum"), 1)
            nc.scalar.sqrt(sq, q4).then_inc(sem("q4_sqrt"), 1)
            act.wait_ge(sem("kn_sum"), 1)
            nc.scalar.sqrt(kn[:, 2:4], kn[:, 0:2]).then_inc(sem("kn_sqrt"), 1)
            act.wait_ge(sem("kvT_done"), 1)
            for k in range(KD):
                nc.scalar.copy(xt[:, 1, k, :], banks[0][:, k * P:(k + 1) * P]).then_inc(sem("kvT_taken"), 1)
                nc.scalar.copy(xt[:, 0, k, :], banks[1][:, k * P:(k + 1) * P]).then_inc(sem("kvT_taken"), 1)
            act.wait_ge(sem("m2_done"), 1)
            for k in range(KD):
                nc.scalar.copy(oh[:, 2 * k:2 * k + 2, :].rearrange("p a b -> p (a b)"), banks[2 + k][:, 0:D])\
                    .then_inc(sem("m2_taken"), 1)
            for t in range(T):
                act.wait_ge(sem("qT_done"), t + 1)
                if t >= 2:
                    act.wait_ge(sem("mixo_done"), T + t - 1)
                nc.scalar.copy(xt[:, t % 2], banks[t % 2][:, 0:2 * P].rearrange("p (k n) -> p k n", k=KD))\
                    .then_inc(sem("qT_taken"), 1)
            for l in range(3):
                indices(l + 1)
                take_transposed(3 + l, hT)
            sqrt_of(3)
            take_transposed(6, xT)
            act.wait_ge(sem("rt_exp1"), 1)
            nc.scalar.activation(top[0:1, 16:24], top[0:1, 8:16], ACT.Exp).then_inc(sem("rt_exp1d"), 1)
            act.wait_ge(sem("rt_exp2"), 1)
            nc.scalar.activation(top[0:1, 16:24], top[0:1, 8:16], ACT.Exp).then_inc(sem("rt_exp2d"), 1)
            act.wait_ge(sem("rt_exp3"), 1)
            nc.scalar.activation(top[0:1, 50:52], top[0:1, 48:50], ACT.Exp).then_inc(sem("rt_exp3d"), 1)
            act.wait_ge(sem("w_ffn1"), 160)
            i = 0
            for c in range(9):
                n = 384 if c < 8 else P
                for j in range(J1):
                    act.wait_ge(sem("h1_done"), i + 1)
                    if j == 0 and c >= 2:
                        act.wait_ge(sem("y1_done"), 3 * (c - 1))
                    nc.scalar.activation(gel[:, c % 2, j, 0:n], banks[i % 4][:, 0:n], ACT.Gelu,
                                         bias=colb[:, j:j + 1]).then_inc(sem("h1_taken"), 1)
                    i += 1
            sqrt_of(4)

        @block.vector
        def _(dve):
            step = [0]
            V = nc.vector

            def link(ins):
                step[0] += 1
                ins.then_inc(sem("dve_step"), 1)
                dve.wait_ge(sem("dve_step"), step[0])

            def layer_norm(k, source, dest, ready):
                for t in range(T):
                    last = V.bn_stats(stats[:, t, :], source[:, t, :])
                link(last)
                for t in range(T):
                    last = V.bn_aggr(mv[:, t, :], stats[:, t, :])
                link(last)
                V.tensor_scalar(ln[:, 0, :], mv[:, :, 1], EPS, None, ALU.add).then_inc(sem("var_ready"), 1)
                dve.wait_ge(sem("sqrt_ready"), k + 1)
                link(V.reciprocal(ln[:, 2, :], ln[:, 1, :]))
                newton(ln[:, 2, :], ln[:, 0, :], ln[:, 3, :])
                for t in range(T):
                    V.tensor_scalar(dest[:, t, :], source[:, t, :], mv[:, t, 0:1], ln[:, 2, t:t + 1],
                                    ALU.subtract, ALU.mult).then_inc(sem(ready), 1)

            def newton(r, v, tmp):
                link(V.tensor_tensor(tmp, r, r, ALU.mult))
                link(V.tensor_tensor(tmp, tmp, v, ALU.mult))
                link(V.tensor_scalar(tmp, tmp, -0.5, 1.5, ALU.mult, ALU.add))
                link(V.tensor_tensor(r, r, tmp, ALU.mult))

            V.memset(srcI[:, EC - 1:EC], T * P).then_inc(sem("edge_pad_set"), 1)
            V.memset(dstI[:, EC - 1:EC], 0).then_inc(sem("edge_pad_set"), 1)
            V.memset(wE[:, EC - 1:EC], 0.0).then_inc(sem("edge_pad_set"), 1)
            V.memset(x_sb[:, T - 1, :], 0.0).then_inc(sem("x_pad_set"), 1)
            link(V.memset(recs[:, :, :], 0.0))
            V.memset(recs[:, :, 1], -1.0).then_inc(sem("recs_empty"), 1)
            V.memset(oneF, 1.0)
            V.memset(addr[:, EC:EP], 0.0)
            link(V.memset(edge[:, EC:EP, :], 0.0))
            dve.wait_ge(sem("edges_loaded"), 96)
            link(V.tensor_scalar(tmpI, srcI, 7, None, ALU.logical_shift_right))
            link(V.tensor_copy(binF, tmpI))
            link(V.tensor_scalar(tmpI, srcI, P - 1, None, ALU.bitwise_and))
            V.tensor_copy(edge[:, 0:EC, 1], tmpI)
            V.tensor_copy(edge[:, 0:EC, 0], dstI)
            V.tensor_copy(edge[:, 0:EC, 2], wE)
            for b in range(T):
                last = V.tensor_scalar(ohs[:, b, :], binF, float(b), None, ALU.is_equal, ALU.add,
                                       accum_out=rowtot[:, b:b + 1])
            last.then_inc(sem("edge_rowtot"), 1)

            def slots_of(nb, pre, total, k):
                dve.wait_ge(sem("bin_counts"), k + 1)
                link(V.tensor_scalar(cntI[:, 0:nb], total, float(P - 1), None, ALU.add))
                link(V.tensor_scalar(cntI[:, 0:nb], cntI[:, 0:nb], 7, None, ALU.logical_shift_right))
                link(V.tensor_copy(cnt[:, 0:nb], cntI[:, 0:nb]))
                link(V.tensor_tensor_scan(endt[:, 0:nb], ones[:, 0:nb], cnt[:, 0:nb], 0.0, ALU.mult, ALU.add))
                link(V.tensor_tensor(off[:, 0:nb], endt[:, 0:nb], cnt[:, 0:nb], ALU.subtract))
                link(V.tensor_scalar(off[:, 0:nb], off[:, 0:nb], float(P), -1.0, ALU.mult, ALU.add))
                link(V.tensor_tensor(off[:, 0:nb], off[:, 0:nb], pre, ALU.add))

            slots_of(T, banks[7][:, 0:T], banks[7][:, 32:32 + T], 0)
            link(V.memset(posF, 0.0))
            for b in range(T):
                link(V.tensor_tensor_scan(scanF, oneF, ohs[:, b, :], off[:, b:b + 1], ALU.mult, ALU.add))
                link(V.tensor_tensor(prodF, scanF, ohs[:, b, :], ALU.mult))
                link(V.tensor_tensor(posF, posF, prodF, ALU.add))
            link(V.tensor_copy(tmpI, posF))
            link(V.tensor_scalar(srcI, tmpI, P - 1, None, ALU.bitwise_and))
            link(V.tensor_scalar(tmpI, tmpI, 7, None, ALU.logical_shift_right))
            V.scalar_tensor_tensor(posF, srcI, float(NT), tmpI, ALU.mult, ALU.add).then_inc(sem("edge_slots"), 1)
            dve.wait_ge(sem("edge_slots"), 1)
            dve.wait_ge(sem("consts"), 8)
            q = NT // 4
            cmp = accF[32:33, 0:q * T].rearrange("p (t b) -> p t b", b=T)
            for i in range(4):
                link(V.tensor_tensor(cmp, iotaT[:, i * q:(i + 1) * q].unsqueeze(2).to_broadcast([1, q, T]),
                                     endt[32:33, 0:T].unsqueeze(1).to_broadcast([1, q, T]), ALU.is_ge))
                link(V.tensor_reduce(accF[32:33, q * T:q * T + q], cmp, AX, ALU.add))
                link(V.tensor_copy(bins[:, i * q:(i + 1) * q], accF[32:33, q * T:q * T + q]))

            dve.wait_ge(sem("x_loaded"), 32)
            layer_norm(0, x_sb, rows, "normed")
            V.memset(accF[:, :], 0.0).then_inc(sem("acc_zero"), 1)
            dve.wait_ge(sem("w_block0"), 11 * 16)
            for t in range(T):
                b = banks[4 + t % 2]
                dve.wait_ge(sem("lin_done"), t + 1)
                V.tensor_copy(rows[:, t, :], b[:, 0:D]).then_inc(sem("rows_ready"), 1)
                V.tensor_tensor(vals[:, t, :], b[:, D:2 * D], bcast[:, :], ALU.add).then_inc(sem("lin_taken"), 1)
            dve.wait_ge(sem("lin_taken"), T)
            dve.sem_inc(sem("v_bias_used"))
            dve.wait_ge(sem("lt_taken"), KD * len(CH))
            for k in range(KD):
                last = V.tensor_reduce(kmax[:, k:k + 1], hT[:, k, 0:N], AX, ALU.max, negate=True)
            last.then_inc(sem("kmax_ready"), 1)
            dve.wait_ge(sem("exp_ready"), KD)
            link(V.reciprocal(kinv, ksum))
            dve.wait_ge(sem("lam_done"), T)
            for k in range(KD):
                last = V.tensor_scalar(bn[:, k, :], banks[4 + k][:, 0:D], kinv[:, k:k + 1], None, ALU.mult)
            link(last)
            for k in range(KD):
                link(V.bn_stats(bnst[:, 6 * k:6 * k + 6], bn[:, k, :]))
                link(V.bn_aggr(bnmv[:, 2 * k:2 * k + 2], bnst[:, 6 * k:6 * k + 6]))
            V.tensor_scalar(bnt[:, 0:2], bnmv.rearrange("p (k c) -> p k c", c=2)[:, :, 1], EPS, None, ALU.add)\
                .then_inc(sem("bn_var"), 1)
            dve.wait_ge(sem("bn_sqrt"), 1)
            link(V.reciprocal(bnt[:, 4:6], bnt[:, 2:4]))
            newton(bnt[:, 4:6], bnt[:, 0:2], bnt[:, 6:8])
            for k in range(KD):
                link(V.tensor_scalar(bn[:, k, :], bn[:, k, :], bnmv[:, 2 * k:2 * k + 1], bnt[:, 4 + k:5 + k],
                                     ALU.subtract, ALU.mult))
                V.tensor_scalar(bn[:, k, :], bn[:, k, :], colb[:, 4 + k:5 + k], colb[:, 6 + k:7 + k],
                                ALU.mult, ALU.add).then_inc(sem("bn_ready"), 1)
            for t in range(T):
                dve.wait_ge(sem("lin_done"), T + t + 1)
                V.tensor_tensor(x_sb[:, t, :], x_sb[:, t, :], banks[4 + t % 2][:, 0:D], ALU.add)\
                    .then_inc(sem("lin_taken"), 1)

            def aggregate(a):
                def row_matrix(s, tiles, done):
                    m = oh[:, s:s + AHEAD, :]
                    ins = V.tensor_tensor(m, iota[:, :].unsqueeze(1).to_broadcast([P, AHEAD, P]),
                                          recs[:, tiles, 1].unsqueeze(2).to_broadcast([P, AHEAD, P]), ALU.is_equal)
                    if a == 0:
                        ins.then_inc(sem("matrix_01"), 1)
                        dve.wait_ge(sem("matrix_01"), done)
                        ins = V.tensor_tensor(m, m, recs[:, tiles, 2].unsqueeze(2).to_broadcast([P, AHEAD, P]), ALU.mult)
                    ins.then_inc(sem("row_matrix"), 1)

                dve.wait_ge(sem("rows_stored"), 16 * len(TG) * (a + 1))
                V.memset(g[:, :, D:AW], 1.0).then_inc(sem("g_ones"), 1)
                row_matrix(0, slice(0, AHEAD), 1)
                with dve.Fori(0, NT // U) as it:
                    for u in range(U):
                        if u % AHEAD == 0:
                            row_matrix((u + AHEAD) % MRING, bass.ds(it * U + (u + AHEAD), AHEAD),
                                       it * (U // AHEAD) + (u // AHEAD + 2))
                        tile = dve.value_load(bins[:, bass.ds(it * U + u, 1)]).with_bounds(min_val=0, max_val=T)
                        if u % 2 == 0:
                            dve.wait_ge(sem("product"), it * U + (a * NT + u + 2 + U))
                        dve.wait_ge(sem("summed"), it * U + (a * NT + u + SLOTS))
                        to = acc[:, bass.ds(tile, 1), :].rearrange("p a b -> p (a b)")
                        V.tensor_tensor(to, to, banks[4 + u % SLOTS][:, 0:AW], ALU.add).then_inc(sem("summed"), 1)
                dve.wait_ge(sem("summed"), (a + 1) * NT + SLOTS)

            dve.wait_ge(sem("recs_loaded"), 16)
            for s in range(4):
                dve.wait_ge(sem(f"f_stored{s}"), 16)
            aggregate(0)
            link(V.tensor_tensor(x_sb[:, :, :], x_sb[:, :, :], acc[:, 0:T, 0:D], ALU.add))
            dve.wait_ge(sem("rows_stored"), 16 * len(TG))
            layer_norm(1, x_sb, rows, "normed")
            for t in range(T):
                dve.wait_ge(sem("lin_done"), 2 * T + t + 1)
                V.tensor_copy(r_lg[:, t, :], banks[4 + t % 2][:, 0:EX]).then_inc(sem("lin_taken"), 1)
            dve.wait_ge(sem("lin_taken"), 3 * T)
            for t in range(T):
                link(V.max(out=r_m8[:, t, :], in_=r_lg[:, t, :]))
                link(V.max_index(out=r_i8[:, t, :], in_max=r_m8[:, t, :], in_values=r_lg[:, t, :]))
            link(V.tensor_copy(r_eid, r_i8[:, :, 0]))
            link(V.tensor_tensor(r_oh, iota[:, 0:EX].unsqueeze(2).to_broadcast([P, EX, T]),
                                 r_eid.unsqueeze(1).to_broadcast([P, EX, T]), ALU.is_equal))
            link(V.tensor_scalar(r_oh[:, :, T - 1], r_oh[:, :, T - 1], rowok[:, :], None, ALU.mult))
            V.tensor_reduce(rowtot[:, 0:EX], r_oh, AX, ALU.add).then_inc(sem("edge_rowtot"), 1)
            link(V.memset(r_msk, 1.0))
            link(V.memset(r_msk[:, :, 0], 0.0))
            link(V.tensor_tensor_scan(r_sc.rearrange("p b t -> p (b t)"), r_msk.rearrange("p b t -> p (b t)"),
                                      r_oh.rearrange("p b t -> p (b t)"), 0.0, ALU.mult, ALU.add))
            slots_of(EX, banks[7][:, 0:EX], banks[7][:, 32:32 + EX], 1)
            link(V.tensor_tensor(r_sc, r_sc, off[:, 0:EX].unsqueeze(2).to_broadcast([P, EX, T]), ALU.add))
            link(V.tensor_tensor(r_sc, r_sc, r_oh, ALU.mult))
            link(V.tensor_reduce(r_eid, r_sc.rearrange("p b t -> p t b"), AX, ALU.add))
            link(V.tensor_copy(posI[:, 0:T], r_eid))
            V.memset(invdeg, 0.0).then_inc(sem("pos_ready"), 1)
            for i in range(4):
                n = FT // 4
                ce = wB[32:33, 0:n * EX].rearrange("p (t b) -> p t b", b=EX)
                link(V.tensor_tensor(ce, iotaT[:, i * n:(i + 1) * n].unsqueeze(2).to_broadcast([1, n, EX]),
                                     endt[32:33, 0:EX].unsqueeze(1).to_broadcast([1, n, EX]), ALU.is_ge))
                link(V.tensor_reduce(top[32:33, i * n:(i + 1) * n], ce, AX, ALU.add))
            V.tensor_scalar(eidx[32:33, 0:FT], top[32:33, 0:FT], float(EX - 1), None, ALU.min).then_inc(sem("expert_table"), 1)
            dve.sem_inc(sem("f_y_done"), 4)
            with dve.Fori(0, FT // 4) as it:
                for s in range(4):
                    dve.wait_ge(sem("f_o_done"), it * 4 + (s + 3))
                    dve.wait_ge(sem(f"f_stored{s}"), it * 16 + 16)
                    V.tensor_scalar(f_y[:, s, :], banks[4 + s % 2][:, 0:D], 0.0, None, ALU.max)\
                        .then_inc(sem("f_y_ready"), 1)
                    dve.wait_ge(sem("f_y_ready"), it * 4 + (s + 1))
                    dve.sem_inc(sem("f_y_done"))
            dve.wait_ge(sem("tokens_back"), 16 * T)
            link(V.tensor_tensor(x_sb[:, 0:T - 1, :], x_sb[:, 0:T - 1, :], vals[:, 0:T - 1, :], ALU.add))
            link(V.tensor_tensor(x_sb[0:TAIL, T - 1, :], x_sb[0:TAIL, T - 1, :], vals[0:TAIL, T - 1, :], ALU.add))
            layer_norm(2, x_sb, rows, "normed")
            dve.wait_ge(sem("tr_done"), 3 * T)

            def rows_and_self(l):
                dve.wait_ge(sem("bhid_loaded"), 16 * (l + 1))
                if l == 0:
                    for s in range(4):
                        dve.wait_ge(sem(f"f_stored{s}"), 16 + 16 * FT // 4)
                for t in range(T):
                    b = banks[4 + t % 2]
                    dve.wait_ge(sem("lin_done"), (3 + l) * T + t + 1)
                    V.tensor_copy(rows[:, t, :], b[:, 0:D]).then_inc(sem("rows_ready"), 1)
                    V.tensor_tensor(vals[:, t, :], b[:, D:2 * D], bcast[:, :], ALU.add).then_inc(sem("lin_taken"), 1)
                dve.wait_ge(sem("lin_taken"), (4 + l) * T)
                V.memset(kn[:, 5:6], 0.0).then_inc(sem("self_ready"), 1)

            rows_and_self(0)
            dve.wait_ge(sem("rows_stored"), 16 * 2 * len(TG))
            for t in range(T):
                dve.wait_ge(sem("qkv_done"), t + 1)
                for i in range(2):
                    last = V.bn_stats(stats[:, i, :], banks[2][:, i * D:(i + 1) * D])
                link(last)
                for i in range(2):
                    last = V.bn_aggr(mv[:, i, :], stats[:, i, :])
                link(last)
                V.tensor_scalar(negm[:, 2 * t:2 * t + 2], mv[:, 0:2, 0], -1.0, None, ALU.mult)
                link(V.tensor_scalar(qs[:, 2 * t:2 * t + 2], mv[:, 0:2, 1], float(D), 1e-7, ALU.mult, ALU.add))
                V.reciprocal(qk[:, 2 * t:2 * t + 2], qs[:, 2 * t:2 * t + 2]).then_inc(sem("qk_means"), 1)
                dve.wait_ge(sem("mixo_done"), t + 1)
                V.tensor_tensor(x_sb[:, t, :], x_sb[:, t, :], banks[1][:, 0:D], ALU.add).then_inc(sem("mixo_taken"), 1)
            dve.wait_ge(sem("q4_ready"), T)
            V.memset(kn[:, 4:5], 0.0).then_inc(sem("q4_sum"), 1)
            dve.wait_ge(sem("kv_done"), T)
            for k in range(KD):
                last = V.tensor_copy(kn[:, k:k + 1], banks[6 + k][:, 0:1])
            last.then_inc(sem("kn_sum"), 1)
            dve.wait_ge(sem("q4_sqrt"), 1)
            rq = qk.rearrange("p (t c) -> p t c", c=2)[:, :, 0]
            link(V.tensor_tensor(sq, sq, rq, ALU.mult))
            link(V.tensor_scalar(sq, sq, 1e-12, None, ALU.max))
            link(V.reciprocal(sq, sq))
            link(V.tensor_tensor(sq, sq, rq, ALU.mult))
            dve.wait_ge(sem("kn_sqrt"), 1)
            link(V.tensor_scalar(kn[:, 2:4], kn[:, 2:4], 1e-12, None, ALU.max))
            link(V.reciprocal(kn[:, 0:2], kn[:, 2:4]))
            link(V.tensor_scalar(kn[:, 0:2], kn[:, 0:2], float(N) ** -0.5, None, ALU.mult))
            for k in range(KD):
                V.tensor_scalar(oh[:, 4 + 2 * k:6 + 2 * k, :].rearrange("p a b -> p (a b)"), banks[4 + k][:, 0:D],
                                kn[:, k:k + 1], None, ALU.mult).then_inc(sem("kv_ready"), 1)
            for t in range(T):
                dve.wait_ge(sem("mixo_done"), T + t + 1)
                V.scalar_tensor_tensor(x_sb[:, t, :], banks[2 + t % 2][:, 0:D], sq[:, t:t + 1], x_sb[:, t, :],
                                       ALU.mult, ALU.add).then_inc(sem("mixo_taken"), 1)
            for l in range(3):
                link(V.memset(accF[:, :], 0.0))
                if l == 0:
                    dve.wait_ge(sem("mixo_done"), 2 * T)
                aggregate(l + 1)
                if l == 0:
                    link(V.tensor_scalar(invdeg, acc[:, 0:T, D], 1.0, None, ALU.max))
                    link(V.reciprocal(invdeg, invdeg))
                dve.wait_ge(sem("rows_stored"), 16 * (l + 2) * len(TG))
                for t in range(T):
                    link(V.scalar_tensor_tensor(rows[:, t, :], acc[:, t, 0:D], invdeg[:, t:t + 1], vals[:, t, :],
                                                ALU.mult, ALU.add))
                    V.tensor_scalar(rows[:, t, :], rows[:, t, :], 0.0, None, ALU.max).then_inc(sem("normed"), 1)
                if l < 2:
                    dve.wait_ge(sem("tr_done"), (4 + l) * T)
                    rows_and_self(l + 1)
            for t in range(T):
                dve.wait_ge(sem("lin_done"), 6 * T + t + 1)
                V.tensor_tensor(x_sb[:, t, :], x_sb[:, t, :], banks[4 + t % 2][:, 0:D], ALU.add)\
                    .then_inc(sem("lin_taken"), 1)
            dve.wait_ge(sem("lin_taken"), 7 * T)
            dve.wait_ge(sem("tr_done"), 6 * T)
            layer_norm(3, x_sb, rows, "normed")
            dve.wait_ge(sem("tr_taken"), 7 * T)
            for k in range(KD):
                link(V.tensor_reduce(kmax[:, k:k + 1], xT[:, k, 0:N], AX, ALU.add))
            V.tensor_scalar(ksum, kmax, 1.0 / N, None, ALU.mult).then_inc(sem("mean_ready"), 1)
            lg, e8, p8 = top[0:1, 0:8], top[0:1, 8:16], top[0:1, 16:24]
            s1, s2, s3, v8 = top[0:1, 24:25], top[0:1, 25:26], top[0:1, 32:40], top[0:1, 40:48]
            dve.wait_ge(sem("route_done"), 1)
            dve.wait_ge(sem("wr_loaded"), 32)
            link(V.tensor_tensor(lg, banks[7][0:1, 0:EX1], rowb[0:1, 512:520], ALU.add))

            def softmax8(k):
                link(V.tensor_reduce(s1, lg, AX, ALU.max))
                V.tensor_scalar(e8, lg, s1, None, ALU.subtract).then_inc(sem(f"rt_exp{k}"), 1)
                dve.wait_ge(sem(f"rt_exp{k}d"), 1)
                link(V.tensor_reduce(s1, p8, AX, ALU.add))
                link(V.reciprocal(s2, s1))
                link(V.tensor_scalar(p8, p8, s2, None, ALU.mult))

            softmax8(1)
            link(V.tensor_scalar(s3, p8, float(N), None, ALU.mult))
            link(V.tensor_scalar(v8, s3, CAPACITY, None, ALU.is_gt))
            link(V.reciprocal(s3, s3))
            link(V.tensor_scalar(s3, s3, CAPACITY, -1.0, ALU.mult, ALU.add))
            link(V.tensor_tensor(s3, s3, v8, ALU.mult))
            link(V.tensor_scalar(s3, s3, 1.0, None, ALU.add))
            link(V.tensor_tensor(lg, p8, s3, ALU.mult))
            softmax8(2)
            link(V.max(out=v8, in_=p8))
            link(V.max_index(out=eidx[0:1, 8:16].bitcast(U32), in_max=v8, in_values=p8))
            link(V.tensor_copy(top[0:1, 56:64], eidx[0:1, 8:16].bitcast(U32)))
            V.tensor_copy(eidx[0:1, 0:8], top[0:1, 56:64]).then_inc(sem("experts_chosen"), 1)
            V.tensor_scalar(top[0:1, 48:50], v8[:, 0:2], v8[:, 0:1], None, ALU.subtract).then_inc(sem("rt_exp3"), 1)
            dve.wait_ge(sem("rt_exp3d"), 1)
            link(V.tensor_reduce(s1, top[0:1, 50:52], AX, ALU.add))
            link(V.reciprocal(s2, s1))
            V.tensor_scalar(top[0:1, 52:54], top[0:1, 50:52], s2, None, ALU.mult).then_inc(sem("gates_ready"), 1)
            dve.wait_ge(sem("gates_spread"), 1)
            link(V.tensor_copy(kinv, banks[7][:, 16:18]))
            dve.wait_ge(sem("w_ffn1"), 160)
            for k in range(2):
                link(V.tensor_scalar(rowb[0:1, k * D:(k + 1) * D], rowb[0:1, k * D:(k + 1) * D], kinv[0:1, k:k + 1],
                                     None, ALU.mult))
            link(V.tensor_tensor(rowb[0:1, 0:D], rowb[0:1, 0:D], rowb[0:1, D:2 * D], ALU.add))
            for j in range(J1):
                V.tensor_scalar(W2c[:, j, :], W2c[:, j, :], kinv[:, j * 2 // J1:j * 2 // J1 + 1], None, ALU.mult)\
                    .then_inc(sem("w2_scaled"), 1)
            for t in range(T):
                dve.wait_ge(sem("y1_done"), t + 1)
                V.tensor_tensor(rows[:, t, :], rows[:, t, :], banks[4 + t % 2][:, 0:D], ALU.add)\
                    .then_inc(sem("y1_taken"), 1)
            dve.wait_ge(sem("y1_taken"), T)
            layer_norm(4, rows, vals, "normed")
            dve.wait_ge(sem("normed"), 8 * T)
            for t in range(T):
                link(V.tensor_tensor(vals[:, t, :], vals[:, t, :], bcast[:, :], ALU.mult))
                link(V.tensor_tensor(vals[:, t, :], vals[:, t, :], wB[:, 0:D], ALU.add))
                V.tensor_tensor(vals[:, t, :], vals[:, t, :], x_sb[:, t, :], ALU.add).then_inc(sem("out_ready"), 1)

        @block.tensor
        def _(pe):
            mm, tr = nc.tensor.matmul, nc.tensor.transpose

            def transposes(s):
                for t in range(T):
                    pe.wait_ge(sem("normed"), s * T + t + 1)
                    if s * T + t >= 2:
                        pe.wait_ge(sem("tr_taken"), s * T + t - 1)
                    for k in range(KD):
                        last = tr(banks[t % 2][:, k * P:(k + 1) * P], rows[:, t, k * P:(k + 1) * P], ident[:, :])
                    last.then_inc(sem("tr_done"), 1)

            def linear(s, source, W, n, bias=None):
                pe.wait_ge(sem("lin_taken"), s * T) if s else None
                for t in range(T):
                    if t >= 2:
                        pe.wait_ge(sem("lin_taken"), s * T + t - 1)
                    o = banks[4 + t % 2][:, 0:n]
                    if bias is not None:
                        mm(o, ones[0:1, :], bias, start=True, stop=False)
                    for k in range(KD):
                        last = mm(o, source[:, k, t * P:(t + 1) * P], W[:, k, 0:n],
                                  start=k == 0 and bias is None, stop=k == KD - 1)
                    last.then_inc(sem("lin_done"), 1)

            def linearT(first, chunks, W):
                for e in range(KD):
                    for c, (a, n) in enumerate(chunks):
                        i = e * len(chunks) + c
                        if first + i >= 2:
                            pe.wait_ge(sem("lt_taken"), first + i - 1)
                        for k in range(KD):
                            last = mm(banks[2 + i % 2][:, 0:n], W[:, k, e * P:(e + 1) * P], xT[:, k, a:a + n],
                                      start=k == 0, stop=k == KD - 1)
                        last.then_inc(sem("lt_done"), 1)

            def bin_counts(nb, k):
                pe.wait_ge(sem("edge_rowtot"), k + 1)
                mm(banks[7][:, 0:nb], tri[:, :], rowtot[:, 0:nb], start=True, stop=True)
                mm(banks[7][:, 32:32 + nb], ones[:, :], rowtot[:, 0:nb], start=True, stop=True)\
                    .then_inc(sem("bin_counts"), 1)

            pe.wait_ge(sem("consts"), 8)
            bin_counts(T, 0)
            transposes(0)
            pe.wait_ge(sem("w_block0"), 11 * 16)
            pe.wait_ge(sem("tr_taken"), T)
            linear(0, xT, W0V, 2 * D)
            linearT(0, CH, Wk)
            pe.wait_ge(sem("exp_ready"), KD)
            pe.wait_ge(sem("lin_taken"), T)
            for t in range(T + 1):
                if t < T:
                    if t >= 2:
                        pe.wait_ge(sem("et_taken"), t - 1)
                    for k in range(KD):
                        last = tr(banks[t % 2][0:tw(t), k * P:(k + 1) * P], hT[:, k, t * P:t * P + tw(t)], ident[:, :])
                    last.then_inc(sem("et_done"), 1)
                if t >= 1:
                    u = t - 1
                    pe.wait_ge(sem("et_taken"), u + 1)
                    for k in range(KD):
                        last = mm(banks[4 + k][:, 0:D], xt[0:tw(u), u % 2, k, :], vals[0:tw(u), u, :],
                                  start=u == 0, stop=u == T - 1)
                    last.then_inc(sem("lam_done"), 1)
            pe.wait_ge(sem("et_taken"), T)
            for k in range(KD):
                for j in range(KD):
                    last = tr(banks[k][:, j * P:(j + 1) * P], Wq[:, j, k * P:(k + 1) * P], ident[:, :])
                last.then_inc(sem("wqT_done"), 1)
            pe.wait_ge(sem("wqT_taken"), KD)
            pe.wait_ge(sem("bn_ready"), KD)
            pe.wait_ge(sem("lt_taken"), KD * len(CH))
            for j in range(KD):
                for k in range(KD):
                    last = mm(banks[2 + j][:, 0:D], WqT[:, k, j * P:(j + 1) * P], bn[:, k, :],
                              start=k == 0, stop=k == KD - 1)
                last.then_inc(sem("mx_done"), 1)
            for k in range(KD):
                last = mm(banks[6][0:1, 0:D], colb[:, 2 + k:3 + k], bn[:, k, :], start=k == 0, stop=k == KD - 1)
            last.then_inc(sem("mx_done"), 1)
            for k in range(KD):
                last = tr(banks[0][:, k * EX:(k + 1) * EX], rw[:, k * P:(k + 1) * P], ident[0:EX, 0:EX])
            last.then_inc(sem("rwT_done"), 1)
            pe.wait_ge(sem("mx_taken"), KD + 1)
            linear(1, xT, Mx, D, rowb[0:1, 256:512])

            def products(a):
                pe.wait_ge(sem("g_ones"), a + 1)
                with pe.Fori(0, NT // U) as it:
                    for u in range(U):
                        pe.wait_ge(sem(f"gathered{u % RING}"), it * (16 * U // RING) + (16 * (a * NT // RING + u // RING + 1)))
                        if u % AHEAD == 0:
                            pe.wait_ge(sem("row_matrix"), it * (U // AHEAD) + (a * (NT // AHEAD + 1) + u // AHEAD + 1))
                        pe.wait_ge(sem("summed"), it * U + (a * NT + u + 1))
                        mm(banks[4 + u % SLOTS][:, 0:AW], oh[:, u % MRING, :], g[:, u % RING, :],
                           start=True, stop=True).then_inc(sem("product"), 1)

            pe.wait_ge(sem("lin_taken"), 2 * T)
            pe.sem_inc(sem("product"), U)
            pe.sem_inc(sem("summed"), SLOTS)
            products(0)
            pe.wait_ge(sem("rwT_taken"), 1)
            transposes(1)
            pe.wait_ge(sem("tr_taken"), 2 * T)
            linear(2, xT, rwT, EX, rowb[0:1, 0:EX])
            bin_counts(EX, 1)
            pe.sem_inc(sem("f_h_done"), 2)
            pe.sem_inc(sem("f_o_done"), 2)
            pe.wait_ge(sem("lin_taken"), 3 * T)
            with pe.Fori(0, FT // 4) as it:
                for s in range(4):
                    b = s % 2
                    pe.wait_ge(sem(f"f_loaded{s}"), it * 80 + 80)
                    pe.wait_ge(sem("f_xt_taken"), it * 4 + (s + 1))
                    for k in range(KD):
                        last = tr(banks[b][:, k * P:(k + 1) * P], f_x[:, s, k * P:(k + 1) * P], ident[:, :])
                    last.then_inc(sem("f_xt_done"), 1)
                    pe.wait_ge(sem("f_xt_taken"), it * 4 + (s + 2))
                    for k in range(KD):
                        last = mm(banks[2 + b][0:H0, 0:P], f_w1[:, s, k, :], f_xT[:, b, k, :],
                                  start=k == 0, stop=k == KD - 1)
                    last.then_inc(sem("f_h_done"), 1)
                    pe.wait_ge(sem("f_h_taken"), it * 4 + (s + 1))
                    pe.wait_ge(sem("f_y_done"), it * 4 + (s + 3))
                    mm(banks[4 + b][:, 0:D], ones[0:1, :], f_b2[:, s, :], start=True, stop=False)
                    mm(banks[4 + b][:, 0:D], f_h[:, b, :], f_w2[:, s, :], start=False, stop=True)\
                        .then_inc(sem("f_o_done"), 1)
            transposes(2)
            pe.wait_ge(sem("tr_taken"), 3 * T)
            pe.wait_ge(sem("w_block1"), 14 * 16)
            linearT(KD * len(CH), CHP, Wio[:, 0])
            pe.wait_ge(sem("lt_taken"), KD * (len(CH) + len(CHP)))
            linear(3, hT, Was[:, 0], 2 * D)
            pe.wait_ge(sem("lin_taken"), 4 * T)
            v, k2, k4 = (oh[:, a:a + 2, :].rearrange("p a b -> p (a b)") for a in (2, 0, 4))
            for t in range(T):
                n = tw(t)
                if t >= 1:
                    pe.wait_ge(sem("q2_ready"), t)
                    pe.wait_ge(sem("k2_ready"), t)
                for o, a, m in ((banks[2], 0, 512), (banks[3], 512, 256)):
                    mm(o[:, 0:m], ones[0:1, :], rowb[0:1, a:a + m], start=True, stop=False)
                    for k in range(KD):
                        last = mm(o[:, 0:m], xT[:, k, t * P:(t + 1) * P], Wqkv[:, k, a:a + m],
                                  start=False, stop=k == KD - 1)
                last.then_inc(sem("qkv_done"), 1)
                pe.wait_ge(sem("v_ready"), t + 1)
                for k in range(KD):
                    last = tr(banks[0][:, k * P:(k + 1) * P], v[:, k * P:(k + 1) * P], ident[:, :])
                last.then_inc(sem("vT_done"), 1)
                pe.wait_ge(sem("vT_taken"), t + 1)
                if t >= 1:
                    pe.wait_ge(sem("mixo_taken"), t)
                mm(banks[1][:, 0:D], ones[0:1, :], rowb[0:1, 1024:1280], start=True, stop=False)
                for k in range(KD):
                    last = mm(banks[1][:, 0:D], xt[:, 0, k, :], Wo1[:, k, :], start=False, stop=k == KD - 1)
                last.then_inc(sem("mixo_done"), 1)
                pe.wait_ge(sem("k2_ready"), t + 1)
                for k in range(KD):
                    mm(banks[4 + k][:, 0:D], k2[0:n, k * P:(k + 1) * P], v[0:n, :], start=t == 0, stop=t == T - 1)
                    last = mm(banks[6 + k][:, 0:1], k4[0:n, k * P:(k + 1) * P], ones[0:n, 0:1],
                              start=t == 0, stop=t == T - 1)
                last.then_inc(sem("kv_done"), 1)
            pe.wait_ge(sem("kv_ready"), KD)
            pe.wait_ge(sem("mixo_taken"), T)
            pe.wait_ge(sem("q4_ready"), T)
            for j in range(KD):
                for k in range(KD):
                    last = tr(banks[j][:, k * P:(k + 1) * P], oh[:, 4 + 2 * k + j, :], ident[:, :])
            last.then_inc(sem("kvT_done"), 1)
            pe.wait_ge(sem("kvT_taken"), 2 * KD)
            for c in range(KD):
                for j in range(KD):
                    last = mm(banks[2 + c][:, 0:D], xt[:, 1 - j, c, :], Wo1[:, j, :], start=j == 0, stop=j == KD - 1)
            last.then_inc(sem("m2_done"), 1)
            pe.wait_ge(sem("m2_taken"), KD)
            for t in range(T + 1):
                if t < T:
                    if t >= 2:
                        pe.wait_ge(sem("qT_taken"), t - 1)
                    for k in range(KD):
                        last = tr(banks[t % 2][:, k * P:(k + 1) * P], rows[:, t, k * P:(k + 1) * P], ident[:, :])
                    last.then_inc(sem("qT_done"), 1)
                if t >= 1:
                    u = t - 1
                    pe.wait_ge(sem("qT_taken"), u + 1)
                    if u >= 2:
                        pe.wait_ge(sem("mixo_taken"), T + u - 1)
                    for k in range(KD):
                        last = mm(banks[2 + u % 2][:, 0:D], xt[:, u % 2, k, :],
                                  oh[:, 2 * k:2 * k + 2, :].rearrange("p a b -> p (a b)"),
                                  start=k == 0, stop=k == KD - 1)
                    last.then_inc(sem("mixo_done"), 1)
            pe.wait_ge(sem("mixo_taken"), 2 * T)
            for l in range(3):
                products(l + 1)
                transposes(3 + l)
                pe.wait_ge(sem("tr_taken"), (4 + l) * T)
                if l < 2:
                    linear(4 + l, hT, Was[:, l + 1], 2 * D)
                    pe.wait_ge(sem("lin_taken"), (5 + l) * T)
                else:
                    linear(6, hT, Wio[:, 1], D, rowb[0:1, 768:1024])
            transposes(6)
            pe.wait_ge(sem("mean_ready"), 1)
            pe.wait_ge(sem("wr_loaded"), 32)
            for k in range(KD):
                last = mm(banks[7][0:1, 0:EX1], ksum[:, k:k + 1], top[:, 64 + 8 * k:72 + 8 * k], start=k == 0, stop=k == KD - 1)
            last.then_inc(sem("route_done"), 1)
            pe.wait_ge(sem("gates_ready"), 1)
            mm(banks[7][:, 16:18], ones[0:1, :], top[0:1, 52:54], start=True, stop=True).then_inc(sem("gates_spread"), 1)
            pe.wait_ge(sem("w_ffn1"), 160)
            pe.wait_ge(sem("lin_taken"), 7 * T)
            i = 0
            for c in range(9):
                n = 384 if c < 8 else P
                for j in range(J1):
                    if i >= 4:
                        pe.wait_ge(sem("h1_taken"), i - 3)
                    for k in range(KD):
                        last = mm(banks[i % 4][:, 0:n], W1c[:, j * 2 // J1, k, (j % (J1 // 2)) * P:(j % (J1 // 2) + 1) * P],
                                  xT[:, k, c * 384:c * 384 + n], start=k == 0, stop=k == KD - 1)
                    last.then_inc(sem("h1_done"), 1)
                    i += 1
                pe.wait_ge(sem("h1_taken"), i)
                pe.wait_ge(sem("w2_scaled"), J1)
                for s in range(n // P):
                    t = 3 * c + s
                    if t >= 2:
                        pe.wait_ge(sem("y1_taken"), t - 1)
                    o = banks[4 + t % 2][:, 0:D]
                    mm(o, ones[0:1, :], rowb[0:1, 0:D], start=True, stop=False)
                    for j in range(J1):
                        last = mm(o, gel[:, c % 2, j, s * P:(s + 1) * P], W2c[:, j, :], start=False, stop=j == J1 - 1)
                    last.then_inc(sem("y1_done"), 1)


_INS = ['x', 'src', 'dst', 'edge_weight', 'L0_gnn_weight', 'L0_mix_W_qk', 'L0_mix_b_qk', 'L0_mix_W_v', 'L0_mix_b_v',
        'L0_mix_gamma', 'L0_mix_beta', 'L0_ffn_router_w', 'L0_ffn_router_b', 'L0_ffn_W1', 'L0_ffn_b1', 'L0_ffn_W2',
        'L0_ffn_b2', 'L1_gnn_W_in', 'L1_gnn_b_in', 'L1_gnn_W_agg', 'L1_gnn_W_self', 'L1_gnn_b_hid', 'L1_gnn_W_out',
        'L1_gnn_b_out', 'L1_mix_W_qkv', 'L1_mix_b_qkv', 'L1_mix_W_out', 'L1_mix_b_out', 'L1_ffn_Wr', 'L1_ffn_br',
        'L1_ffn_W1', 'L1_ffn_b1', 'L1_ffn_W2', 'L1_ffn_b2', 'L1_ffn_gamma', 'L1_ffn_beta']


def kernel(**inputs):
    import numpy as _np
    import concourse.bacc as _bacc
    from concourse import mybir as _mybir
    from concourse.bass_utils import run_bass_kernel_spmd as _run

    nc = _bacc.Bacc("TRN2", target_bir_lowering=False, num_devices=1)
    arrays, args = {}, []
    for name in _INS:
        a = _np.ascontiguousarray(inputs[name])
        arrays[f"in_{name}"] = a
        args.append(nc.dram_tensor(f"in_{name}", a.shape, _mybir.dt.from_np(a.dtype), kind="ExternalInput").ap())
    args.append(nc.dram_tensor("out_0", (N, D), F32, kind="ExternalOutput").ap())
    gps_kernel(nc, *args)
    r = _run(nc, [arrays], core_ids=[0])
    return r.results[0]["out_0"]
```

```python
from contextlib import ExitStack

import concourse.bass as bass
from concourse import mybir

F32 = mybir.dt.float32
BF16 = mybir.dt.bfloat16
I32 = mybir.dt.int32
U32 = mybir.dt.uint32
ALU = mybir.AluOpType
ACT = mybir.ActivationFunctionType
AX = mybir.AxisListType.X

P = 128
N, D, E = 3125, 256, 50000
KD = D // P
T = -(-N // P)
TAIL = N - (T - 1) * P
NP = T * P
EC = -(-E // P)
EREST = E - (EC - 1) * P
U = 32
NT = -(-((E + T * (P - 1)) // P) // U) * U
RING = 16
MRING = 8
SLOTS = 4
AHEAD = 4
AW = D + 1
EX, H0 = 32, 64
FT = -(-((N + EX * (P - 1)) // P) // 8) * 8
EX1, H1 = 8, 512
J1 = 2 * H1 // P
EPS = 1e-5
CAPACITY = float(-(-N * 5 // (4 * EX1)))
CH = [(c * 512, min(512, N - c * 512)) for c in range(-(-N // 512))]
CHP = [(c * 512, min(512, NP - c * 512)) for c in range(-(-NP // 512))]
TG = [(0, 7), (7, 7), (14, 6), (20, 5)]


def gps_kernel(nc, x, src, dst, edge_weight, gnn0_W, mix0_Wqk, mix0_bqk, mix0_Wv, mix0_bv, mix0_gamma,
               mix0_beta, ffn0_rw, ffn0_rb, ffn0_W1, ffn0_b1, ffn0_W2, ffn0_b2, gnn1_Win, gnn1_bin,
               gnn1_Wagg, gnn1_Wself, gnn1_bhid, gnn1_Wout, gnn1_bout, mix1_Wqkv, mix1_bqkv, mix1_Wout,
               mix1_bout, ffn1_Wr, ffn1_br, ffn1_W1, ffn1_b1, ffn1_W2, ffn1_b2, ffn1_gamma, ffn1_beta, out):
    records_d = nc.dram_tensor("records_d", [P, NT, 3], F32).ap()
    rows_d = nc.dram_tensor("rows_d", [NP, D], F32).ap()
    xs_d = nc.dram_tensor("xs_d", [FT * P, D], F32).ap()
    ys_d = nc.dram_tensor("ys_d", [FT * P, D], F32).ap()

    with ExitStack() as ctx:
        def sb(name, shape, dt=F32):
            return ctx.enter_context(nc.sbuf_tensor(name, shape, dt))

        sems = {}

        def sem(name):
            if name not in sems:
                sems[name] = ctx.enter_context(nc.semaphore(name))
            return sems[name]

        x_sb = sb("x_sb", [P, T, D])
        rows = sb("rows", [P, T, D])
        xT = sb("xT", [P, KD, NP])
        hT = sb("hT", [P, KD, NP])
        vals = sb("vals", [P, T, D])
        accF = sb("accF", [P, (T + 1) * AW])
        acc = accF[:, :].rearrange("p (t w) -> p t w", w=AW)
        recs = sb("recs", [P, NT + AHEAD, 3])
        wA = sb("wA", [P, 4096])
        wB = sb("wB", [P, 2048])
        gF = sb("gF", [P, 2056])
        g = rows[:, :, :].rearrange("p t d -> p (t d)")[:, 0:RING * AW].rearrange("p (s w) -> p s w", w=AW)
        oh = sb("oh", [P, MRING, P])
        xt = sb("xt", [P, 2, KD, P])
        idx = sb("idx", [P, U], I32)
        srt = sb("srt", [P, U, 3])
        misc = sb("misc", [P, 1280])
        rowb = misc[0:1, :]
        bins = misc[32:33, 0:NT].bitcast(I32)
        iotaT = misc[32:33, NT:2 * NT]
        zero_row = misc[64:65, 0:AW]
        ident = sb("ident", [P, P])
        tri = sb("tri", [P, P])
        ones = sb("ones", [P, P])
        iota = sb("iota", [P, P])
        rowok = sb("rowok", [P, 1])
        rowid = sb("rowid", [P, 1])
        small = sb("small", [P, 768])
        stats = sb("stats", [P, T, 6])
        mv = sb("mv", [P, T, 2])
        ln = sb("ln", [P, 4, T])
        bcast = sb("bcast", [P, D])
        banks = [ctx.enter_context(nc.psum_tensor(f"bank{i}", [P, 512], F32)) for i in range(8)]

        def cols(a, n):
            return small[:, a:a + n]
        rowtot, pref, tot, cnt, endt, off = (cols(32 * i, 32) for i in range(6))
        colb = cols(192, 16)
        invdeg = cols(208, T)
        kmax, ksum, kinv = cols(240, 2), cols(242, 2), cols(244, 2)
        bnst, bnmv, bnt = cols(248, 12), cols(260, 4), cols(264, 8)
        posI = cols(424, 32).bitcast(I32)
        kn = cols(272, 6)
        top = cols(528, 96)
        cntI = cols(640, 32).bitcast(I32)
        eidx = cols(672, 64).bitcast(I32)

        block = ctx.enter_context(nc.Block())

        ohs = accF[:, 0:T * EC // 2 + 1].bitcast(BF16)[:, 0:T * EC].rearrange("p (b j) -> p b j", j=EC)
        o = T * EC // 2 + 2
        srcI, dstI, wE, tmpI = (accF[:, o + EC * i:o + EC * (i + 1)] for i in range(4))
        srcI, dstI, tmpI = srcI.bitcast(I32), dstI.bitcast(I32), tmpI.bitcast(I32)
        EP = EC + 1
        binF, scanF, posF, prodF, oneF = (gF[:, EP * i:EP * i + EC] for i in range(5))
        addr = gF[:, EP * 2:EP * 3]
        edge = wB[:, 0:3 * EP].rearrange("p (j c) -> p j c", c=3)

        W0V = wA[:, 0:1024].rearrange("p (k n) -> p k n", k=KD)
        Wk = wA[:, 1024:1536].rearrange("p (k n) -> p k n", k=KD)
        Wq = wA[:, 1536:2048].rearrange("p (k n) -> p k n", k=KD)
        WqT = wA[:, 2048:2560].rearrange("p (k n) -> p k n", k=KD)
        bn = wA[:, 2560:3072].rearrange("p (k n) -> p k n", k=KD)
        Mx = wA[:, 3072:3584].rearrange("p (k n) -> p k n", k=KD)
        rw = wA[0:EX, 3584:3840]
        rwT = wA[:, 3840:3904].rearrange("p (k n) -> p k n", k=KD)
        f_x = accF[:, 0:1024].rearrange("p (s n) -> p s n", s=4)
        f_w1 = accF[:, 1024:1536].rearrange("p (s k n) -> p s k n", s=4, k=KD)
        f_w2 = accF[0:H0, 4356:6404].rearrange("p (s n) -> p s n", s=8)
        f_sel = accF[0:3 * EX, 2560:2816].bitcast(BF16).rearrange("p (s n) -> p s n", s=4)
        f_row, f_exp = accF[0:3 * EX, 2816:2944], top[0:3 * EX, 0:FT]
        f_b, f_rest = accF[0:3 * EX, 2944:2944 + D + H0], accF[0:3 * EX, 3264:3264 + D + H0]
        f_parts = accF[0:3 * EX, 6404:6404 + (D + H0) // 2].bitcast(BF16)
        f_b2, f_b1 = f_parts[:, 0:D], f_parts[:, D:D + H0]
        f_xT = accF[:, 3588:4100].rearrange("p (s k n) -> p s k n", s=2, k=KD)
        f_h = accF[0:H0, 4100:4356].rearrange("p (s n) -> p s n", s=2)
        f_y = accF[:, 1536:2560].rearrange("p (s n) -> p s n", s=4)
        r_oh = wB[:, 0:EX * T].rearrange("p (b t) -> p b t", t=T)
        r_sc = wB[:, 800:1600].rearrange("p (b t) -> p b t", t=T)
        r_lg = oh[:, 0:7, :].rearrange("p a b -> p (a b)")[:, 0:T * EX].rearrange("p (t b) -> p t b", b=EX)
        r_m8 = gF[:, 0:8 * T].rearrange("p (t e) -> p t e", e=8)
        r_i8 = gF[:, 8 * T:16 * T].bitcast(U32).rearrange("p (t e) -> p t e", e=8)
        r_msk = gF[:, 16 * T:16 * T + EX * T].rearrange("p (b t) -> p b t", t=T)
        r_eid = gF[:, 1400:1400 + T]
        Wio = wA[:, 0:1024].rearrange("p (w k n) -> p w k n", w=2, k=KD)
        Was = wA[:, 1024:4096].rearrange("p (l k n) -> p l k n", l=3, k=KD)
        Wself = Was[:, :, :, D:2 * D]
        Wqkv = wB[:, 0:1536].rearrange("p (k n) -> p k n", k=KD)
        Wo1 = wB[:, 1536:2048].rearrange("p (k n) -> p k n", k=KD)
        WT = oh[:, :, :].rearrange("p a b -> p (a b)").rearrange("p (w k n) -> p w k n", w=2, k=KD)
        Wvo = xt[:, :, :, :].rearrange("p a k n -> p a (k n)")
        b_in = gF[:, 0:D].rearrange("p (k n) -> p k n", k=KD)
        gbias = hT[:, 0, 0:D]
        s_x, s_h = (gF[:, i * D:(i + 1) * D].rearrange("p (k n) -> p k n", k=KD) for i in range(2))
        s_v, s_k2, s_k4, s_q2, s_junk = (gF[:, i * D:(i + 1) * D] for i in range(2, 7))
        s_q2T = gF[:, 7 * D:8 * D].rearrange("p (k n) -> p k n", k=KD)
        kv = Wio[:, 0]
        kvs, kvT = (gF[:, i * 2 * D:(i + 1) * 2 * D].rearrange("p (k n) -> p k n", k=KD) for i in (0, 1))
        m1 = cols(506, 16)
        W1c = wA[:, 0:2 * KD * H1].rearrange("p (e k n) -> p e k n", e=2, k=KD)
        W2c = wA[:, 2048:4096].rearrange("p (j n) -> p j n", n=D)
        gel = hT[:, :, :].rearrange("p k n -> p (k n)")[:, 0:2 * J1 * 384].rearrange("p (s j n) -> p s j n", s=2, j=J1)

        def pt(ap):
            return ap.rearrange("(t p) d -> p t d", p=P)

        def kp(ap):
            return ap.rearrange("(k p) n -> p k n", p=P)

        def row(ap):
            return ap.rearrange("(a n) -> a n", a=1)

        def tw(t):
            return P if t < T - 1 else TAIL

        @block.sync
        def _(sp):
            ld = sem("edges_loaded")
            sp.wait_ge(sem("edge_pad_set"), 3)
            for tile, a in ((srcI, src), (dstI, dst), (wE, edge_weight)):
                sp.dma_start(tile[:, 0:EC - 1], a[0:(EC - 1) * P].rearrange("(p j) -> p j", p=P)).then_inc(ld, 16)
                sp.dma_start(tile[0:EREST, EC - 1:EC],
                             a[(EC - 1) * P:E].rearrange("(p j) -> p j", j=1)).then_inc(ld, 16)
            sp.wait_ge(sem("x_pad_set"), 1)
            sp.dma_start(x_sb[:, 0:T - 1, :], pt(x[0:(T - 1) * P, :])).then_inc(sem("x_loaded"), 16)
            sp.dma_start(x_sb[0:TAIL, T - 1, :], x[(T - 1) * P:N, :]).then_inc(sem("x_loaded"), 16)
            w = sem("w_block0")
            sp.dma_start(W0V[:, :, 0:D], kp(gnn0_W)).then_inc(w, 16)
            sp.dma_start(W0V[:, :, D:2 * D], kp(mix0_Wv)).then_inc(w, 16)
            sp.dma_start(Wk, kp(mix0_Wqk[1])).then_inc(w, 16)
            sp.dma_start(Wq, kp(mix0_Wqk[0])).then_inc(w, 16)
            sp.dma_start(colb[:, 0:2], mix0_bqk[1].rearrange("(k p) -> p k", p=P), allow_slow_non_contiguous=True).then_inc(w, 16)
            sp.dma_start(colb[:, 2:4], mix0_bqk[0].rearrange("(k p) -> p k", p=P), allow_slow_non_contiguous=True).then_inc(w, 16)
            sp.dma_start(colb[:, 4:6], mix0_gamma.rearrange("(k p) -> p k", p=P), allow_slow_non_contiguous=True).then_inc(w, 16)
            sp.dma_start(colb[:, 6:8], mix0_beta.rearrange("(k p) -> p k", p=P), allow_slow_non_contiguous=True).then_inc(w, 16)
            sp.dma_start(bcast[:, :], row(mix0_bv).to_broadcast([P, D])).then_inc(w, 16)
            sp.dma_start(rw, ffn0_rw).then_inc(w, 16)
            sp.dma_start(rowb[0:1, 0:EX], row(ffn0_rb)).then_inc(w, 16)
            for a, n in TG:
                sp.wait_ge(sem("rows_ready"), a + n)
                sp.dma_start(pt(rows_d)[:, a:a + n, :], rows[:, a:a + n, :]).then_inc(sem("rows_stored"), 16)
            sp.wait_ge(sem("sort_part0"), 16 * (8 * (EC // U) + EC % U))
            for q in (1, 2, 3):
                sp.wait_ge(sem(f"sort_part{q}"), 16 + 16 * 8 * (EC // U))
            sp.dma_start(recs[:, 0:NT, :], records_d).then_inc(sem("recs_loaded"), 16)
            sp.wait_ge(sem("acc_zero"), 1)
            xs_flat = xs_d.rearrange("(p a) d -> p (a d)", p=P)
            q = FT * D // 4
            for i in range(4):
                sp.dma_start(xs_flat[:, i * q:(i + 1) * q], accF[:, 0:q]).then_inc(sem(f"f_stored{i}"), 16)
            sp.wait_ge(sem("tokens_scattered"), 16 * T)
            sp.wait_ge(sem("expert_table"), 1)
            for i in range(3):
                sp.dma_start(f_b[EX * i:EX * (i + 1), 0:D], ffn0_b2).then_inc(sem("f_biases"), 16)
                sp.dma_start(f_b[EX * i:EX * (i + 1), D:D + H0], ffn0_b1).then_inc(sem("f_biases"), 16)

            def load_tile(n, s):
                e = sp.value_load(eidx[32:33, bass.ds(n, 1)], min_val=0, max_val=EX - 1)
                f = sem(f"f_loaded{s % 4}")
                sp.dma_start(f_x[:, s % 4, :], xs_d[bass.ds(n * P, P), :]).then_inc(f, 16)
                sp.dma_start(f_w1[:, s % 4], ffn0_W1[bass.ds(e, 1)].rearrange("a (k p) n -> p (a k) n", p=P)).then_inc(f, 16)
                sp.dma_start(f_w2[:, s, :], ffn0_W2[bass.ds(e, 1)].rearrange("a p n -> (a p) n")).then_inc(f, 16)

            for s in range(4):
                load_tile(s, s)
            with sp.Fori(0, FT // 8 - 1) as it:
                for s in range(4, 12):
                    sp.wait_ge(sem("f_h_done"), it * 8 + (s - 1))
                    load_tile(it * 8 + s, s % 8)
            for n in range(FT - 4, FT):
                sp.wait_ge(sem("f_h_done"), n - 1)
                load_tile(n, n % 8)
            w = sem("w_mix1")
            sp.wait_ge(sem("expert_table"), 1)
            sp.dma_start(Wqkv, kp(mix1_Wqkv)).then_inc(w, 16)
            sp.dma_start(Wo1, kp(mix1_Wout)).then_inc(w, 16)
            sp.dma_start(rowb[0:1, 0:768], row(mix1_bqkv)).then_inc(w, 16)
            sp.dma_start(rowb[0:1, 768:1024], row(gnn1_bout)).then_inc(w, 16)
            sp.dma_start(rowb[0:1, 1024:1280], row(mix1_bout)).then_inc(w, 16)
            for l in range(3):
                if l > 0:
                    sp.wait_ge(sem("self_taken"), l * T + 1)
                    sp.wait_ge(sem("agg_gathered"), l + 1)
                else:
                    sp.wait_ge(sem("v_bias_used"), 1)
                sp.dma_start(bcast[:, :], row(gnn1_bhid[l]).to_broadcast([P, D])).then_inc(sem("bhid_loaded"), 16)
                for a, n in TG:
                    sp.wait_ge(sem("rows_ready"), (l + 1) * T + a + n)
                    sp.dma_start(pt(rows_d)[:, a:a + n, :], rows[:, a:a + n, :]).then_inc(sem("rows_stored"), 16)
            sp.wait_ge(sem("lin_taken"), 7 * T)
            sp.dma_start(top[:, 64:80].rearrange("p (k e) -> p k e", e=EX1), kp(ffn1_Wr)).then_inc(sem("wr_loaded"), 16)
            sp.dma_start(rowb[0:1, 512:520], row(ffn1_br)).then_inc(sem("wr_loaded"), 16)
            sp.wait_ge(sem("experts_chosen"), 1)
            w = sem("w_ffn1")
            sp.dma_start(bcast[:, :], row(ffn1_gamma).to_broadcast([P, D])).then_inc(w, 16)
            sp.dma_start(wB[:, 0:D], row(ffn1_beta).to_broadcast([P, D])).then_inc(w, 16)
            for k in range(2):
                e = sp.value_load(eidx[0:1, k:k + 1], min_val=0, max_val=EX1 - 1)
                sp.dma_start(W1c[:, k], ffn1_W1[bass.ds(e, 1)].rearrange("a (k p) n -> p (a k) n", p=P)).then_inc(w, 16)
                sp.dma_start(W2c[:, k * J1 // 2:(k + 1) * J1 // 2, :],
                             ffn1_W2[bass.ds(e, 1)].rearrange("a (j p) n -> p (a j) n", p=P)).then_inc(w, 16)
                sp.dma_start(colb[:, k * J1 // 2:(k + 1) * J1 // 2],
                             ffn1_b1[bass.ds(e, 1)].rearrange("a (j p) -> p (a j)", p=P),
                             allow_slow_non_contiguous=True).then_inc(w, 16)
                sp.dma_start(rowb[0:1, k * D:(k + 1) * D], ffn1_b2[bass.ds(e, 1)]).then_inc(w, 16)
            for c in range(9):
                sp.wait_ge(sem("out_ready"), c + 1)
                a, n = 3 * c, 3 if c < 8 else 0
                if n:
                    sp.dma_start(pt(out[a * P:(a + n) * P, :]), vals[:, a:a + n, :]).then_inc(sem("out_stored"), 16)
                else:
                    sp.dma_start(out[a * P:N, :], vals[0:TAIL, a, :]).then_inc(sem("out_stored"), 16)
            sp.wait_ge(sem("out_stored"), 16 * 9)
            sp.wait_ge(sem("rows_stored"), 16 * 4 * len(TG))

        @block.gpsimd
        def _(pool):
            c = sem("consts")
            nc.gpsimd.iota(iota[:, :], pattern=[[1, P]], base=0, channel_multiplier=0,
                           allow_small_or_imprecise_dtypes=True).then_inc(c, 1)
            pool.wait_ge(c, 1)
            nc.gpsimd.iota(iotaT, pattern=[[1, NT]], base=0, channel_multiplier=0,
                           allow_small_or_imprecise_dtypes=True).then_inc(c, 1)
            pool.wait_ge(c, 2)
            nc.gpsimd.iota(rowid[:, :], pattern=[[0, 1]], base=0, channel_multiplier=1,
                           allow_small_or_imprecise_dtypes=True).then_inc(c, 1)
            nc.gpsimd.memset(ones[:, :], 1.0).then_inc(c, 1)
            nc.gpsimd.memset(ident[:, :], 0.0).then_inc(c, 1)
            pool.wait_ge(c, 5)
            nc.gpsimd.affine_select(out=ident[:, :], in_=ident[:, :], compare_op=ALU.not_equal, fill=1.0, base=0,
                                    pattern=[[-1, P]], channel_multiplier=1).then_inc(c, 1)
            nc.gpsimd.affine_select(out=tri[:, :], in_=ones[:, :], compare_op=ALU.is_gt, fill=0.0, base=0,
                                    pattern=[[1, P]], channel_multiplier=-1).then_inc(c, 1)
            nc.gpsimd.tensor_scalar(rowok[:, :], rowid[:, :], float(TAIL), None, ALU.is_lt).then_inc(c, 1)

            copied = sem("sort_copied")

            def fill(h, j):
                nc.gpsimd.tensor_copy(idx[:, 8 * h:8 * h + 8], addr[:, bass.ds(j, 8)]).then_inc(copied, 1)
                nc.gpsimd.tensor_copy(srt[:, 8 * h:8 * h + 8, :], edge[:, bass.ds(j, 8), :]).then_inc(copied, 1)

            def scatter(u, rows_n, part):
                pool.indirect_dma_start(records_d.rearrange("p t c -> (p t) c"),
                                        bass.IndirectOffsetOnAxis(ap=idx[0:rows_n, u:u + 1], axis=0),
                                        srt[0:rows_n, u, :], None).then_inc(sem(f"sort_part{part}"), 16)

            pool.wait_ge(sem("recs_empty"), 1)
            for q in (1, 2, 3):
                pool.dma_start(records_d[:, NT * (q - 1) // 3:NT * q // 3], recs[:, NT * (q - 1) // 3:NT * q // 3, :])\
                    .then_inc(sem(f"sort_part{q}"), 16)
            for q in (1, 2, 3):
                pool.wait_ge(sem(f"sort_part{q}"), 16)
            pool.wait_ge(sem("edge_slots"), 1)
            fill(0, 0)
            with pool.Fori(0, EC // U) as it:
                for q in range(4):
                    pool.wait_ge(sem(f"sort_part{(q + 1) % 4}"), it * 128 + (128 if q == 3 else 16))
                    fill((q + 1) % 4, it * U + 8 * q + 8)
                    pool.wait_ge(copied, it * 8 + (2 * q + 2))
                    pool.sem_inc(sem("sort_turn"))
                    for u in range(8 * q, 8 * q + 8):
                        scatter(u, P, q)
            pool.wait_ge(copied, 8 * (EC // U) + 2)
            for u in range(EC % U):
                scatter(u, P if u < EC % U - 1 else EREST, 0)

            def gathers(a):
                pool.wait_ge(sem("rows_stored"), 16 * len(TG) * (a + 1))
                with pool.Fori(0, NT // U) as it:
                    for q in range(U // 8):
                        pool.wait_ge(sem("gather_idx"), it * (U // 8) + (a * NT // 8 + q + 1))
                        for u in range(8 * q, 8 * q + 8):
                            if u % 4 == 0:
                                pool.wait_ge(sem("product"), it * U + (a * NT + u + 4 + U - RING))
                                pool.sem_inc(sem("gather_turn"))
                            pool.indirect_dma_start(g[:, u % RING, 0:D], None, rows_d,
                                                    bass.IndirectOffsetOnAxis(ap=idx[:, u:u + 1], axis=0))\
                                .then_inc(sem(f"gathered{u % RING}"), 16)
                pool.wait_ge(sem("product"), U + (a + 1) * NT)
                pool.sem_inc(sem("agg_gathered"))

            gathers(0)
            for s in range(4):
                pool.wait_ge(sem(f"f_stored{s}"), 16)
            pool.wait_ge(sem("pos_ready"), 1)
            for t in range(T):
                pool.indirect_dma_start(xs_d, bass.IndirectOffsetOnAxis(ap=posI[0:tw(t), t:t + 1], axis=0),
                                        rows[0:tw(t), t, :], None).then_inc(sem("tokens_scattered"), 16)
            for s in range(4):
                pool.wait_ge(sem(f"f_stored{s}"), 16 + 16 * FT // 4)
            for t in range(T):
                pool.indirect_dma_start(vals[0:tw(t), t, :], None, ys_d,
                                        bass.IndirectOffsetOnAxis(ap=posI[0:tw(t), t:t + 1], axis=0))\
                    .then_inc(sem("tokens_back"), 16)
            for a in range(1, 4):
                gathers(a)


        @block.scalar
        def _(act):
            step = [0]

            def link(ins):
                step[0] += 1
                ins.then_inc(sem("act_step"), 1)
                act.wait_ge(sem("act_step"), step[0])

            def sqrt_of(k):
                act.wait_ge(sem("var_ready"), k + 1)
                nc.scalar.sqrt(ln[:, 1, :], ln[:, 0, :]).then_inc(sem("sqrt_ready"), 1)

            def take_transposed(s, dest, relu=False, rows_stage=None):
                for t in range(T + 2):
                    if t < T:
                        act.wait_ge(sem("tr_done"), s * T + t + 1)
                        nc.scalar.activation(dest[:, :, t * P:(t + 1) * P],
                                             banks[t % 2][:, 0:2 * P].rearrange("p (k n) -> p k n", k=KD),
                                             ACT.Relu if relu else ACT.Copy).then_inc(sem("tr_taken"), 1)
                    if rows_stage is not None and t >= 2:
                        act.wait_ge(sem("lin_done"), rows_stage * T + t - 1)
                        nc.scalar.copy(rows[:, t - 2, :], banks[4 + t % 2][:, 0:D]).then_inc(sem("lin_taken"), 1)
                        act.wait_ge(sem("lin_taken"), rows_stage * T + t - 1)
                        act.sem_inc(sem("rows_ready"), 1)

            def take_linearT(first, chunks, dest, bias):
                for e in range(KD):
                    for c, (a, n) in enumerate(chunks):
                        i = e * len(chunks) + c
                        act.wait_ge(sem("lt_done"), first + i + 1)
                        nc.scalar.activation(dest[:, e, a:a + n], banks[2 + i % 2][:, 0:n], ACT.Identity,
                                             bias=bias[:, e:e + 1]).then_inc(sem("lt_taken"), 1)

            def indices(a, it, parts):
                for q in parts:
                    act.wait_ge(sem("product"), it * U + (a * NT + 8 * q + 8))
                    nc.scalar.copy(idx[:, 8 * (q % 4):8 * (q % 4) + 8], recs[:, bass.ds(it * U + 8 * q, 8), 0])\
                        .then_inc(sem("gather_idx"), 1)

            def link_loop(ins, name, k, n, i):
                ins.then_inc(sem(name), 1)
                act.wait_ge(sem(name), k * n + (i + 1))

            def mix_first(k):
                act.wait_ge(sem("m_kv_done"), k + 1)
                nc.scalar.copy(s_x, xT[:, :, bass.ds(k * P, P)]).then_inc(sem("m_x"), 1)
                act.wait_ge(sem("m_proj"), k + 1)
                link_loop(nc.scalar.activation(s_junk, banks[2][:, 0:D], ACT.Copy, accum_out=m1[:, 0:1]), "m_link", k, 3, 0)
                link_loop(nc.scalar.mul(m1[:, 1:2], m1[:, 0:1], -1.0 / D), "m_link", k, 3, 1)
                nc.scalar.activation(s_k2, banks[2][:, 0:D], ACT.Square, bias=m1[:, 1:2],
                                     accum_out=m1[:, 2:3]).then_inc(sem("m_square"), 1)
                nc.scalar.copy(s_v, banks[2][:, D:2 * D]).then_inc(sem("m_v"), 1)
                act.wait_ge(sem("m_scale"), k + 1)
                link_loop(nc.scalar.mul(s_k2, s_k2, m1[:, 4:5]), "m_link", k, 3, 2)
                nc.scalar.square(s_k4, s_k2).then_inc(sem("m_k4"), 1)

            def mix_second(k):
                act.wait_ge(sem("n_mixed"), k + 1)
                act.wait_ge(sem("n_scale"), k + 1)
                nc.scalar.copy(s_x, xT[:, :, bass.ds(k * P, P)]).then_inc(sem("n_x"), 1)
                act.wait_ge(sem("n_proj"), k + 1)
                link_loop(nc.scalar.activation(s_junk, banks[2][:, 0:D], ACT.Copy, accum_out=m1[:, 0:1]), "n_alink", k, 3, 0)
                link_loop(nc.scalar.mul(m1[:, 1:2], m1[:, 0:1], -1.0 / D), "n_alink", k, 3, 1)
                nc.scalar.activation(s_q2, banks[2][:, 0:D], ACT.Square, bias=m1[:, 1:2],
                                     accum_out=m1[:, 2:3]).then_inc(sem("n_square"), 1)
                act.wait_ge(sem("n_square"), k + 1)
                link_loop(nc.scalar.activation(s_junk, s_q2, ACT.Square, accum_out=m1[:, 3:4]), "n_alink", k, 3, 2)
                nc.scalar.sqrt(m1[:, 5:6], m1[:, 3:4]).then_inc(sem("n_root"), 1)
                act.wait_ge(sem("n_qT"), k + 1)
                nc.scalar.copy(s_q2T, banks[0][:, 0:D].rearrange("p (k n) -> p k n", k=KD)).then_inc(sem("n_qT_taken"), 1)

            def self_rows(l, k):
                act.wait_ge(sem("self_taken"), k + (l * T + 1))
                nc.scalar.copy(s_h, hT[:, :, bass.ds(k * P, P)]).then_inc(sem("self_x"), 1)

            def beside(l, k):
                if l > 0:
                    self_rows(l, k)
                if l == 0:
                    mix_first(k)
                elif l == 1:
                    mix_second(k)

            def layer(l):
                last = NT // U - 1
                indices(l + 1, 0, (0, 1))
                with act.Fori(0, last) as it:
                    indices(l + 1, it, (2, 3))
                    beside(l, it * 2)
                    indices(l + 1, it, (4, 5))
                    beside(l, it * 2 + 1)
                indices(l + 1, last, (2, 3))
                beside(l, last * 2)

            sqrt_of(0)
            take_transposed(0, xT)
            take_linearT(0, CH, hT, colb[:, 0:2])
            act.wait_ge(sem("kmax_ready"), 1)
            for k in range(KD):
                nc.scalar.activation(hT[:, k, 0:N], hT[:, k, 0:N], ACT.Exp, bias=kmax[:, k:k + 1],
                                     accum_out=ksum[:, k:k + 1]).then_inc(sem("exp_ready"), 1)
            for t in range(T):
                act.wait_ge(sem("et_done"), t + 1)
                if t >= 2:
                    act.wait_ge(sem("lam_done"), t - 1)
                nc.scalar.copy(xt[0:tw(t), t % 2].rearrange("p k n -> p (k n)"), banks[t % 2][0:tw(t), 0:D])\
                    .then_inc(sem("et_taken"), 1)
            act.wait_ge(sem("bn_var"), 1)
            nc.scalar.sqrt(bnt[:, 2:4], bnt[:, 0:2]).then_inc(sem("bn_sqrt"), 1)
            for k in range(KD):
                act.wait_ge(sem("wqT_done"), k + 1)
                nc.scalar.copy(WqT[:, k, :], banks[k][:, 0:D]).then_inc(sem("wqT_taken"), 1)
            act.wait_ge(sem("mx_done"), KD + 1)
            for k in range(KD):
                nc.scalar.copy(Mx[:, k, :], banks[2 + k][:, 0:D]).then_inc(sem("mx_taken"), 1)
            nc.scalar.copy(rowb[0:1, 256:512], banks[6][0:1, 0:D]).then_inc(sem("mx_taken"), 1)
            act.wait_ge(sem("rwT_done"), 1)
            nc.scalar.copy(rwT, banks[0][:, 0:2 * EX].rearrange("p (k n) -> p k n", k=KD)).then_inc(sem("rwT_taken"), 1)
            act.wait_ge(sem("recs_loaded"), 16)
            with act.Fori(0, NT // U) as it:
                indices(0, it, range(U // 8))
            sqrt_of(1)
            take_transposed(1, xT)
            act.wait_ge(sem("lin_taken"), 3 * T)
            w = sem("w_gnn1")
            act.dma_start(Wio[:, 0], kp(gnn1_Win)).then_inc(w, 16)
            act.dma_start(Wio[:, 1], kp(gnn1_Wout)).then_inc(w, 16)
            for l in range(3):
                act.dma_start(Was[:, l, :, 0:D], kp(gnn1_Wagg[l])).then_inc(w, 16)
                act.dma_start(Was[:, l, :, D:2 * D], kp(gnn1_Wself[l])).then_inc(w, 16)
            act.dma_start(colb[:, 8:10], gnn1_bin.rearrange("(k p) -> p k", p=P), allow_slow_non_contiguous=True).then_inc(w, 16)
            act.dma_start(colb[:, 10:12], mix1_bqkv[2 * D:3 * D].rearrange("(k p) -> p k", p=P), allow_slow_non_contiguous=True).then_inc(w, 16)
            def take_xT(n, b):
                act.wait_ge(sem("f_xt_done"), n + 1)
                act.wait_ge(sem("f_h_done"), n + 1)
                nc.scalar.copy(f_xT[:, b], banks[b][:, 0:2 * P].rearrange("p (k n) -> p k n", k=KD))\
                    .then_inc(sem("f_xt_taken"), 1)

            def take_h(n, b):
                act.wait_ge(sem("f_h_done"), n + 3)
                act.wait_ge(sem("f_o_done"), n + 1)
                nc.scalar.activation(f_h[:, b, :], banks[2 + b][0:H0, 0:P], ACT.Relu).then_inc(sem("f_h_taken"), 1)

            take_xT(0, 0)
            take_xT(1, 1)
            take_h(0, 0)
            def store_tile(n, s):
                act.wait_ge(sem("f_y_ready"), n + 3)
                act.dma_start(ys_d[bass.ds(n * P, P), :], f_y[:, s, :]).then_inc(sem(f"f_stored{s}"), 16)

            with act.Fori(0, FT // 8 - 1) as it:
                for s in range(8):
                    take_xT(it * 8 + (s + 2), s % 2)
                    take_h(it * 8 + (s + 1), (s + 1) % 2)
                    store_tile(it * 8 + s, s % 4)
            for n in range(FT - 8, FT):
                if n + 2 < FT:
                    take_xT(n + 2, n % 2)
                if n + 1 < FT:
                    take_h(n + 1, (n + 1) % 2)
                store_tile(n, n % 4)
            for w in range(2):
                act.wait_ge(sem("WT_done"), w + 1)
                for k in range(KD):
                    nc.scalar.copy(WT[:, w, k, :], banks[k][:, 0:D]).then_inc(sem("WT_taken"), 1)
            act.wait_ge(sem("fold_done"), 4)
            for k in range(KD):
                nc.scalar.copy(Was[:, 0, k, :], banks[2 + k][:, :]).then_inc(sem("fold_taken"), 1)
                nc.scalar.copy(Wvo[:, k, :], banks[4 + k][:, 0:D]).then_inc(sem("fold_taken"), 1)
            nc.scalar.copy(rowb[0:1, 768:1024], banks[7][0:1, 0:D]).then_inc(sem("fold_taken"), 1)
            sqrt_of(2)
            take_transposed(2, xT)
            for l in range(3):
                if l == 1:
                    act.wait_ge(sem("kn_ready"), 1)
                    nc.scalar.sqrt(kn[:, 2:4], kn[:, 0:2]).then_inc(sem("kn_sqrt"), 1)
                    act.wait_ge(sem("kvT_done"), 1)
                    for k in range(KD):
                        nc.scalar.copy(kvT[:, k, :], banks[k][:, 0:D]).then_inc(sem("kvT_taken"), 1)
                    act.wait_ge(sem("m2_done"), 1)
                    for k in range(KD):
                        nc.scalar.copy(kv[:, k, :], banks[2 + k][:, 0:D]).then_inc(sem("m2_taken"), 1)
                layer(l)
                take_transposed(3 + l, hT, relu=True, rows_stage=4 + l if l < 2 else None)
            sqrt_of(3)
            take_transposed(6, xT)
            act.wait_ge(sem("rt_exp1"), 1)
            nc.scalar.activation(top[0:1, 16:24], top[0:1, 8:16], ACT.Exp).then_inc(sem("rt_exp1d"), 1)
            act.wait_ge(sem("rt_exp2"), 1)
            nc.scalar.activation(top[0:1, 16:24], top[0:1, 8:16], ACT.Exp).then_inc(sem("rt_exp2d"), 1)
            act.wait_ge(sem("rt_exp3"), 1)
            nc.scalar.activation(top[0:1, 50:52], top[0:1, 48:50], ACT.Exp).then_inc(sem("rt_exp3d"), 1)
            act.wait_ge(sem("w_ffn1"), 160)
            i = 0
            for c in range(9):
                n = 384 if c < 8 else P
                for j in range(J1):
                    act.wait_ge(sem("h1_done"), i + 1)
                    if j == 0 and c >= 2:
                        act.wait_ge(sem("y1_done"), 3 * (c - 1))
                    nc.scalar.activation(gel[:, c % 2, j, 0:n], banks[i % 4][:, 0:n], ACT.Gelu,
                                         bias=colb[:, j:j + 1]).then_inc(sem("h1_taken"), 1)
                    i += 1

        @block.vector
        def _(dve):
            step = [0]
            V = nc.vector

            def link(ins):
                step[0] += 1
                ins.then_inc(sem("dve_step"), 1)
                dve.wait_ge(sem("dve_step"), step[0])

            def layer_norm(k, source, dest, ready, after=None):
                for t in range(T):
                    last = V.bn_stats(stats[:, t, :], source[:, t, :])
                link(last)
                for t in range(T):
                    last = V.bn_aggr(mv[:, t, :], stats[:, t, :])
                link(last)
                V.tensor_scalar(ln[:, 0, :], mv[:, :, 1], EPS, None, ALU.add).then_inc(sem("var_ready"), 1)
                dve.wait_ge(sem("sqrt_ready"), k + 1)
                link(V.reciprocal(ln[:, 2, :], ln[:, 1, :]))
                newton(ln[:, 2, :], ln[:, 0, :], ln[:, 3, :])
                for t in range(T + 4):
                    if t < T:
                        V.tensor_scalar(dest[:, t, :], source[:, t, :], mv[:, t, 0:1], ln[:, 2, t:t + 1],
                                        ALU.subtract, ALU.mult).then_inc(sem(ready), 1)
                    if after and t >= 4:
                        after(t - 4)

            def newton(r, v, tmp):
                link(V.tensor_tensor(tmp, r, r, ALU.mult))
                link(V.tensor_tensor(tmp, tmp, v, ALU.mult))
                link(V.tensor_scalar(tmp, tmp, -0.5, 1.5, ALU.mult, ALU.add))
                link(V.tensor_tensor(r, r, tmp, ALU.mult))

            V.memset(zero_row, 0.0).then_inc(sem("zero_row"), 1)
            V.memset(srcI[:, EC - 1:EC], T * P).then_inc(sem("edge_pad_set"), 1)
            V.memset(dstI[:, EC - 1:EC], 0).then_inc(sem("edge_pad_set"), 1)
            V.memset(wE[:, EC - 1:EC], 0.0).then_inc(sem("edge_pad_set"), 1)
            V.memset(x_sb[:, T - 1, :], 0.0).then_inc(sem("x_pad_set"), 1)
            link(V.memset(recs[:, :, :], 0.0))
            V.memset(recs[:, :, 1], -1.0).then_inc(sem("recs_empty"), 1)
            V.memset(oneF, 1.0)
            V.memset(addr[:, EC:EP], 0.0)
            link(V.memset(edge[:, EC:EP, :], 0.0))
            dve.wait_ge(sem("edges_loaded"), 96)
            link(V.tensor_scalar(tmpI, srcI, 7, None, ALU.logical_shift_right))
            link(V.tensor_copy(binF, tmpI))
            link(V.tensor_scalar(tmpI, srcI, P - 1, None, ALU.bitwise_and))
            V.tensor_copy(edge[:, 0:EC, 1], tmpI)
            V.tensor_copy(edge[:, 0:EC, 0], dstI)
            V.tensor_copy(edge[:, 0:EC, 2], wE)
            for b in range(T):
                last = V.tensor_scalar(ohs[:, b, :], binF, float(b), None, ALU.is_equal, ALU.add,
                                       accum_out=rowtot[:, b:b + 1])
            last.then_inc(sem("edge_rowtot"), 1)

            def slots_of(nb, pre, total, k):
                dve.wait_ge(sem("bin_counts"), k + 1)
                link(V.tensor_scalar(cntI[:, 0:nb], total, float(P - 1), None, ALU.add))
                link(V.tensor_scalar(cntI[:, 0:nb], cntI[:, 0:nb], 7, None, ALU.logical_shift_right))
                link(V.tensor_copy(cnt[:, 0:nb], cntI[:, 0:nb]))
                link(V.tensor_tensor_scan(endt[:, 0:nb], ones[:, 0:nb], cnt[:, 0:nb], 0.0, ALU.mult, ALU.add))
                link(V.tensor_tensor(off[:, 0:nb], endt[:, 0:nb], cnt[:, 0:nb], ALU.subtract))
                link(V.tensor_scalar(off[:, 0:nb], off[:, 0:nb], float(P), -1.0, ALU.mult, ALU.add))
                link(V.tensor_tensor(off[:, 0:nb], off[:, 0:nb], pre, ALU.add))

            slots_of(T, banks[7][:, 0:T], banks[7][:, 32:32 + T], 0)
            link(V.memset(posF, 0.0))
            for b in range(T):
                link(V.tensor_tensor_scan(scanF, oneF, ohs[:, b, :], off[:, b:b + 1], ALU.mult, ALU.add))
                link(V.tensor_tensor(prodF, scanF, ohs[:, b, :], ALU.mult))
                link(V.tensor_tensor(posF, posF, prodF, ALU.add))
            link(V.tensor_copy(tmpI, posF))
            link(V.tensor_scalar(srcI, tmpI, P - 1, None, ALU.bitwise_and))
            link(V.tensor_scalar(tmpI, tmpI, 7, None, ALU.logical_shift_right))
            V.scalar_tensor_tensor(posF, srcI, float(NT), tmpI, ALU.mult, ALU.add).then_inc(sem("edge_slots"), 1)
            dve.wait_ge(sem("edge_slots"), 1)
            dve.wait_ge(sem("consts"), 8)
            q = NT // 4
            cmp = accF[32:33, 0:q * T].rearrange("p (t b) -> p t b", b=T)
            for i in range(4):
                link(V.tensor_tensor(cmp, iotaT[:, i * q:(i + 1) * q].unsqueeze(2).to_broadcast([1, q, T]),
                                     endt[32:33, 0:T].unsqueeze(1).to_broadcast([1, q, T]), ALU.is_ge))
                link(V.tensor_reduce(accF[32:33, q * T:q * T + q], cmp, AX, ALU.add))
                link(V.tensor_copy(bins[:, i * q:(i + 1) * q], accF[32:33, q * T:q * T + q]))

            dve.wait_ge(sem("x_loaded"), 32)
            layer_norm(0, x_sb, rows, "normed")
            V.memset(accF[:, :], 0.0).then_inc(sem("acc_zero"), 1)
            dve.wait_ge(sem("w_block0"), 11 * 16)
            for t in range(T):
                b = banks[4 + t % 2]
                dve.wait_ge(sem("lin_done"), t + 1)
                V.tensor_copy(rows[:, t, :], b[:, 0:D]).then_inc(sem("rows_ready"), 1)
                V.tensor_tensor(vals[:, t, :], b[:, D:2 * D], bcast[:, :], ALU.add).then_inc(sem("lin_taken"), 1)
            dve.wait_ge(sem("lin_taken"), T)
            dve.sem_inc(sem("v_bias_used"))
            dve.wait_ge(sem("lt_taken"), KD * len(CH))
            for k in range(KD):
                last = V.tensor_reduce(kmax[:, k:k + 1], hT[:, k, 0:N], AX, ALU.max, negate=True)
            last.then_inc(sem("kmax_ready"), 1)
            dve.wait_ge(sem("exp_ready"), KD)
            link(V.reciprocal(kinv, ksum))
            dve.wait_ge(sem("lam_done"), T)
            for k in range(KD):
                last = V.tensor_scalar(bn[:, k, :], banks[4 + k][:, 0:D], kinv[:, k:k + 1], None, ALU.mult)
            link(last)
            for k in range(KD):
                link(V.bn_stats(bnst[:, 6 * k:6 * k + 6], bn[:, k, :]))
                link(V.bn_aggr(bnmv[:, 2 * k:2 * k + 2], bnst[:, 6 * k:6 * k + 6]))
            V.tensor_scalar(bnt[:, 0:2], bnmv.rearrange("p (k c) -> p k c", c=2)[:, :, 1], EPS, None, ALU.add)\
                .then_inc(sem("bn_var"), 1)
            dve.wait_ge(sem("bn_sqrt"), 1)
            link(V.reciprocal(bnt[:, 4:6], bnt[:, 2:4]))
            newton(bnt[:, 4:6], bnt[:, 0:2], bnt[:, 6:8])
            for k in range(KD):
                link(V.tensor_scalar(bn[:, k, :], bn[:, k, :], bnmv[:, 2 * k:2 * k + 1], bnt[:, 4 + k:5 + k],
                                     ALU.subtract, ALU.mult))
                V.tensor_scalar(bn[:, k, :], bn[:, k, :], colb[:, 4 + k:5 + k], colb[:, 6 + k:7 + k],
                                ALU.mult, ALU.add).then_inc(sem("bn_ready"), 1)
            for t in range(T):
                dve.wait_ge(sem("lin_done"), T + t + 1)
                V.tensor_tensor(x_sb[:, t, :], x_sb[:, t, :], banks[4 + t % 2][:, 0:D], ALU.add)\
                    .then_inc(sem("lin_taken"), 1)

            def row_matrices(a, slot, tiles, done):
                m = oh[:, slot:slot + AHEAD, :]
                ins = V.tensor_tensor(m, iota[:, :].unsqueeze(1).to_broadcast([P, AHEAD, P]),
                                      recs[:, tiles, 1].unsqueeze(2).to_broadcast([P, AHEAD, P]), ALU.is_equal)
                if a == 0:
                    ins.then_inc(sem("matrix_01"), 1)
                    dve.wait_ge(sem("matrix_01"), done)
                    ins = V.tensor_tensor(m, m, recs[:, tiles, 2].unsqueeze(2).to_broadcast([P, AHEAD, P]), ALU.mult)
                ins.then_inc(sem("row_matrix"), 1)

            def sum_products(a, it, u):
                if u % AHEAD == 0:
                    row_matrices(a, (u + AHEAD) % MRING, bass.ds(it * U + (u + AHEAD), AHEAD),
                                 it * (U // AHEAD) + (u // AHEAD + 2))
                tile = dve.value_load(bins[:, bass.ds(it * U + u, 1)]).with_bounds(min_val=0, max_val=T)
                if u % 2 == 0:
                    dve.wait_ge(sem("product"), it * U + (a * NT + u + 2 + U))
                dve.wait_ge(sem("summed"), it * U + (a * NT + u + SLOTS))
                to = acc[:, bass.ds(tile, 1), :].rearrange("p a b -> p (a b)")
                V.tensor_tensor(to, to, banks[4 + u % SLOTS][:, 0:AW], ALU.add).then_inc(sem("summed"), 1)

            def start_sums(a):
                dve.wait_ge(sem("rows_stored"), 16 * len(TG) * (a + 1))
                V.memset(g[:, :, D:AW], 1.0).then_inc(sem("g_ones"), 1)
                row_matrices(a, 0, slice(0, AHEAD), 1)

            def take_self(k):
                dve.wait_ge(sem("self_done"), k[1])
                V.tensor_tensor(vals[:, bass.ds(k[0], 1), :].rearrange("p a b -> p (a b)"), banks[3][:, D:2 * D],
                                bcast[:, :], ALU.add).then_inc(sem("self_taken"), 1)

            def beside(l, k, u):
                xk = x_sb[:, bass.ds(k, 1), :].rearrange("p a b -> p (a b)")
                if l == 0 and u == 6:
                    dve.wait_ge(sem("m_square"), k + 1)
                    link_loop(V.tensor_scalar(m1[:, 3:4], m1[:, 2:3], 1e-7, None, ALU.add), "m_plus", k, 1, 0)
                    V.reciprocal(m1[:, 4:5], m1[:, 3:4]).then_inc(sem("m_scale"), 1)
                if l == 0 and u == 10:
                    dve.wait_ge(sem("m_out"), k + 1)
                    V.tensor_tensor(xk, xk, banks[3][:, 0:D], ALU.add).then_inc(sem("m_out_taken"), 1)
                    take_self((k, k + 1))
                if l == 1 and u == 8:
                    dve.wait_ge(sem("n_root"), k + 1)
                    link_loop(V.tensor_scalar(m1[:, 8:9], m1[:, 2:3], 1e-7, None, ALU.add), "n_link", k, 4, 0)
                    link_loop(V.reciprocal(m1[:, 9:10], m1[:, 8:9]), "n_link", k, 4, 1)
                    link_loop(V.tensor_scalar(m1[:, 10:11], m1[:, 5:6], m1[:, 9:10], 1e-12, ALU.mult, ALU.max),
                              "n_link", k, 4, 2)
                    link_loop(V.reciprocal(m1[:, 11:12], m1[:, 10:11]), "n_link", k, 4, 3)
                    V.tensor_tensor(m1[:, 12:13], m1[:, 11:12], m1[:, 9:10], ALU.mult).then_inc(sem("n_scale"), 1)
                if l == 1 and u == 13:
                    dve.wait_ge(sem("n_mixed"), k + 2)
                    dve.wait_ge(sem("n_scale"), k + 2)
                    V.scalar_tensor_tensor(xk, banks[1][:, 0:D], m1[:, 12:13], xk, ALU.mult, ALU.add)\
                        .then_inc(sem("n_mixed_taken"), 1)
                if l >= 1 and u == 5:
                    take_self((k, k + (l * T + 1)))

            def link_loop(ins, name, k, n, i):
                ins.then_inc(sem(name), 1)
                dve.wait_ge(sem(name), k * n + (i + 1))

            def layer_sums(l):
                start_sums(l + 1)
                last = NT // U - 1
                with dve.Fori(0, last) as it:
                    for u in range(U):
                        beside(l, it * 2 + u // 16, u % 16)
                        sum_products(l + 1, it, u)
                for u in range(U):
                    if u < 16:
                        beside(l, last * 2, u)
                    sum_products(l + 1, last, u)
                dve.wait_ge(sem("summed"), (l + 2) * NT + SLOTS)

            dve.wait_ge(sem("recs_loaded"), 16)
            for s in range(4):
                dve.wait_ge(sem(f"f_stored{s}"), 16)
            start_sums(0)
            with dve.Fori(0, NT // U) as it:
                for u in range(U):
                    sum_products(0, it, u)
            dve.wait_ge(sem("summed"), NT + SLOTS)
            link(V.tensor_tensor(x_sb[:, :, :], x_sb[:, :, :], acc[:, 0:T, 0:D], ALU.add))
            dve.wait_ge(sem("rows_stored"), 16 * len(TG))
            layer_norm(1, x_sb, rows, "normed")
            for t in range(T):
                dve.wait_ge(sem("lin_done"), 2 * T + t + 1)
                V.tensor_copy(r_lg[:, t, :], banks[4 + t % 2][:, 0:EX]).then_inc(sem("lin_taken"), 1)
            dve.wait_ge(sem("lin_taken"), 3 * T)
            for t in range(T):
                last = V.max(out=r_m8[:, t, :], in_=r_lg[:, t, :])
            link(last)
            for t in range(T):
                last = (V.max_index(out=r_i8[:, t, :], in_max=r_m8[:, t, :], in_values=r_lg[:, t, :]))
            link(last)
            link(V.tensor_copy(r_eid, r_i8[:, :, 0]))
            link(V.tensor_tensor(r_oh, iota[:, 0:EX].unsqueeze(2).to_broadcast([P, EX, T]),
                                 r_eid.unsqueeze(1).to_broadcast([P, EX, T]), ALU.is_equal))
            link(V.tensor_scalar(r_oh[:, :, T - 1], r_oh[:, :, T - 1], rowok[:, :], None, ALU.mult))
            V.tensor_reduce(rowtot[:, 0:EX], r_oh, AX, ALU.add).then_inc(sem("edge_rowtot"), 1)
            link(V.memset(r_msk, 1.0))
            link(V.memset(r_msk[:, :, 0], 0.0))
            link(V.tensor_tensor_scan(r_sc.rearrange("p b t -> p (b t)"), r_msk.rearrange("p b t -> p (b t)"),
                                      r_oh.rearrange("p b t -> p (b t)"), 0.0, ALU.mult, ALU.add))
            slots_of(EX, banks[7][:, 0:EX], banks[7][:, 32:32 + EX], 1)
            link(V.tensor_tensor(r_sc, r_sc, off[:, 0:EX].unsqueeze(2).to_broadcast([P, EX, T]), ALU.add))
            link(V.tensor_tensor(r_sc, r_sc, r_oh, ALU.mult))
            link(V.tensor_reduce(r_eid, r_sc.rearrange("p b t -> p t b"), AX, ALU.add))
            link(V.tensor_copy(posI[:, 0:T], r_eid))
            V.memset(invdeg, 0.0).then_inc(sem("pos_ready"), 1)
            ce = wB[0:3 * EX, 0:FT * EX].rearrange("p (t b) -> p t b", b=EX)
            link(V.tensor_tensor(ce, iota[0:3 * EX, 0:FT].unsqueeze(2).to_broadcast([3 * EX, FT, EX]),
                                 endt[0:3 * EX, 0:EX].unsqueeze(1).to_broadcast([3 * EX, FT, EX]), ALU.is_ge))
            link(V.tensor_reduce(f_exp, ce, AX, ALU.add))
            link(V.tensor_scalar(f_exp, f_exp, float(EX - 1), None, ALU.min))
            V.tensor_copy(eidx[32:33, 0:FT], f_exp[32:33, :]).then_inc(sem("expert_table"), 1)
            link(V.tensor_scalar(f_row, ones[0:3 * EX, :], rowid[0:3 * EX, :], None, ALU.mult))
            for i in (1, 2):
                r = f_row[EX * i:EX * (i + 1), :]
                link(V.tensor_scalar(r, r, float(EX * i), None, ALU.subtract))
            dve.wait_ge(sem("f_biases"), 96)
            link(V.tensor_copy(f_parts, f_b))
            for i in (1, 2):
                for j in range(i, 3):
                    s = slice(EX * j, EX * (j + 1))
                    link(V.tensor_tensor(f_rest[s, :], (f_b if i == 1 else f_rest)[s, :], f_parts[s, :], ALU.subtract))
                    link(V.tensor_copy(f_parts[s, :], f_rest[s, :]))
            dve.sem_inc(sem("f_parts"), 1)

            def select(s, e):
                V.tensor_scalar(f_sel[:, s, :], f_row, e, None, ALU.is_equal).then_inc(sem("f_selected"), 1)

            def take_y(n, s, stored):
                dve.wait_ge(sem("f_o_done"), n + 3)
                dve.wait_ge(sem(f"f_stored{s}"), stored)
                V.tensor_scalar(f_y[:, s, :], banks[4 + s % 2][:, 0:D], 0.0, None, ALU.max)\
                    .then_inc(sem("f_y_ready"), 1)

            for s in range(4):
                select(s, f_exp[:, s:s + 1])
            dve.sem_inc(sem("f_y_ready"), 2)
            with dve.Fori(0, FT // 8 - 1) as it:
                for s in range(8):
                    take_y(it * 8 + s, s % 4, it * 32 + (16 + 16 * (s // 4)))
                    select(s % 4, f_exp[:, bass.ds(it * 8 + (s + 4), 1)])
            for n in range(FT - 8, FT):
                take_y(n, n % 4, 16 + 16 * (n // 4))
                if n + 4 < FT:
                    select(n % 4, f_exp[:, n + 4:n + 5])
            dve.wait_ge(sem("w_gnn1"), 10 * 16)
            for k in range(KD):
                V.tensor_scalar(b_in[:, k, :], ones[:, :], colb[:, 8 + k:9 + k], None, ALU.mult).then_inc(sem("b_in_ready"), 1)
            dve.wait_ge(sem("fold_done"), 4)
            V.tensor_copy(gbias, banks[6][:, 0:D]).then_inc(sem("gbias_ready"), 1)
            dve.wait_ge(sem("bhid_loaded"), 16)
            link(V.tensor_tensor(bcast[:, :], bcast[:, :], banks[6][:, D:2 * D], ALU.add))
            dve.sem_inc(sem("bhid_used"), 1)
            dve.wait_ge(sem("gbias_ready"), 1)
            dve.wait_ge(sem("tokens_back"), 16 * T)
            link(V.tensor_tensor(x_sb[:, 0:T - 1, :], x_sb[:, 0:T - 1, :], vals[:, 0:T - 1, :], ALU.add))
            link(V.tensor_tensor(x_sb[0:TAIL, T - 1, :], x_sb[0:TAIL, T - 1, :], vals[0:TAIL, T - 1, :], ALU.add))
            def rows_out(t):
                dve.wait_ge(sem("lin_done"), 3 * T + t + 1)
                V.tensor_tensor(rows[:, t, :], banks[4 + t % 2][:, 0:D], gbias, ALU.add).then_inc(sem("lin_taken"), 1)
                dve.wait_ge(sem("lin_taken"), 3 * T + t + 1)
                dve.sem_inc(sem("rows_ready"), 1)

            layer_norm(2, x_sb, rows, "normed", after=rows_out)
            dve.sem_inc(sem("self_taken"), 1)
            dve.wait_ge(sem("rows_ready"), 2 * T)
            for l in range(3):
                dve.wait_ge(sem("normed"), (3 + l) * T)
                link(V.memset(accF[:, :], 0.0))
                dve.wait_ge(sem("bhid_used"), 1) if l == 0 else dve.wait_ge(sem("bhid_loaded"), 16 * (l + 1))
                if l == 1:
                    dve.wait_ge(sem("kn_sqrt"), 1)
                    link(V.tensor_scalar(kn[:, 2:4], kn[:, 2:4], 1e-12, None, ALU.max))
                    link(V.reciprocal(kn[:, 0:2], kn[:, 2:4]))
                    link(V.tensor_scalar(kn[:, 0:2], kn[:, 0:2], float(N) ** -0.5, None, ALU.mult))
                    for k in range(KD):
                        V.tensor_scalar(kvs[:, k, :], kv[:, k, :], kn[:, k:k + 1], None, ALU.mult)\
                            .then_inc(sem("kv_scaled"), 1)
                layer_sums(l)
                if l == 0:
                    dve.wait_ge(sem("kv_closed"), 1)
                    for k in range(KD):
                        V.tensor_copy(kv[:, k, :], banks[k][:, 0:D]).then_inc(sem("kv_saved"), 1)
                        V.tensor_copy(kn[:, k:k + 1], banks[k][:, D:AW]).then_inc(sem("kv_saved"), 1)
                    dve.wait_ge(sem("kv_saved"), 2 * KD)
                    dve.sem_inc(sem("kn_ready"), 1)
                    link(V.tensor_scalar(invdeg, acc[:, 0:T, D], 1.0, None, ALU.max))
                    link(V.reciprocal(invdeg, invdeg))
                for t in range(T + 4):
                    if t < T:
                        V.scalar_tensor_tensor(rows[:, t, :], acc[:, t, 0:D], invdeg[:, t:t + 1], vals[:, t, :],
                                               ALU.mult, ALU.add).then_inc(sem("normed"), 1)
                    if l == 2 and t >= 4:
                        dve.wait_ge(sem("lin_done"), 6 * T + t - 3)
                        V.tensor_tensor(x_sb[:, t - 4, :], x_sb[:, t - 4, :], banks[4 + t % 2][:, 0:D], ALU.add)\
                            .then_inc(sem("lin_taken"), 1)
            dve.wait_ge(sem("lin_taken"), 7 * T)
            dve.wait_ge(sem("tr_done"), 6 * T)
            layer_norm(3, x_sb, rows, "normed")
            dve.wait_ge(sem("tr_taken"), 7 * T)
            for k in range(KD):
                link(V.tensor_reduce(kmax[:, k:k + 1], xT[:, k, 0:N], AX, ALU.add))
            V.tensor_scalar(ksum, kmax, 1.0 / N, None, ALU.mult).then_inc(sem("mean_ready"), 1)
            lg, e8, p8 = top[0:1, 0:8], top[0:1, 8:16], top[0:1, 16:24]
            s1, s2, s3, v8 = top[0:1, 24:25], top[0:1, 25:26], top[0:1, 32:40], top[0:1, 40:48]
            dve.wait_ge(sem("route_done"), 1)
            dve.wait_ge(sem("wr_loaded"), 32)
            link(V.tensor_tensor(lg, banks[7][0:1, 0:EX1], rowb[0:1, 512:520], ALU.add))

            def softmax8(k):
                link(V.tensor_reduce(s1, lg, AX, ALU.max))
                V.tensor_scalar(e8, lg, s1, None, ALU.subtract).then_inc(sem(f"rt_exp{k}"), 1)
                dve.wait_ge(sem(f"rt_exp{k}d"), 1)
                link(V.tensor_reduce(s1, p8, AX, ALU.add))
                link(V.reciprocal(s2, s1))
                link(V.tensor_scalar(p8, p8, s2, None, ALU.mult))

            softmax8(1)
            link(V.tensor_scalar(s3, p8, float(N), None, ALU.mult))
            link(V.tensor_scalar(v8, s3, CAPACITY, None, ALU.is_gt))
            link(V.reciprocal(s3, s3))
            link(V.tensor_scalar(s3, s3, CAPACITY, -1.0, ALU.mult, ALU.add))
            link(V.tensor_tensor(s3, s3, v8, ALU.mult))
            link(V.tensor_scalar(s3, s3, 1.0, None, ALU.add))
            link(V.tensor_tensor(lg, p8, s3, ALU.mult))
            softmax8(2)
            link(V.max(out=v8, in_=p8))
            link(V.max_index(out=eidx[0:1, 8:16].bitcast(U32), in_max=v8, in_values=p8))
            link(V.tensor_copy(top[0:1, 56:64], eidx[0:1, 8:16].bitcast(U32)))
            V.tensor_copy(eidx[0:1, 0:8], top[0:1, 56:64]).then_inc(sem("experts_chosen"), 1)
            V.tensor_scalar(top[0:1, 48:50], v8[:, 0:2], v8[:, 0:1], None, ALU.subtract).then_inc(sem("rt_exp3"), 1)
            dve.wait_ge(sem("rt_exp3d"), 1)
            link(V.tensor_reduce(s1, top[0:1, 50:52], AX, ALU.add))
            link(V.reciprocal(s2, s1))
            V.tensor_scalar(top[0:1, 52:54], top[0:1, 50:52], s2, None, ALU.mult).then_inc(sem("gates_ready"), 1)
            dve.wait_ge(sem("gates_spread"), 1)
            link(V.tensor_copy(kinv, banks[7][:, 16:18]))
            dve.wait_ge(sem("w_ffn1"), 160)
            for k in range(2):
                link(V.tensor_scalar(rowb[0:1, k * D:(k + 1) * D], rowb[0:1, k * D:(k + 1) * D], kinv[0:1, k:k + 1],
                                     None, ALU.mult))
            link(V.tensor_tensor(rowb[0:1, 0:D], rowb[0:1, 0:D], rowb[0:1, D:2 * D], ALU.add))
            for j in range(J1):
                V.tensor_scalar(W2c[:, j, :], W2c[:, j, :], kinv[:, j * 2 // J1:j * 2 // J1 + 1], None, ALU.mult)\
                    .then_inc(sem("w2_scaled"), 1)
            for c in range(9):
                ts = range(3 * c, min(3 * c + 3, T))
                a, b = ts[0], ts[-1] + 1
                for t in ts:
                    dve.wait_ge(sem("y1_done"), t + 1)
                    V.tensor_tensor(rows[:, t, :], rows[:, t, :], banks[4 + t % 2][:, 0:D], ALU.add)\
                        .then_inc(sem("y1_taken"), 1)
                dve.wait_ge(sem("y1_taken"), b)
                for t in ts:
                    last = V.bn_stats(stats[:, t, :], rows[:, t, :])
                link(last)
                for t in ts:
                    last = V.bn_aggr(mv[:, t, :], stats[:, t, :])
                link(last)
                link(V.tensor_scalar(ln[:, 0, a:b], mv[:, a:b, 1], EPS, None, ALU.add))
                bits = ln[:, 2, a:b].bitcast(I32)
                link(V.tensor_scalar(bits, ln[:, 0, a:b].bitcast(I32), 1, None, ALU.logical_shift_right))
                link(V.tensor_scalar(bits, bits, -1.0, float(0x5f3759df), ALU.mult, ALU.add))
                for _ in range(3):
                    newton(ln[:, 2, a:b], ln[:, 0, a:b], ln[:, 3, a:b])
                for t in ts:
                    last = V.tensor_scalar(vals[:, t, :], rows[:, t, :], mv[:, t, 0:1], ln[:, 2, t:t + 1],
                                           ALU.subtract, ALU.mult)
                link(last)
                v = vals[:, a:b, :]
                link(V.tensor_tensor(v, v, bcast[:, :].unsqueeze(1).to_broadcast([P, b - a, D]), ALU.mult))
                link(V.tensor_tensor(v, v, wB[:, 0:D].unsqueeze(1).to_broadcast([P, b - a, D]), ALU.add))
                V.tensor_tensor(v, v, x_sb[:, a:b, :], ALU.add).then_inc(sem("out_ready"), 1)

        @block.tensor
        def _(pe):
            mm, tr = nc.tensor.matmul, nc.tensor.transpose

            def transpose(s, t):
                pe.wait_ge(sem("normed"), s * T + t + 1)
                if s * T + t >= 2:
                    pe.wait_ge(sem("tr_taken"), s * T + t - 1)
                for k in range(KD):
                    last = tr(banks[t % 2][:, k * P:(k + 1) * P], rows[:, t, k * P:(k + 1) * P], ident[:, :])
                last.then_inc(sem("tr_done"), 1)

            def transposes(s):
                for t in range(T):
                    transpose(s, t)

            def transposes_and_linear(s, s2, source, W, n, bias=None):
                for t in range(T + 2):
                    if t < T:
                        transpose(s, t)
                    if t >= 2:
                        pe.wait_ge(sem("tr_taken"), s * T + t - 1)
                        linear_tile(s2, t - 2, source, W, n, bias)

            def linear_tile(s, t, source, W, n, bias=None):
                pe.wait_ge(sem("lin_taken"), s * T + max(t - 1, 0)) if s or t >= 2 else None
                o = banks[4 + t % 2][:, 0:n]
                if bias is not None:
                    mm(o, ones[0:1, :], bias, start=True, stop=False)
                for k in range(KD):
                    last = mm(o, source[:, k, t * P:(t + 1) * P], W[:, k, 0:n],
                              start=k == 0 and bias is None, stop=k == KD - 1)
                last.then_inc(sem("lin_done"), 1)

            def linear(s, source, W, n, bias=None):
                for t in range(T):
                    linear_tile(s, t, source, W, n, bias)

            def linearT(first, chunks, W):
                for e in range(KD):
                    for c, (a, n) in enumerate(chunks):
                        i = e * len(chunks) + c
                        if first + i >= 2:
                            pe.wait_ge(sem("lt_taken"), first + i - 1)
                        for k in range(KD):
                            last = mm(banks[2 + i % 2][:, 0:n], W[:, k, e * P:(e + 1) * P], xT[:, k, a:a + n],
                                      start=k == 0, stop=k == KD - 1)
                        last.then_inc(sem("lt_done"), 1)

            def bin_counts(nb, k):
                pe.wait_ge(sem("edge_rowtot"), k + 1)
                mm(banks[7][:, 0:nb], tri[:, :], rowtot[:, 0:nb], start=True, stop=True)
                mm(banks[7][:, 32:32 + nb], ones[:, :], rowtot[:, 0:nb], start=True, stop=True)\
                    .then_inc(sem("bin_counts"), 1)

            pe.wait_ge(sem("consts"), 8)
            bin_counts(T, 0)
            transposes(0)
            pe.wait_ge(sem("w_block0"), 11 * 16)
            pe.wait_ge(sem("tr_taken"), T)
            linear(0, xT, W0V, 2 * D)
            linearT(0, CH, Wk)
            pe.wait_ge(sem("exp_ready"), KD)
            pe.wait_ge(sem("lin_taken"), T)
            for t in range(T + 1):
                if t < T:
                    if t >= 2:
                        pe.wait_ge(sem("et_taken"), t - 1)
                    for k in range(KD):
                        last = tr(banks[t % 2][0:tw(t), k * P:(k + 1) * P], hT[:, k, t * P:t * P + tw(t)], ident[:, :])
                    last.then_inc(sem("et_done"), 1)
                if t >= 1:
                    u = t - 1
                    pe.wait_ge(sem("et_taken"), u + 1)
                    for k in range(KD):
                        last = mm(banks[4 + k][:, 0:D], xt[0:tw(u), u % 2, k, :], vals[0:tw(u), u, :],
                                  start=u == 0, stop=u == T - 1)
                    last.then_inc(sem("lam_done"), 1)
            pe.wait_ge(sem("et_taken"), T)
            for k in range(KD):
                for j in range(KD):
                    last = tr(banks[k][:, j * P:(j + 1) * P], Wq[:, j, k * P:(k + 1) * P], ident[:, :])
                last.then_inc(sem("wqT_done"), 1)
            pe.wait_ge(sem("wqT_taken"), KD)
            pe.wait_ge(sem("bn_ready"), KD)
            pe.wait_ge(sem("lt_taken"), KD * len(CH))
            for j in range(KD):
                for k in range(KD):
                    last = mm(banks[2 + j][:, 0:D], WqT[:, k, j * P:(j + 1) * P], bn[:, k, :],
                              start=k == 0, stop=k == KD - 1)
                last.then_inc(sem("mx_done"), 1)
            for k in range(KD):
                last = mm(banks[6][0:1, 0:D], colb[:, 2 + k:3 + k], bn[:, k, :], start=k == 0, stop=k == KD - 1)
            last.then_inc(sem("mx_done"), 1)
            for k in range(KD):
                last = tr(banks[0][:, k * EX:(k + 1) * EX], rw[:, k * P:(k + 1) * P], ident[0:EX, 0:EX])
            last.then_inc(sem("rwT_done"), 1)
            pe.wait_ge(sem("mx_taken"), KD + 1)
            linear(1, xT, Mx, D, rowb[0:1, 256:512])

            def product(a, it, u):
                pe.wait_ge(sem(f"gathered{u % RING}"), it * (16 * U // RING) + (16 * (a * NT // RING + u // RING + 1)))
                if u % AHEAD == 0:
                    pe.wait_ge(sem("row_matrix"), it * (U // AHEAD) + (a * (NT // AHEAD + 1) + u // AHEAD + 1))
                pe.wait_ge(sem("summed"), it * U + (a * NT + u + 1))
                mm(banks[4 + u % SLOTS][:, 0:AW], oh[:, u % MRING, :], g[:, u % RING, :],
                   start=True, stop=True).then_inc(sem("product"), 1)

            pe.wait_ge(sem("lin_taken"), 2 * T)
            pe.sem_inc(sem("product"), U)
            pe.sem_inc(sem("summed"), SLOTS)
            pe.wait_ge(sem("g_ones"), 1)
            with pe.Fori(0, NT // U) as it:
                for u in range(U):
                    product(0, it, u)
            pe.wait_ge(sem("rwT_taken"), 1)
            transposes(1)
            pe.wait_ge(sem("tr_taken"), 2 * T)
            linear(2, xT, rwT, EX, rowb[0:1, 0:EX])
            bin_counts(EX, 1)
            pe.sem_inc(sem("f_h_done"), 2)
            pe.sem_inc(sem("f_o_done"), 2)
            pe.wait_ge(sem("lin_taken"), 3 * T)
            def f_transpose(s, loaded):
                pe.wait_ge(sem(f"f_loaded{s}"), loaded)
                for k in range(KD):
                    last = tr(banks[s % 2][:, k * P:(k + 1) * P], f_x[:, s, k * P:(k + 1) * P], ident[:, :])
                last.then_inc(sem("f_xt_done"), 1)

            def f_hidden(n, s):
                pe.wait_ge(sem("f_xt_taken"), n + 1)
                pe.wait_ge(sem("f_selected"), n + 1)
                o = banks[2 + s % 2][0:H0, 0:P]
                mm(o, f_b1, f_sel[:, s % 4, :], start=True, stop=False)
                for k in range(KD):
                    last = mm(o, f_w1[:, s % 4, k, :], f_xT[:, s % 2, k, :], start=False, stop=k == KD - 1)
                last.then_inc(sem("f_h_done"), 1)

            def f_out(n, s):
                pe.wait_ge(sem("f_h_taken"), n + 1)
                pe.wait_ge(sem("f_y_ready"), n + 1)
                o = banks[4 + s % 2][:, 0:D]
                mm(o, f_sel[:, s % 4, :], f_b2, start=True, stop=False)
                mm(o, f_h[:, s % 2, :], f_w2[:, s, :], start=False, stop=True).then_inc(sem("f_o_done"), 1)

            pe.wait_ge(sem("f_parts"), 1)
            f_transpose(0, 48)
            f_transpose(1, 48)
            f_hidden(0, 0)
            with pe.Fori(0, FT // 8 - 1) as it:
                for s in range(8):
                    f_transpose((s + 2) % 4, it * 96 + 48 * ((s + 2) // 4 + 1))
                    f_hidden(it * 8 + (s + 1), (s + 1) % 8)
                    f_out(it * 8 + s, s)
            for n in range(FT - 8, FT):
                if n + 2 < FT:
                    f_transpose((n + 2) % 4, 48 * ((n + 2) // 4 + 1))
                if n + 1 < FT:
                    f_hidden(n + 1, (n + 1) % 8)
                f_out(n, n % 8)
            pe.wait_ge(sem("w_gnn1"), 10 * 16)
            for w, W in enumerate((Wio[:, 0], Wqkv[:, :, 2 * D:3 * D])):
                if w == 1:
                    pe.wait_ge(sem("w_mix1"), 5 * 16)
                    pe.wait_ge(sem("WT_taken"), KD)
                for k in range(KD):
                    for j in range(KD):
                        last = tr(banks[k][:, j * P:(j + 1) * P], W[:, j, k * P:(k + 1) * P], ident[:, :])
                last.then_inc(sem("WT_done"), 1)
            pe.wait_ge(sem("WT_taken"), 2 * KD)
            for w, (W, n) in enumerate(((Was[:, 0], 2 * D), (Wo1, D))):
                for j in range(KD):
                    for k in range(KD):
                        last = mm(banks[2 + 2 * w + j][:, 0:n], WT[:, w, k, j * P:(j + 1) * P], W[:, k, 0:n],
                                  start=k == 0, stop=k == KD - 1)
                last.then_inc(sem("fold_done"), 1)
            pe.wait_ge(sem("b_in_ready"), KD)
            for k in range(KD):
                last = mm(banks[6][:, :], b_in[:, k, :], Was[:, 0, k, :], start=k == 0, stop=k == KD - 1)
            last.then_inc(sem("fold_done"), 1)
            mm(banks[7][0:1, 0:D], ones[0:1, 0:1], rowb[0:1, 768:1024], start=True, stop=False)
            mm(banks[7][0:1, 0:D], ones[0:1, 0:1], rowb[0:1, 1024:1280], start=False, stop=False)
            for k in range(KD):
                last = mm(banks[7][0:1, 0:D], colb[:, 10 + k:11 + k], Wo1[:, k, :], start=False, stop=k == KD - 1)
            last.then_inc(sem("fold_done"), 1)
            pe.wait_ge(sem("fold_taken"), 2 * KD + 1)
            pe.wait_ge(sem("bhid_used"), 1)
            transposes_and_linear(2, 3, xT, Was[:, 0], D)

            def beside(l, k, u, n):
                if l == 0 and u == 0:
                    pe.wait_ge(sem("m_x"), k + 1)
                    mm(banks[2][:, :], ones[0:1, :], rowb[0:1, D:3 * D], start=True, stop=False)
                    for c in range(KD):
                        last = mm(banks[2][:, :], s_x[:, c, :], Wqkv[:, c, D:3 * D], start=False, stop=c == KD - 1)
                    last.then_inc(sem("m_proj"), 1)
                if l == 0 and u == 2:
                    pe.wait_ge(sem("self_taken"), k + 1)
                    for c in range(KD):
                        last = mm(banks[3][:, 0:D], s_x[:, c, :], Wvo[:, c, :], start=c == 0, stop=c == KD - 1)
                    last.then_inc(sem("m_out"), 1)
                    for c in range(KD):
                        last = mm(banks[3][:, D:2 * D], s_x[:, c, :], Wself[:, 0, c, :], start=c == 0, stop=c == KD - 1)
                    last.then_inc(sem("self_done"), 1)
                if l == 0 and u == 12:
                    pe.wait_ge(sem("m_k4"), k + 1)
                    for c in range(KD):
                        mm(banks[c][:, 0:D], s_k2[0:n, c * P:(c + 1) * P], s_v[0:n, :], start=False, stop=False)
                        last = mm(banks[c][:, D:AW], s_k4[0:n, c * P:(c + 1) * P], ones[0:n, 0:1],
                                  start=False, stop=False)
                    last.then_inc(sem("m_kv_done"), 1)
                if l == 1 and u == 0:
                    pe.wait_ge(sem("n_x"), k + 1)
                    mm(banks[2][:, 0:D], ones[0:1, :], rowb[0:1, 0:D], start=True, stop=False)
                    for c in range(KD):
                        last = mm(banks[2][:, 0:D], s_x[:, c, :], Wqkv[:, c, 0:D], start=False, stop=c == KD - 1)
                    last.then_inc(sem("n_proj"), 1)
                if l >= 1 and u == 2:
                    pe.wait_ge(sem("self_x"), k + ((l - 1) * T + 1))
                    for c in range(KD):
                        last = mm(banks[3][:, D:2 * D], s_h[:, c, :], Wself[:, l, c, :], start=c == 0, stop=c == KD - 1)
                    last.then_inc(sem("self_done"), 1)
                if l == 1 and u == 6:
                    pe.wait_ge(sem("n_square"), k + 1)
                    for c in range(KD):
                        last = tr(banks[0][:, c * P:(c + 1) * P], s_q2[:, c * P:(c + 1) * P], ident[:, :])
                    last.then_inc(sem("n_qT"), 1)
                if l == 1 and u == 9:
                    pe.wait_ge(sem("n_qT_taken"), k + 1)
                    pe.wait_ge(sem("n_mixed_taken"), k + 1)
                    for c in range(KD):
                        last = mm(banks[1][:, 0:D], s_q2T[:, c, :], kv[:, c, :], start=c == 0, stop=c == KD - 1)
                    last.then_inc(sem("n_mixed"), 1)

            def layer_products(l):
                pe.wait_ge(sem("g_ones"), l + 2)
                last = NT // U - 1
                with pe.Fori(0, last) as it:
                    for u in range(U):
                        beside(l, it * 2 + u // 16, u % 16, P)
                        product(l + 1, it, u)
                for u in range(U):
                    if u < 16:
                        beside(l, last * 2, u, TAIL)
                    product(l + 1, last, u)

            pe.wait_ge(sem("zero_row"), 1)
            pe.wait_ge(sem("tr_taken"), 3 * T)
            for c in range(KD):
                mm(banks[c][:, 0:AW], ones[64:65, :], zero_row, start=True, stop=False)
            pe.sem_inc(sem("m_kv_done"), 1)
            pe.sem_inc(sem("n_scale"), 1)
            pe.sem_inc(sem("n_mixed"), 1)
            pe.sem_inc(sem("n_mixed_taken"), 1)
            pe.wait_ge(sem("lin_taken"), 4 * T)
            for l in range(3):
                if l == 1:
                    pe.wait_ge(sem("kv_scaled"), KD)
                    for j in range(KD):
                        for k in range(KD):
                            last = tr(banks[j][:, k * P:(k + 1) * P], kvs[:, k, j * P:(j + 1) * P], ident[:, :])
                    last.then_inc(sem("kvT_done"), 1)
                    pe.wait_ge(sem("kvT_taken"), KD)
                    for c in range(KD):
                        for j in range(KD):
                            last = mm(banks[2 + c][:, 0:D], kvT[:, j, c * P:(c + 1) * P], Wo1[:, j, :],
                                      start=j == 0, stop=j == KD - 1)
                    last.then_inc(sem("m2_done"), 1)
                    pe.wait_ge(sem("m2_taken"), KD)
                layer_products(l)
                if l == 0:
                    for c in range(KD):
                        last = mm(banks[c][:, 0:AW], ones[64:65, :], zero_row, start=False, stop=True)
                    last.then_inc(sem("kv_closed"), 1)
                    pe.wait_ge(sem("kv_saved"), 2 * KD)
                if l < 2:
                    transposes_and_linear(3 + l, 4 + l, hT, Was[:, l + 1], D)
                    pe.wait_ge(sem("lin_taken"), (5 + l) * T)
                else:
                    transposes_and_linear(5, 6, hT, Wio[:, 1], D, rowb[0:1, 768:1024])
            transposes(6)
            pe.wait_ge(sem("mean_ready"), 1)
            pe.wait_ge(sem("wr_loaded"), 32)
            for k in range(KD):
                last = mm(banks[7][0:1, 0:EX1], ksum[:, k:k + 1], top[:, 64 + 8 * k:72 + 8 * k], start=k == 0, stop=k == KD - 1)
            last.then_inc(sem("route_done"), 1)
            pe.wait_ge(sem("gates_ready"), 1)
            mm(banks[7][:, 16:18], ones[0:1, :], top[0:1, 52:54], start=True, stop=True).then_inc(sem("gates_spread"), 1)
            pe.wait_ge(sem("w_ffn1"), 160)
            pe.wait_ge(sem("lin_taken"), 7 * T)
            i = 0
            for c in range(9):
                n = 384 if c < 8 else P
                for j in range(J1):
                    if i >= 4:
                        pe.wait_ge(sem("h1_taken"), i - 3)
                    for k in range(KD):
                        last = mm(banks[i % 4][:, 0:n], W1c[:, j * 2 // J1, k, (j % (J1 // 2)) * P:(j % (J1 // 2) + 1) * P],
                                  xT[:, k, c * 384:c * 384 + n], start=k == 0, stop=k == KD - 1)
                    last.then_inc(sem("h1_done"), 1)
                    i += 1
                pe.wait_ge(sem("h1_taken"), i)
                pe.wait_ge(sem("w2_scaled"), J1)
                for s in range(n // P):
                    t = 3 * c + s
                    if t >= 2:
                        pe.wait_ge(sem("y1_taken"), t - 1)
                    o = banks[4 + t % 2][:, 0:D]
                    mm(o, ones[0:1, :], rowb[0:1, 0:D], start=True, stop=False)
                    for j in range(J1):
                        last = mm(o, gel[:, c % 2, j, s * P:(s + 1) * P], W2c[:, j, :], start=False, stop=j == J1 - 1)
                    last.then_inc(sem("y1_done"), 1)


_INS = ['x', 'src', 'dst', 'edge_weight', 'L0_gnn_weight', 'L0_mix_W_qk', 'L0_mix_b_qk', 'L0_mix_W_v', 'L0_mix_b_v',
        'L0_mix_gamma', 'L0_mix_beta', 'L0_ffn_router_w', 'L0_ffn_router_b', 'L0_ffn_W1', 'L0_ffn_b1', 'L0_ffn_W2',
        'L0_ffn_b2', 'L1_gnn_W_in', 'L1_gnn_b_in', 'L1_gnn_W_agg', 'L1_gnn_W_self', 'L1_gnn_b_hid', 'L1_gnn_W_out',
        'L1_gnn_b_out', 'L1_mix_W_qkv', 'L1_mix_b_qkv', 'L1_mix_W_out', 'L1_mix_b_out', 'L1_ffn_Wr', 'L1_ffn_br',
        'L1_ffn_W1', 'L1_ffn_b1', 'L1_ffn_W2', 'L1_ffn_b2', 'L1_ffn_gamma', 'L1_ffn_beta']


def kernel(**inputs):
    import numpy as _np
    import concourse.bacc as _bacc
    from concourse import mybir as _mybir
    from concourse.bass_utils import run_bass_kernel_spmd as _run

    nc = _bacc.Bacc("TRN2", target_bir_lowering=False, num_devices=1)
    arrays, args = {}, []
    for name in _INS:
        a = _np.ascontiguousarray(inputs[name])
        arrays[f"in_{name}"] = a
        args.append(nc.dram_tensor(f"in_{name}", a.shape, _mybir.dt.from_np(a.dtype), kind="ExternalInput").ap())
    args.append(nc.dram_tensor("out_0", (N, D), F32, kind="ExternalOutput").ap())
    gps_kernel(nc, *args)
    r = _run(nc, [arrays], core_ids=[0])
    return r.results[0]["out_0"]
```

```python
from contextlib import ExitStack

import concourse.bass as bass
from concourse import mybir

F32 = mybir.dt.float32
BF16 = mybir.dt.bfloat16
I32 = mybir.dt.int32
U32 = mybir.dt.uint32
ALU = mybir.AluOpType
ACT = mybir.ActivationFunctionType
AX = mybir.AxisListType.X

P = 128
N, D, E = 3125, 256, 50000
KD = D // P
T = -(-N // P)
TAIL = N - (T - 1) * P
NP = T * P
EC = -(-E // P)
EREST = E - (EC - 1) * P
U = 32
SU = U // 2
NT = -(-((E + T * (P - 1)) // P) // U) * U
RING = 16
MRING = 8
SLOTS = 4
AHEAD = 4
AW = D + 1
EX, H0 = 32, 64
FT = -(-((N + EX * (P - 1)) // P) // 8) * 8
EX1, H1 = 8, 512
J1 = 2 * H1 // P
EPS = 1e-5
CAPACITY = float(-(-N * 5 // (4 * EX1)))
CH = [(c * 512, min(512, N - c * 512)) for c in range(-(-N // 512))]
CHP = [(c * 512, min(512, NP - c * 512)) for c in range(-(-NP // 512))]
TG = [(0, 8), (8, 8), (16, 6), (22, 3)]


def gps_kernel(nc, x, src, dst, edge_weight, gnn0_W, mix0_Wqk, mix0_bqk, mix0_Wv, mix0_bv, mix0_gamma,
               mix0_beta, ffn0_rw, ffn0_rb, ffn0_W1, ffn0_b1, ffn0_W2, ffn0_b2, gnn1_Win, gnn1_bin,
               gnn1_Wagg, gnn1_Wself, gnn1_bhid, gnn1_Wout, gnn1_bout, mix1_Wqkv, mix1_bqkv, mix1_Wout,
               mix1_bout, ffn1_Wr, ffn1_br, ffn1_W1, ffn1_b1, ffn1_W2, ffn1_b2, ffn1_gamma, ffn1_beta, out):
    records_d = nc.dram_tensor("records_d", [P, NT, 3], F32).ap()
    rows_d = nc.dram_tensor("rows_d", [NP, D], F32).ap()
    xs_d = nc.dram_tensor("xs_d", [FT * P, D], F32).ap()
    ys_d = nc.dram_tensor("ys_d", [FT * P, D], F32).ap()

    with ExitStack() as ctx:
        def sb(name, shape, dt=F32):
            return ctx.enter_context(nc.sbuf_tensor(name, shape, dt))

        sems = {}

        def sem(name):
            if name not in sems:
                sems[name] = ctx.enter_context(nc.semaphore(name))
            return sems[name]

        x_sb = sb("x_sb", [P, T, D])
        rows = sb("rows", [P, T, D])
        xT = sb("xT", [P, KD, NP])
        hT = sb("hT", [P, KD, NP])
        vals = sb("vals", [P, T, D])
        accF = sb("accF", [P, (T + 1) * AW])
        acc = accF[:, :].rearrange("p (t w) -> p t w", w=AW)
        recs = sb("recs", [P, NT + AHEAD, 3])
        wA = sb("wA", [P, 4096])
        wB = sb("wB", [P, 2048])
        gF = sb("gF", [P, 2056])
        g = rows[:, :, :].rearrange("p t d -> p (t d)")[:, 0:RING * AW].rearrange("p (s w) -> p s w", w=AW)
        oh = sb("oh", [P, MRING, P])
        xt = sb("xt", [P, 2, KD, P])
        idx = sb("idx", [P, U], I32)
        srt = sb("srt", [P, U, 3])
        misc = sb("misc", [P, 1280])
        rowb = misc[0:1, :]
        bins = misc[32:33, 0:NT].bitcast(I32)
        iotaT = misc[32:33, NT:2 * NT]
        zero_row = misc[64:65, 0:AW]
        ident = sb("ident", [P, P])
        tri = sb("tri", [P, P])
        ones = sb("ones", [P, P])
        iota = sb("iota", [P, P])
        rowok = sb("rowok", [P, 1])
        rowid = sb("rowid", [P, 1])
        small = sb("small", [P, 768])
        stats = sb("stats", [P, T, 6])
        mv = sb("mv", [P, T, 2])
        ln = sb("ln", [P, 4, T])
        bcast = sb("bcast", [P, D])
        banks = [ctx.enter_context(nc.psum_tensor(f"bank{i}", [P, 512], F32)) for i in range(8)]

        def cols(a, n):
            return small[:, a:a + n]
        rowtot, cnt, endt, off = (cols(32 * i, 32) for i in range(4))
        colb = cols(192, 16)
        invdeg = cols(208, T)
        kmax, ksum, kinv = cols(240, 2), cols(242, 2), cols(244, 2)
        bnst, bnmv, bnt = cols(248, 12), cols(260, 4), cols(264, 8)
        posI = cols(424, 32).bitcast(I32)
        kn = cols(272, 6)
        rbias = cols(280, EX)
        top = cols(528, 96)
        cntI = cols(640, 32).bitcast(I32)
        eidx = cols(672, 64).bitcast(I32)

        block = ctx.enter_context(nc.Block())

        EP = EC + 1
        ohs = accF[:, 0:T * EP // 2].bitcast(BF16).rearrange("p (q b j) -> p q b j", q=4, b=T)
        o = T * EP // 2
        srcI, dstI, wE, tmpI = (accF[:, o + EC * i:o + EC * (i + 1)] for i in range(4))
        srcI, dstI, tmpI = srcI.bitcast(I32), dstI.bitcast(I32), tmpI.bitcast(I32)
        EQ = EP // 4
        binF = gF[:, 0:EP]
        EE = -(-EC // SU) * SU
        posF, posI0, addr = gF[:, EP:2 * EP], gF[:, 2 * EP:3 * EP], gF[:, 3 * EP:3 * EP + EE]
        lowI = gF[:, 3 * EP + EE:3 * EP + EE + EQ].bitcast(I32)
        posI0 = posI0.bitcast(I32)
        e_scan, e_prod = (hT[:, k, 0:T * EQ].rearrange("p (b j) -> p b j", j=EQ) for k in range(2))
        e_mask = xT[:, 0, 0:T * EQ].rearrange("p (b j) -> p b j", j=EQ)
        edge = wB[:, 0:3 * EE].rearrange("p (j c) -> p j c", c=3)

        W0V = wA[:, 0:1024].rearrange("p (k n) -> p k n", k=KD)
        Wk = wA[:, 1024:1536].rearrange("p (k n) -> p k n", k=KD)
        Wq = wA[:, 1536:2048].rearrange("p (k n) -> p k n", k=KD)
        WqT = wA[:, 2048:2560].rearrange("p (k n) -> p k n", k=KD)
        bn = wA[:, 2560:3072].rearrange("p (k n) -> p k n", k=KD)
        Mx = wA[:, 3072:3584].rearrange("p (k n) -> p k n", k=KD)
        rw = wA[0:EX, 3584:3840]
        rwT = wA[:, 3840:3904].rearrange("p (k n) -> p k n", k=KD)
        f_x = accF[:, 0:1024].rearrange("p (s n) -> p s n", s=4)
        f_w1 = accF[:, 1024:1536].rearrange("p (s k n) -> p s k n", s=4, k=KD)
        f_w2 = accF[0:H0, 4356:6404].rearrange("p (s n) -> p s n", s=8)
        f_sel = accF[0:3 * EX, 2560:2816].bitcast(BF16).rearrange("p (s n) -> p s n", s=4)
        f_row, f_exp = accF[0:3 * EX, 2816:2944], top[0:3 * EX, 0:FT]
        f_b, f_rest = accF[0:3 * EX, 2944:2944 + D + H0], accF[0:3 * EX, 3264:3264 + D + H0]
        f_parts = accF[0:3 * EX, 6404:6404 + (D + H0) // 2].bitcast(BF16)
        f_b2, f_b1 = f_parts[:, 0:D], f_parts[:, D:D + H0]
        f_xT = accF[:, 3588:4100].rearrange("p (s k n) -> p s k n", s=2, k=KD)
        f_h = accF[0:H0, 4100:4356].rearrange("p (s n) -> p s n", s=2)
        f_y = accF[:, 1536:2560].rearrange("p (s n) -> p s n", s=4)
        r_oh = wB[:, 0:EX * T].rearrange("p (b t) -> p b t", t=T)
        r_sc = wB[:, 800:1600].rearrange("p (b t) -> p b t", t=T)
        r_lg = oh[:, 0:7, :].rearrange("p a b -> p (a b)")[:, 0:T * EX].rearrange("p (t b) -> p t b", b=EX)
        r_m8 = gF[:, 0:8 * T].rearrange("p (t e) -> p t e", e=8)
        r_i8 = gF[:, 8 * T:16 * T].bitcast(U32).rearrange("p (t e) -> p t e", e=8)
        r_msk = gF[:, 16 * T:16 * T + EX * T].rearrange("p (b t) -> p b t", t=T)
        r_eid = gF[:, 1400:1400 + T]
        Wio = wA[:, 0:1024].rearrange("p (w k n) -> p w k n", w=2, k=KD)
        Was = wA[:, 1024:4096].rearrange("p (l k n) -> p l k n", l=3, k=KD)
        Wself = Was[:, :, :, D:2 * D]
        Wqkv = wB[:, 0:1536].rearrange("p (k n) -> p k n", k=KD)
        Wo1 = wB[:, 1536:2048].rearrange("p (k n) -> p k n", k=KD)
        WT = oh[:, :, :].rearrange("p a b -> p (a b)").rearrange("p (w k n) -> p w k n", w=2, k=KD)
        Wvo = xt[:, :, :, :].rearrange("p a k n -> p a (k n)")
        b_in = gF[:, 0:D].rearrange("p (k n) -> p k n", k=KD)
        gbias = hT[:, 0, 0:D]
        s_x, s_h = (gF[:, i * D:(i + 1) * D].rearrange("p (k n) -> p k n", k=KD) for i in range(2))
        s_v, s_k2, s_k4, s_q2, s_junk = (gF[:, i * D:(i + 1) * D] for i in range(2, 7))
        s_q2T = gF[:, 7 * D:8 * D].rearrange("p (k n) -> p k n", k=KD)
        kv = Wio[:, 0]
        kvs, kvT = (gF[:, i * 2 * D:(i + 1) * 2 * D].rearrange("p (k n) -> p k n", k=KD) for i in (0, 1))
        m1 = cols(506, 16)
        W1c = wA[:, 0:2 * KD * H1].rearrange("p (e k n) -> p e k n", e=2, k=KD)
        W2c = wA[:, 2048:4096].rearrange("p (j n) -> p j n", n=D)
        gel = hT[:, :, :].rearrange("p k n -> p (k n)")[:, 0:2 * J1 * 384].rearrange("p (s j n) -> p s j n", s=2, j=J1)

        def pt(ap):
            return ap.rearrange("(t p) d -> p t d", p=P)

        def kp(ap):
            return ap.rearrange("(k p) n -> p k n", p=P)

        def row(ap):
            return ap.rearrange("(a n) -> a n", a=1)

        def tw(t):
            return P if t < T - 1 else TAIL

        @block.sync
        def _(sp):
            ld = sem("edges_loaded")
            sp.wait_ge(sem("edge_pad_set"), 3)
            for tile, a in ((srcI, src), (dstI, dst), (wE, edge_weight)):
                sp.dma_start(tile[:, 0:EC - 1], a[0:(EC - 1) * P].rearrange("(p j) -> p j", p=P)).then_inc(ld, 16)
                sp.dma_start(tile[0:EREST, EC - 1:EC],
                             a[(EC - 1) * P:E].rearrange("(p j) -> p j", j=1)).then_inc(ld, 16)
            sp.wait_ge(sem("x_pad_set"), 1)
            sp.dma_start(x_sb[:, 0:T - 1, :], pt(x[0:(T - 1) * P, :])).then_inc(sem("x_loaded"), 16)
            sp.dma_start(x_sb[0:TAIL, T - 1, :], x[(T - 1) * P:N, :]).then_inc(sem("x_loaded"), 16)
            w = sem("w_block0")
            sp.dma_start(W0V[:, :, 0:D], kp(gnn0_W)).then_inc(w, 16)
            sp.dma_start(W0V[:, :, D:2 * D], kp(mix0_Wv)).then_inc(w, 16)
            sp.dma_start(Wk, kp(mix0_Wqk[1])).then_inc(w, 16)
            sp.dma_start(Wq, kp(mix0_Wqk[0])).then_inc(w, 16)
            sp.dma_start(colb[:, 0:2], mix0_bqk[1].rearrange("(k p) -> p k", p=P), allow_slow_non_contiguous=True).then_inc(w, 16)
            sp.dma_start(colb[:, 2:4], mix0_bqk[0].rearrange("(k p) -> p k", p=P), allow_slow_non_contiguous=True).then_inc(w, 16)
            sp.dma_start(colb[:, 4:6], mix0_gamma.rearrange("(k p) -> p k", p=P), allow_slow_non_contiguous=True).then_inc(w, 16)
            sp.dma_start(colb[:, 6:8], mix0_beta.rearrange("(k p) -> p k", p=P), allow_slow_non_contiguous=True).then_inc(w, 16)
            sp.dma_start(bcast[:, :], row(mix0_bv).to_broadcast([P, D])).then_inc(w, 16)
            sp.dma_start(rw, ffn0_rw).then_inc(w, 16)
            sp.dma_start(rbias, row(ffn0_rb).to_broadcast([P, EX])).then_inc(w, 16)
            for a, n in TG:
                sp.wait_ge(sem("rows_ready"), a + n)
                sp.dma_start(pt(rows_d)[:, a:a + n, :], rows[:, a:a + n, :]).then_inc(sem("rows_stored"), 16)
            sp.wait_ge(sem("sort_part0"), 16 * (SU * (EC // U) + EC % U))
            sp.wait_ge(sem("sort_part1"), 16 + 16 * SU * (EC // U))
            sp.dma_start(recs[:, 0:NT, :], records_d).then_inc(sem("recs_loaded"), 16)
            sp.wait_ge(sem("acc_zero"), 1)
            xs_flat = xs_d.rearrange("(p a) d -> p (a d)", p=P)
            q = FT * D // 4
            for i in range(4):
                sp.dma_start(xs_flat[:, i * q:(i + 1) * q], accF[:, 0:q]).then_inc(sem("zeros_stored"), 16)
            sp.wait_ge(sem("expert_table"), 1)
            for i in range(3):
                sp.dma_start(f_b[EX * i:EX * (i + 1), 0:D], ffn0_b2).then_inc(sem("f_biases"), 16)
                sp.dma_start(f_b[EX * i:EX * (i + 1), D:D + H0], ffn0_b1).then_inc(sem("f_biases"), 16)

            def load_tile(n, s):
                e = sp.value_load(eidx[32:33, bass.ds(n, 1)], min_val=0, max_val=EX - 1)
                f = sem(f"f_loaded{s % 4}")
                sp.dma_start(f_w1[:, s % 4], ffn0_W1[bass.ds(e, 1)].rearrange("a (k p) n -> p (a k) n", p=P)).then_inc(f, 16)
                sp.dma_start(f_w2[:, s, :], ffn0_W2[bass.ds(e, 1)].rearrange("a p n -> (a p) n")).then_inc(f, 16)

            for s in range(4):
                load_tile(s, s)
            with sp.Fori(0, FT // 8 - 1) as it:
                for s in range(4, 12):
                    sp.wait_ge(sem("f_h_done"), it * 8 + (s - 1))
                    load_tile(it * 8 + s, s % 8)
            for n in range(FT - 4, FT):
                sp.wait_ge(sem("f_h_done"), n - 1)
                load_tile(n, n % 8)
            w = sem("w_mix1")
            sp.wait_ge(sem("expert_table"), 1)
            sp.dma_start(Wqkv, kp(mix1_Wqkv)).then_inc(w, 16)
            sp.dma_start(Wo1, kp(mix1_Wout)).then_inc(w, 16)
            sp.dma_start(rowb[0:1, 0:768], row(mix1_bqkv)).then_inc(w, 16)
            sp.dma_start(rowb[0:1, 768:1024], row(gnn1_bout)).then_inc(w, 16)
            sp.dma_start(rowb[0:1, 1024:1280], row(mix1_bout)).then_inc(w, 16)
            for l in range(3):
                if l > 0:
                    sp.wait_ge(sem("self_taken"), l * T + 1)
                    sp.wait_ge(sem("agg_gathered"), l + 1)
                else:
                    sp.wait_ge(sem("v_bias_used"), 1)
                sp.dma_start(bcast[:, :], row(gnn1_bhid[l]).to_broadcast([P, D])).then_inc(sem("bhid_loaded"), 16)
                for a, n in TG:
                    sp.wait_ge(sem("rows_ready"), (l + 1) * T + a + n)
                    sp.dma_start(pt(rows_d)[:, a:a + n, :], rows[:, a:a + n, :]).then_inc(sem("rows_stored"), 16)
            sp.wait_ge(sem("lin_taken"), 7 * T)
            sp.dma_start(top[:, 64:80].rearrange("p (k e) -> p k e", e=EX1), kp(ffn1_Wr)).then_inc(sem("wr_loaded"), 16)
            sp.dma_start(rowb[0:1, 512:520], row(ffn1_br)).then_inc(sem("wr_loaded"), 16)
            sp.wait_ge(sem("experts_chosen"), 1)
            chosen = [sp.value_load(eidx[0:1, k:k + 1], min_val=0, max_val=EX1 - 1) for k in range(2)]
            w = sem("w_ffn1_in")
            for k, e in enumerate(chosen):
                sp.dma_start(W1c[:, k], ffn1_W1[bass.ds(e, 1)].rearrange("a (k p) n -> p (a k) n", p=P)).then_inc(w, 16)
                sp.dma_start(colb[:, k * J1 // 2:(k + 1) * J1 // 2],
                             ffn1_b1[bass.ds(e, 1)].rearrange("a (j p) -> p (a j)", p=P),
                             allow_slow_non_contiguous=True).then_inc(w, 16)
            w = sem("w_ffn1_out")
            for k, e in enumerate(chosen):
                sp.dma_start(W2c[:, k * J1 // 2:(k + 1) * J1 // 2, :],
                             ffn1_W2[bass.ds(e, 1)].rearrange("a (j p) n -> p (a j) n", p=P)).then_inc(w, 16)
                sp.dma_start(rowb[0:1, k * D:(k + 1) * D], ffn1_b2[bass.ds(e, 1)]).then_inc(w, 16)
            sp.dma_start(bcast[:, :], row(ffn1_gamma).to_broadcast([P, D])).then_inc(w, 16)
            sp.dma_start(wB[:, 0:D], row(ffn1_beta).to_broadcast([P, D])).then_inc(w, 16)
            for c in range(9):
                sp.wait_ge(sem("out_ready"), c + 1)
                a, n = 3 * c, 3 if c < 8 else 0
                if n:
                    sp.dma_start(pt(out[a * P:(a + n) * P, :]), vals[:, a:a + n, :]).then_inc(sem("out_stored"), 16)
                else:
                    sp.dma_start(out[a * P:N, :], vals[0:TAIL, a, :]).then_inc(sem("out_stored"), 16)
            sp.wait_ge(sem("out_stored"), 16 * 9)
            sp.wait_ge(sem("rows_stored"), 16 * 4 * len(TG))

        @block.gpsimd
        def _(pool):
            c = sem("consts")
            nc.gpsimd.iota(iota[:, :], pattern=[[1, P]], base=0, channel_multiplier=0,
                           allow_small_or_imprecise_dtypes=True).then_inc(c, 1)
            pool.wait_ge(c, 1)
            nc.gpsimd.iota(iotaT, pattern=[[1, NT]], base=0, channel_multiplier=0,
                           allow_small_or_imprecise_dtypes=True).then_inc(c, 1)
            pool.wait_ge(c, 2)
            nc.gpsimd.iota(rowid[:, :], pattern=[[0, 1]], base=0, channel_multiplier=1,
                           allow_small_or_imprecise_dtypes=True).then_inc(c, 1)
            nc.gpsimd.memset(ones[:, :], 1.0).then_inc(c, 1)
            nc.gpsimd.memset(ident[:, :], 0.0).then_inc(c, 1)
            pool.wait_ge(c, 5)
            nc.gpsimd.affine_select(out=ident[:, :], in_=ident[:, :], compare_op=ALU.not_equal, fill=1.0, base=0,
                                    pattern=[[-1, P]], channel_multiplier=1).then_inc(c, 1)
            nc.gpsimd.affine_select(out=tri[:, :], in_=ones[:, :], compare_op=ALU.is_gt, fill=0.0, base=0,
                                    pattern=[[1, P]], channel_multiplier=-1).then_inc(c, 1)
            nc.gpsimd.tensor_scalar(rowok[:, :], rowid[:, :], float(TAIL), None, ALU.is_lt).then_inc(c, 1)

            copied = sem("sort_copied")

            def fill(h, j):
                part = slice(SU * h, SU * (h + 1))
                nc.gpsimd.tensor_copy(idx[:, part], addr[:, bass.ds(j, SU)]).then_inc(copied, 1)
                nc.gpsimd.tensor_copy(srt[:, part, :], edge[:, bass.ds(j, SU), :]).then_inc(copied, 1)

            def scatter(u, rows_n, part):
                pool.indirect_dma_start(records_d.rearrange("p t c -> (p t) c"),
                                        bass.IndirectOffsetOnAxis(ap=idx[0:rows_n, u:u + 1], axis=0),
                                        srt[0:rows_n, u, :], None).then_inc(sem(f"sort_part{part}"), 16)

            pool.wait_ge(sem("recs_empty"), 1)
            pool.dma_start(records_d, recs[:, 0:NT, :]).then_inc(sem("sort_part1"), 16)
            pool.wait_ge(sem("sort_part1"), 16)
            pool.wait_ge(sem("edge_slots"), 1)
            fill(0, 0)
            with pool.Fori(0, EC // U) as it:
                for h in range(2):
                    pool.wait_ge(copied, it * 4 + (2 * h + 2))
                    pool.sem_inc(sem("turn"))
                    for u in range(SU * h, SU * (h + 1)):
                        if u == SU * h + 10:
                            if h == 1:
                                pool.wait_ge(sem("edge_slots"), it + 2)
                            pool.wait_ge(sem(f"sort_part{1 - h}"), it * (16 * SU) + (16 if h == 0 else 16 * SU))
                            fill(1 - h, it * U + SU * (h + 1))
                        scatter(u, P, h)
            pool.wait_ge(copied, 4 * (EC // U) + 2)
            for u in range(EC % U):
                scatter(u, P if u < EC % U - 1 else EREST, 0)

            def gathers(a):
                pool.wait_ge(sem("rows_stored"), 16 * len(TG) * (a + 1))
                with pool.Fori(0, NT // U) as it:
                    for q in range(U // 8):
                        pool.wait_ge(sem("gather_idx"), it * (U // 8) + (a * NT // 8 + q + 1))
                        for u in range(8 * q, 8 * q + 8):
                            if u % 4 == 0:
                                pool.wait_ge(sem("product"), it * U + (a * NT + u + 4 + U - RING))
                                pool.sem_inc(sem("turn"))
                            pool.indirect_dma_start(g[:, u % RING, 0:D], None, rows_d,
                                                    bass.IndirectOffsetOnAxis(ap=idx[:, u:u + 1], axis=0))\
                                .then_inc(sem(f"gathered{u % RING}"), 16)
                pool.wait_ge(sem("product"), U + (a + 1) * NT)
                pool.sem_inc(sem("agg_gathered"))

            gathers(0)
            pool.wait_ge(sem("zeros_stored"), 64)
            pool.wait_ge(sem("pos_ready"), 1)
            for t in range(T):
                pool.indirect_dma_start(xs_d, bass.IndirectOffsetOnAxis(ap=posI[0:tw(t), t:t + 1], axis=0),
                                        rows[0:tw(t), t, :], None).then_inc(sem("tokens_scattered"), 16)
            with pool.Fori(0, FT // 4) as it:
                for s in range(4):
                    pool.wait_ge(sem("f_y_ready"), it * 4 + (s + 3))
                    pool.sem_inc(sem("turn"))
                    pool.dma_start(ys_d[bass.ds((it * 4 + s) * P, P), :], f_y[:, s, :]).then_inc(sem(f"f_stored{s}"), 16)
            for s in range(4):
                pool.wait_ge(sem(f"f_stored{s}"), 16 * FT // 4)
            for t in range(T):
                if t >= RING:
                    pool.wait_ge(sem("x_added"), t - RING + 1)
                pool.indirect_dma_start(vals[0:tw(t), t, :], None, ys_d,
                                        bass.IndirectOffsetOnAxis(ap=posI[0:tw(t), t:t + 1], axis=0))\
                    .then_inc(sem(f"gathered{t % RING}"), 16)
            for a in range(1, 4):
                gathers(a)


        @block.scalar
        def _(act):
            step = [0]

            def link(ins):
                step[0] += 1
                ins.then_inc(sem("act_step"), 1)
                act.wait_ge(sem("act_step"), step[0])

            def sqrt_of(k):
                act.wait_ge(sem("var_ready"), k + 1)
                nc.scalar.sqrt(ln[:, 1, :], ln[:, 0, :]).then_inc(sem("sqrt_ready"), 1)

            def take_transposed(s, dest, relu=False, rows_stage=None):
                for t in range(T + 2):
                    if t < T:
                        act.wait_ge(sem("tr_done"), s * T + t + 1)
                        nc.scalar.activation(dest[:, :, t * P:(t + 1) * P],
                                             banks[t % 4][:, 0:2 * P].rearrange("p (k n) -> p k n", k=KD),
                                             ACT.Relu if relu else ACT.Copy).then_inc(sem("tr_taken"), 1)
                    if rows_stage is not None and t >= 2:
                        act.wait_ge(sem("lin_done"), rows_stage * T + t - 1)
                        nc.scalar.copy(rows[:, t - 2, :], banks[4 + t % 2][:, 0:D]).then_inc(sem("lin_taken"), 1)
                        act.wait_ge(sem("lin_taken"), rows_stage * T + t - 1)
                        act.sem_inc(sem("rows_ready"), 1)

            def take_linearT(first, chunks, dest, bias):
                for e in range(KD):
                    for c, (a, n) in enumerate(chunks):
                        i = e * len(chunks) + c
                        act.wait_ge(sem("lt_done"), first + i + 1)
                        nc.scalar.activation(dest[:, e, a:a + n], banks[2 + i % 2][:, 0:n], ACT.Identity,
                                             bias=bias[:, e:e + 1]).then_inc(sem("lt_taken"), 1)

            def indices(a, it, parts):
                for q in parts:
                    act.wait_ge(sem("product"), it * U + (a * NT + 8 * q + 8))
                    nc.scalar.copy(idx[:, 8 * (q % 4):8 * (q % 4) + 8], recs[:, bass.ds(it * U + 8 * q, 8), 0])\
                        .then_inc(sem("gather_idx"), 1)

            def link_loop(ins, name, k, n, i):
                ins.then_inc(sem(name), 1)
                act.wait_ge(sem(name), k * n + (i + 1))

            def mix_first(k):
                act.wait_ge(sem("m_kv_done"), k + 1)
                nc.scalar.copy(s_x, xT[:, :, bass.ds(k * P, P)]).then_inc(sem("m_x"), 1)
                act.wait_ge(sem("m_proj"), k + 1)
                link_loop(nc.scalar.activation(s_junk, banks[2][:, 0:D], ACT.Copy, accum_out=m1[:, 0:1]), "m_link", k, 3, 0)
                link_loop(nc.scalar.mul(m1[:, 1:2], m1[:, 0:1], -1.0 / D), "m_link", k, 3, 1)
                nc.scalar.activation(s_k2, banks[2][:, 0:D], ACT.Square, bias=m1[:, 1:2],
                                     accum_out=m1[:, 2:3]).then_inc(sem("m_square"), 1)
                nc.scalar.copy(s_v, banks[2][:, D:2 * D])
                act.wait_ge(sem("m_scale"), k + 1)
                link_loop(nc.scalar.mul(s_k2, s_k2, m1[:, 4:5]), "m_link", k, 3, 2)
                nc.scalar.square(s_k4, s_k2).then_inc(sem("m_k4"), 1)

            def mix_second(k):
                act.wait_ge(sem("n_mixed"), k + 1)
                act.wait_ge(sem("n_scale"), k + 1)
                nc.scalar.copy(s_x, xT[:, :, bass.ds(k * P, P)]).then_inc(sem("n_x"), 1)
                act.wait_ge(sem("n_proj"), k + 1)
                link_loop(nc.scalar.activation(s_junk, banks[2][:, 0:D], ACT.Copy, accum_out=m1[:, 0:1]), "n_alink", k, 3, 0)
                link_loop(nc.scalar.mul(m1[:, 1:2], m1[:, 0:1], -1.0 / D), "n_alink", k, 3, 1)
                nc.scalar.activation(s_q2, banks[2][:, 0:D], ACT.Square, bias=m1[:, 1:2],
                                     accum_out=m1[:, 2:3]).then_inc(sem("n_square"), 1)
                act.wait_ge(sem("n_square"), k + 1)
                link_loop(nc.scalar.activation(s_junk, s_q2, ACT.Square, accum_out=m1[:, 3:4]), "n_alink", k, 3, 2)
                nc.scalar.sqrt(m1[:, 5:6], m1[:, 3:4]).then_inc(sem("n_root"), 1)
                act.wait_ge(sem("n_qT"), k + 1)
                nc.scalar.copy(s_q2T, banks[0][:, 0:D].rearrange("p (k n) -> p k n", k=KD)).then_inc(sem("n_qT_taken"), 1)

            def self_rows(l, k):
                act.wait_ge(sem("self_taken"), k + (l * T + 1))
                nc.scalar.copy(s_h, hT[:, :, bass.ds(k * P, P)]).then_inc(sem("self_x"), 1)

            def beside(l, k):
                if l > 0:
                    self_rows(l, k)
                if l == 0:
                    mix_first(k)
                elif l == 1:
                    mix_second(k)

            def layer(l):
                last = NT // U - 1
                indices(l + 1, 0, (0, 1))
                with act.Fori(0, last) as it:
                    indices(l + 1, it, (2, 3))
                    beside(l, it * 2)
                    indices(l + 1, it, (4, 5))
                    beside(l, it * 2 + 1)
                indices(l + 1, last, (2, 3))
                beside(l, last * 2)

            sqrt_of(0)
            take_transposed(0, xT)
            take_linearT(0, CH, hT, colb[:, 0:2])
            act.wait_ge(sem("kmax_ready"), 1)
            for k in range(KD):
                nc.scalar.activation(hT[:, k, 0:N], hT[:, k, 0:N], ACT.Exp, bias=kmax[:, k:k + 1],
                                     accum_out=ksum[:, k:k + 1]).then_inc(sem("exp_ready"), 1)
            for t in range(T):
                act.wait_ge(sem("et_done"), t + 1)
                if t >= 2:
                    act.wait_ge(sem("lam_done"), t - 1)
                nc.scalar.copy(xt[0:tw(t), t % 2].rearrange("p k n -> p (k n)"), banks[t % 2][0:tw(t), 0:D])\
                    .then_inc(sem("et_taken"), 1)
            act.wait_ge(sem("bn_var"), 1)
            nc.scalar.sqrt(bnt[:, 2:4], bnt[:, 0:2]).then_inc(sem("bn_sqrt"), 1)
            for k in range(KD):
                act.wait_ge(sem("wqT_done"), k + 1)
                nc.scalar.copy(WqT[:, k, :], banks[k][:, 0:D]).then_inc(sem("wqT_taken"), 1)
            act.wait_ge(sem("mx_done"), KD + 1)
            for k in range(KD):
                nc.scalar.copy(Mx[:, k, :], banks[2 + k][:, 0:D]).then_inc(sem("mx_taken"), 1)
            nc.scalar.copy(rowb[0:1, 256:512], banks[6][0:1, 0:D]).then_inc(sem("mx_taken"), 1)
            act.wait_ge(sem("rwT_done"), 1)
            nc.scalar.copy(rwT, banks[0][:, 0:2 * EX].rearrange("p (k n) -> p k n", k=KD)).then_inc(sem("rwT_taken"), 1)
            act.wait_ge(sem("recs_loaded"), 16)
            with act.Fori(0, NT // U) as it:
                indices(0, it, range(U // 8))
            sqrt_of(1)
            take_transposed(1, xT)
            act.wait_ge(sem("lin_taken"), 3 * T)
            w = sem("w_gnn1")
            act.dma_start(Wio[:, 0], kp(gnn1_Win)).then_inc(w, 16)
            act.dma_start(Wio[:, 1], kp(gnn1_Wout)).then_inc(w, 16)
            for l in range(3):
                act.dma_start(Was[:, l, :, 0:D], kp(gnn1_Wagg[l])).then_inc(w, 16)
                act.dma_start(Was[:, l, :, D:2 * D], kp(gnn1_Wself[l])).then_inc(w, 16)
            act.dma_start(colb[:, 8:10], gnn1_bin.rearrange("(k p) -> p k", p=P), allow_slow_non_contiguous=True).then_inc(w, 16)
            act.dma_start(colb[:, 10:12], mix1_bqkv[2 * D:3 * D].rearrange("(k p) -> p k", p=P), allow_slow_non_contiguous=True).then_inc(w, 16)
            def take_xT(n, b):
                act.wait_ge(sem("f_xt_done"), n + 1)
                act.wait_ge(sem("f_h_done"), n + 1)
                nc.scalar.copy(f_xT[:, b], banks[b][:, 0:2 * P].rearrange("p (k n) -> p k n", k=KD))\
                    .then_inc(sem("f_xt_taken"), 1)

            def take_h(n, b):
                act.wait_ge(sem("f_h_done"), n + 3)
                act.wait_ge(sem("f_o_done"), n + 1)
                nc.scalar.activation(f_h[:, b, :], banks[2 + b][0:H0, 0:P], ACT.Relu).then_inc(sem("f_h_taken"), 1)

            def load_x(n, s):
                act.dma_start(f_x[:, s, :], xs_d[bass.ds(n * P, P), :]).then_inc(sem(f"f_x_loaded{s}"), 16)

            act.wait_ge(sem("tokens_scattered"), 16 * T)
            for s in range(4):
                load_x(s, s)
            for s in range(2):
                take_xT(s, s)
                load_x(s + 4, s)
            take_h(0, 0)
            with act.Fori(0, FT // 8 - 1) as it:
                for s in range(8):
                    take_xT(it * 8 + (s + 2), s % 2)
                    load_x(it * 8 + (s + 6), (s + 2) % 4)
                    take_h(it * 8 + (s + 1), (s + 1) % 2)
            for n in range(FT - 8, FT):
                if n + 2 < FT:
                    take_xT(n + 2, n % 2)
                if n + 6 < FT:
                    load_x(n + 6, (n + 2) % 4)
                if n + 1 < FT:
                    take_h(n + 1, (n + 1) % 2)
            for w in range(2):
                act.wait_ge(sem("WT_done"), w + 1)
                for k in range(KD):
                    nc.scalar.copy(WT[:, w, k, :], banks[k][:, 0:D]).then_inc(sem("WT_taken"), 1)
            act.wait_ge(sem("fold_done"), 4)
            for k in range(KD):
                nc.scalar.copy(Was[:, 0, k, :], banks[2 + k][:, :]).then_inc(sem("fold_taken"), 1)
                nc.scalar.copy(Wvo[:, k, :], banks[4 + k][:, 0:D]).then_inc(sem("fold_taken"), 1)
            nc.scalar.copy(rowb[0:1, 768:1024], banks[7][0:1, 0:D]).then_inc(sem("fold_taken"), 1)
            sqrt_of(2)
            take_transposed(2, xT)
            for l in range(3):
                if l == 1:
                    act.wait_ge(sem("kn_ready"), 1)
                    nc.scalar.sqrt(kn[:, 2:4], kn[:, 0:2]).then_inc(sem("kn_sqrt"), 1)
                    act.wait_ge(sem("kvT_done"), 1)
                    for k in range(KD):
                        nc.scalar.copy(kvT[:, k, :], banks[k][:, 0:D]).then_inc(sem("kvT_taken"), 1)
                    act.wait_ge(sem("m2_done"), 1)
                    for k in range(KD):
                        nc.scalar.copy(kv[:, k, :], banks[2 + k][:, 0:D]).then_inc(sem("m2_taken"), 1)
                layer(l)
                take_transposed(3 + l, hT, relu=True, rows_stage=4 + l if l < 2 else None)
            sqrt_of(3)
            take_transposed(6, xT)
            act.wait_ge(sem("rt_exp"), 1)
            nc.scalar.activation(top[0:1, 16:24], top[0:1, 8:16], ACT.Exp).then_inc(sem("rt_exp_done"), 1)
            act.wait_ge(sem("rt_exp"), 2)
            nc.scalar.activation(top[0:1, 16:24], top[0:1, 8:16], ACT.Exp).then_inc(sem("rt_exp_done"), 1)
            act.wait_ge(sem("rt_exp"), 3)
            nc.scalar.activation(top[0:1, 50:52], top[0:1, 48:50], ACT.Exp).then_inc(sem("rt_exp_done"), 1)
            act.wait_ge(sem("w_ffn1_in"), 64)
            i = 0
            for c in range(9):
                n = 384 if c < 8 else P
                for j in range(J1):
                    act.wait_ge(sem("h1_done"), i + 1)
                    if j == 0 and c >= 2:
                        act.wait_ge(sem("y1_done"), 3 * (c - 1))
                    nc.scalar.activation(gel[:, c % 2, j, 0:n], banks[i % 4][:, 0:n], ACT.Gelu,
                                         bias=colb[:, j:j + 1]).then_inc(sem("h1_taken"), 1)
                    i += 1

        @block.vector
        def _(dve):
            step = [0]
            V = nc.vector

            def link(ins):
                step[0] += 1
                ins.then_inc(sem("dve_step"), 1)
                dve.wait_ge(sem("dve_step"), step[0])

            def layer_norm(k, source, dest, ready, after=None, have_stats=False):
                if not have_stats:
                    for t in range(T):
                        last = V.bn_stats(stats[:, t, :], source[:, t, :])
                    link(last)
                for t in range(T):
                    last = V.bn_aggr(mv[:, t, :], stats[:, t, :])
                link(last)
                V.tensor_scalar(ln[:, 0, :], mv[:, :, 1], EPS, None, ALU.add).then_inc(sem("var_ready"), 1)
                dve.wait_ge(sem("sqrt_ready"), k + 1)
                link(V.reciprocal(ln[:, 2, :], ln[:, 1, :]))
                newton(ln[:, 2, :], ln[:, 0, :], ln[:, 3, :])
                for t in range(T + 4):
                    if t < T:
                        V.tensor_scalar(dest[:, t, :], source[:, t, :], mv[:, t, 0:1], ln[:, 2, t:t + 1],
                                        ALU.subtract, ALU.mult).then_inc(sem(ready), 1)
                    if after and t >= 4:
                        after(t - 4)

            def newton(r, v, tmp):
                link(V.tensor_tensor(tmp, r, r, ALU.mult))
                link(V.tensor_tensor(tmp, tmp, v, ALU.mult))
                link(V.tensor_scalar(tmp, tmp, -0.5, 1.5, ALU.mult, ALU.add))
                link(V.tensor_tensor(r, r, tmp, ALU.mult))

            V.memset(zero_row, 0.0).then_inc(sem("zero_row"), 1)
            V.memset(srcI[:, EC - 1:EC], T * P).then_inc(sem("edge_pad_set"), 1)
            V.memset(dstI[:, EC - 1:EC], 0).then_inc(sem("edge_pad_set"), 1)
            V.memset(wE[:, EC - 1:EC], 0.0).then_inc(sem("edge_pad_set"), 1)
            V.memset(x_sb[:, T - 1, :], 0.0).then_inc(sem("x_pad_set"), 1)
            link(V.memset(recs[:, :, :], 0.0))
            V.memset(recs[:, :, 1], -1.0).then_inc(sem("recs_empty"), 1)
            V.memset(binF[:, EC:EP], float(T))
            link(V.memset(e_mask, 1.0))
            V.memset(e_mask[:, :, 0:1], 0.0)
            V.memset(addr[:, EP:EE], 0.0)
            link(V.memset(edge[:, EC:EE, :], 0.0))
            dve.wait_ge(sem("edges_loaded"), 96)
            link(V.tensor_scalar(tmpI, srcI, 7, None, ALU.logical_shift_right))
            link(V.tensor_copy(binF[:, 0:EC], tmpI))
            link(V.tensor_scalar(tmpI, srcI, P - 1, None, ALU.bitwise_and))
            V.tensor_copy(edge[:, 0:EC, 1], tmpI)
            V.tensor_copy(edge[:, 0:EC, 0], dstI)
            V.tensor_copy(edge[:, 0:EC, 2], wE)
            for b in range(T):
                last = V.tensor_scalar(ohs[:, :, b, :], binF.rearrange("p (q j) -> p q j", q=4), float(b), None, ALU.is_equal, ALU.add,
                                       accum_out=rowtot[:, b:b + 1])
            last.then_inc(sem("edge_rowtot"), 1)

            def slots_of(nb, pre, total, k):
                dve.wait_ge(sem("bin_counts"), k + 1)
                link(V.tensor_scalar(cntI[:, 0:nb], total, float(P - 1), None, ALU.add))
                link(V.tensor_scalar(cntI[:, 0:nb], cntI[:, 0:nb], 7, None, ALU.logical_shift_right))
                link(V.tensor_copy(cnt[:, 0:nb], cntI[:, 0:nb]))
                link(V.tensor_tensor_scan(endt[:, 0:nb], ones[:, 0:nb], cnt[:, 0:nb], 0.0, ALU.mult, ALU.add))
                link(V.tensor_tensor(off[:, 0:nb], endt[:, 0:nb], cnt[:, 0:nb], ALU.subtract))
                link(V.tensor_scalar(off[:, 0:nb], off[:, 0:nb], float(P), -1.0, ALU.mult, ALU.add))
                link(V.tensor_tensor(off[:, 0:nb], off[:, 0:nb], pre, ALU.add))

            slots_of(T, banks[7][:, 0:T], banks[7][:, 32:32 + T], 0)
            for q in range(4):
                part = slice(q * EQ, (q + 1) * EQ)
                link(V.tensor_tensor_scan(e_scan.rearrange("p b j -> p (b j)"), e_mask.rearrange("p b j -> p (b j)"),
                                          ohs[:, q].rearrange("p b j -> p (b j)"), 0.0, ALU.mult, ALU.add))
                link(V.tensor_tensor(e_scan, e_scan, off[:, 0:T].unsqueeze(2).to_broadcast([P, T, EQ]), ALU.add))
                V.tensor_copy(off[:, 0:T], e_scan[:, :, EQ - 1])
                link(V.tensor_tensor(e_prod, e_scan, ohs[:, q], ALU.mult))
                link(V.tensor_reduce(posF[:, part], e_prod.rearrange("p b j -> p j b"), AX, ALU.add))
                link(V.tensor_copy(posI0[:, part], posF[:, part]))
                link(V.tensor_scalar(lowI, posI0[:, part], P - 1, None, ALU.bitwise_and))
                link(V.tensor_scalar(posI0[:, part], posI0[:, part], 7, None, ALU.logical_shift_right))
                link(V.scalar_tensor_tensor(addr[:, part], lowI, float(NT), posI0[:, part], ALU.mult, ALU.add))
                dve.sem_inc(sem("edge_slots"), (q + 1) * EQ // U - q * EQ // U + (1 if q == 3 else 0))
            dve.wait_ge(sem("consts"), 8)
            q = NT // 4
            cmp = accF[32:33, 0:q * T].rearrange("p (t b) -> p t b", b=T)
            for i in range(4):
                link(V.tensor_tensor(cmp, iotaT[:, i * q:(i + 1) * q].unsqueeze(2).to_broadcast([1, q, T]),
                                     endt[32:33, 0:T].unsqueeze(1).to_broadcast([1, q, T]), ALU.is_ge))
                link(V.tensor_reduce(accF[32:33, q * T:q * T + q], cmp, AX, ALU.add))
                link(V.tensor_copy(bins[:, i * q:(i + 1) * q], accF[32:33, q * T:q * T + q]))

            dve.wait_ge(sem("x_loaded"), 32)
            layer_norm(0, x_sb, rows, "normed")
            V.memset(accF[:, :], 0.0).then_inc(sem("acc_zero"), 1)
            dve.wait_ge(sem("w_block0"), 11 * 16)
            for t in range(T):
                b = banks[4 + t % 2]
                dve.wait_ge(sem("lin_done"), t + 1)
                V.tensor_copy(rows[:, t, :], b[:, 0:D]).then_inc(sem("rows_ready"), 1)
                V.tensor_tensor(vals[:, t, :], b[:, D:2 * D], bcast[:, :], ALU.add).then_inc(sem("lin_taken"), 1)
            dve.wait_ge(sem("lin_taken"), T)
            dve.sem_inc(sem("v_bias_used"))
            dve.wait_ge(sem("lt_taken"), KD * len(CH))
            for k in range(KD):
                last = V.tensor_reduce(kmax[:, k:k + 1], hT[:, k, 0:N], AX, ALU.max, negate=True)
            last.then_inc(sem("kmax_ready"), 1)
            dve.wait_ge(sem("exp_ready"), KD)
            link(V.reciprocal(kinv, ksum))
            dve.wait_ge(sem("lam_done"), T)
            for k in range(KD):
                last = V.tensor_scalar(bn[:, k, :], banks[4 + k][:, 0:D], kinv[:, k:k + 1], None, ALU.mult)
            link(last)
            for k in range(KD):
                link(V.bn_stats(bnst[:, 6 * k:6 * k + 6], bn[:, k, :]))
                link(V.bn_aggr(bnmv[:, 2 * k:2 * k + 2], bnst[:, 6 * k:6 * k + 6]))
            V.tensor_scalar(bnt[:, 0:2], bnmv.rearrange("p (k c) -> p k c", c=2)[:, :, 1], EPS, None, ALU.add)\
                .then_inc(sem("bn_var"), 1)
            dve.wait_ge(sem("bn_sqrt"), 1)
            link(V.reciprocal(bnt[:, 4:6], bnt[:, 2:4]))
            newton(bnt[:, 4:6], bnt[:, 0:2], bnt[:, 6:8])
            for k in range(KD):
                link(V.tensor_scalar(bn[:, k, :], bn[:, k, :], bnmv[:, 2 * k:2 * k + 1], bnt[:, 4 + k:5 + k],
                                     ALU.subtract, ALU.mult))
                V.tensor_scalar(bn[:, k, :], bn[:, k, :], colb[:, 4 + k:5 + k], colb[:, 6 + k:7 + k],
                                ALU.mult, ALU.add).then_inc(sem("bn_ready"), 1)
            for t in range(T):
                dve.wait_ge(sem("lin_done"), T + t + 1)
                V.tensor_tensor(x_sb[:, t, :], x_sb[:, t, :], banks[4 + t % 2][:, 0:D], ALU.add)\
                    .then_inc(sem("lin_taken"), 1)

            def row_matrices(a, slot, tiles, done):
                m = oh[:, slot:slot + AHEAD, :]
                ins = V.tensor_tensor(m, iota[:, :].unsqueeze(1).to_broadcast([P, AHEAD, P]),
                                      recs[:, tiles, 1].unsqueeze(2).to_broadcast([P, AHEAD, P]), ALU.is_equal)
                if a == 0:
                    ins.then_inc(sem("matrix_01"), 1)
                    dve.wait_ge(sem("matrix_01"), done)
                    ins = V.tensor_tensor(m, m, recs[:, tiles, 2].unsqueeze(2).to_broadcast([P, AHEAD, P]), ALU.mult)
                ins.then_inc(sem("row_matrix"), 1)

            def sum_products(a, it, u):
                if u % AHEAD == 0:
                    row_matrices(a, (u + AHEAD) % MRING, bass.ds(it * U + (u + AHEAD), AHEAD),
                                 it * (U // AHEAD) + (u // AHEAD + 2))
                tile = dve.value_load(bins[:, bass.ds(it * U + u, 1)]).with_bounds(min_val=0, max_val=T)
                if u % 2 == 0:
                    dve.wait_ge(sem("product"), it * U + (a * NT + u + 2 + U))
                dve.wait_ge(sem("summed"), it * U + (a * NT + u + SLOTS))
                to = acc[:, bass.ds(tile, 1), :].rearrange("p a b -> p (a b)")
                V.tensor_tensor(to, to, banks[4 + u % SLOTS][:, 0:AW], ALU.add).then_inc(sem("summed"), 1)

            def start_sums(a):
                dve.wait_ge(sem("rows_stored"), 16 * len(TG) * (a + 1))
                V.memset(g[:, :, D:AW], 1.0).then_inc(sem("g_ones"), 1)
                row_matrices(a, 0, slice(0, AHEAD), 1)

            def take_self(k):
                dve.wait_ge(sem("self_done"), k[1])
                V.tensor_tensor(vals[:, bass.ds(k[0], 1), :].rearrange("p a b -> p (a b)"), banks[3][:, D:2 * D],
                                bcast[:, :], ALU.add).then_inc(sem("self_taken"), 1)

            def beside(l, k, u):
                xk = x_sb[:, bass.ds(k, 1), :].rearrange("p a b -> p (a b)")
                if l == 0 and u == 6:
                    dve.wait_ge(sem("m_square"), k + 1)
                    link_loop(V.tensor_scalar(m1[:, 3:4], m1[:, 2:3], 1e-7, None, ALU.add), "m_plus", k, 1, 0)
                    V.reciprocal(m1[:, 4:5], m1[:, 3:4]).then_inc(sem("m_scale"), 1)
                if l == 0 and u == 10:
                    dve.wait_ge(sem("m_out"), k + 1)
                    V.tensor_tensor(xk, xk, banks[3][:, 0:D], ALU.add)
                    take_self((k, k + 1))
                if l == 1 and u == 8:
                    dve.wait_ge(sem("n_root"), k + 1)
                    link_loop(V.tensor_scalar(m1[:, 8:9], m1[:, 2:3], 1e-7, None, ALU.add), "n_link", k, 4, 0)
                    link_loop(V.reciprocal(m1[:, 9:10], m1[:, 8:9]), "n_link", k, 4, 1)
                    link_loop(V.tensor_scalar(m1[:, 10:11], m1[:, 5:6], m1[:, 9:10], 1e-12, ALU.mult, ALU.max),
                              "n_link", k, 4, 2)
                    link_loop(V.reciprocal(m1[:, 11:12], m1[:, 10:11]), "n_link", k, 4, 3)
                    V.tensor_tensor(m1[:, 12:13], m1[:, 11:12], m1[:, 9:10], ALU.mult).then_inc(sem("n_scale"), 1)
                if l == 1 and u == 13:
                    dve.wait_ge(sem("n_mixed"), k + 2)
                    dve.wait_ge(sem("n_scale"), k + 2)
                    V.scalar_tensor_tensor(xk, banks[1][:, 0:D], m1[:, 12:13], xk, ALU.mult, ALU.add)\
                        .then_inc(sem("n_mixed_taken"), 1)
                if l >= 1 and u == 5:
                    take_self((k, k + (l * T + 1)))

            def link_loop(ins, name, k, n, i):
                ins.then_inc(sem(name), 1)
                dve.wait_ge(sem(name), k * n + (i + 1))

            def layer_sums(l):
                start_sums(l + 1)
                last = NT // U - 1
                with dve.Fori(0, last) as it:
                    for u in range(U):
                        beside(l, it * 2 + u // 16, u % 16)
                        sum_products(l + 1, it, u)
                for u in range(U):
                    if u < 16:
                        beside(l, last * 2, u)
                    sum_products(l + 1, last, u)
                dve.wait_ge(sem("summed"), (l + 2) * NT + SLOTS)

            dve.wait_ge(sem("recs_loaded"), 16)
            dve.wait_ge(sem("zeros_stored"), 64)
            start_sums(0)
            with dve.Fori(0, NT // U) as it:
                for u in range(U):
                    sum_products(0, it, u)
            dve.wait_ge(sem("summed"), NT + SLOTS)
            link(V.tensor_tensor(x_sb[:, :, :], x_sb[:, :, :], acc[:, 0:T, 0:D], ALU.add))
            dve.wait_ge(sem("rows_stored"), 16 * len(TG))
            def take_logits(t):
                dve.wait_ge(sem("lin_done"), 2 * T + t + 1)
                V.tensor_tensor(r_lg[:, t, :], banks[4 + t % 2][:, 0:EX], rbias, ALU.add).then_inc(sem("lin_taken"), 1)

            layer_norm(1, x_sb, rows, "normed", after=take_logits)
            dve.wait_ge(sem("lin_taken"), 3 * T)
            for t in range(T):
                last = V.max(out=r_m8[:, t, :], in_=r_lg[:, t, :])
            link(last)
            for t in range(T):
                last = V.max_index(out=r_i8[:, t, :], in_max=r_m8[:, t, :], in_values=r_lg[:, t, :])
            link(last)
            link(V.tensor_copy(r_eid, r_i8[:, :, 0]))
            link(V.tensor_tensor(r_oh, iota[:, 0:EX].unsqueeze(2).to_broadcast([P, EX, T]),
                                 r_eid.unsqueeze(1).to_broadcast([P, EX, T]), ALU.is_equal))
            link(V.tensor_scalar(r_oh[:, :, T - 1], r_oh[:, :, T - 1], rowok[:, :], None, ALU.mult))
            V.tensor_reduce(rowtot[:, 0:EX], r_oh, AX, ALU.add).then_inc(sem("edge_rowtot"), 1)
            link(V.memset(r_msk, 1.0))
            link(V.memset(r_msk[:, :, 0], 0.0))
            link(V.tensor_tensor_scan(r_sc.rearrange("p b t -> p (b t)"), r_msk.rearrange("p b t -> p (b t)"),
                                      r_oh.rearrange("p b t -> p (b t)"), 0.0, ALU.mult, ALU.add))
            slots_of(EX, banks[7][:, 0:EX], banks[7][:, 32:32 + EX], 1)
            link(V.tensor_tensor(r_sc, r_sc, off[:, 0:EX].unsqueeze(2).to_broadcast([P, EX, T]), ALU.add))
            link(V.tensor_tensor(r_sc, r_sc, r_oh, ALU.mult))
            link(V.tensor_reduce(r_eid, r_sc.rearrange("p b t -> p t b"), AX, ALU.add))
            link(V.tensor_copy(posI[:, 0:T], r_eid))
            V.memset(invdeg, 0.0).then_inc(sem("pos_ready"), 1)
            ce = wB[0:3 * EX, 0:FT * EX].rearrange("p (t b) -> p t b", b=EX)
            link(V.tensor_tensor(ce, iota[0:3 * EX, 0:FT].unsqueeze(2).to_broadcast([3 * EX, FT, EX]),
                                 endt[0:3 * EX, 0:EX].unsqueeze(1).to_broadcast([3 * EX, FT, EX]), ALU.is_ge))
            link(V.tensor_reduce(f_exp, ce, AX, ALU.add))
            link(V.tensor_scalar(f_exp, f_exp, float(EX - 1), None, ALU.min))
            V.tensor_copy(eidx[32:33, 0:FT], f_exp[32:33, :]).then_inc(sem("expert_table"), 1)
            link(V.tensor_scalar(f_row, ones[0:3 * EX, :], rowid[0:3 * EX, :], None, ALU.mult))
            for i in (1, 2):
                r = f_row[EX * i:EX * (i + 1), :]
                link(V.tensor_scalar(r, r, float(EX * i), None, ALU.subtract))
            dve.wait_ge(sem("f_biases"), 96)
            link(V.tensor_copy(f_parts, f_b))
            for i in (1, 2):
                for j in range(i, 3):
                    s = slice(EX * j, EX * (j + 1))
                    link(V.tensor_tensor(f_rest[s, :], (f_b if i == 1 else f_rest)[s, :], f_parts[s, :], ALU.subtract))
                    link(V.tensor_copy(f_parts[s, :], f_rest[s, :]))
            dve.sem_inc(sem("f_parts"), 1)

            def select(s, e):
                V.tensor_scalar(f_sel[:, s, :], f_row, e, None, ALU.is_equal).then_inc(sem("f_selected"), 1)

            def take_y(n, s, stored):
                dve.wait_ge(sem("f_o_done"), n + 3)
                if stored is not None:
                    dve.wait_ge(sem(f"f_stored{s}"), stored)
                V.tensor_scalar(f_y[:, s, :], banks[4 + s % 2][:, 0:D], 0.0, None, ALU.max)\
                    .then_inc(sem("f_y_ready"), 1)

            for s in range(4):
                select(s, f_exp[:, s:s + 1])
            dve.sem_inc(sem("f_y_ready"), 2)
            for n in range(4):
                take_y(n, n, None)
                select(n, f_exp[:, n + 4:n + 5])
            with dve.Fori(0, FT // 4 - 2) as it:
                for s in range(4):
                    take_y(it * 4 + (s + 4), s, it * 16 + 16)
                    select(s, f_exp[:, bass.ds(it * 4 + (s + 8), 1)])
            for n in range(FT - 4, FT):
                take_y(n, n % 4, 16 * (n // 4))
                if n + 4 < FT:
                    select(n % 4, f_exp[:, n + 4:n + 5])
            dve.wait_ge(sem("w_gnn1"), 10 * 16)
            for k in range(KD):
                V.tensor_scalar(b_in[:, k, :], ones[:, :], colb[:, 8 + k:9 + k], None, ALU.mult).then_inc(sem("b_in_ready"), 1)
            dve.wait_ge(sem("fold_done"), 4)
            V.tensor_copy(gbias, banks[6][:, 0:D]).then_inc(sem("gbias_ready"), 1)
            dve.wait_ge(sem("bhid_loaded"), 16)
            link(V.tensor_tensor(bcast[:, :], bcast[:, :], banks[6][:, D:2 * D], ALU.add))
            dve.sem_inc(sem("bhid_used"), 1)
            dve.wait_ge(sem("gbias_ready"), 1)
            for t in range(T + 1):
                if t < T:
                    dve.wait_ge(sem(f"gathered{t % RING}"), 16 * (NT // RING + t // RING + 1))
                    xt_ = x_sb[0:tw(t), t, :]
                    V.tensor_tensor(xt_, xt_, vals[0:tw(t), t, :], ALU.add).then_inc(sem("x_added"), 1)
                if t >= 1:
                    dve.wait_ge(sem("x_added"), t)
                    last = V.bn_stats(stats[:, t - 1, :], x_sb[:, t - 1, :])
            link(last)
            def rows_out(t):
                dve.wait_ge(sem("lin_done"), 3 * T + t + 1)
                V.tensor_tensor(rows[:, t, :], banks[4 + t % 2][:, 0:D], gbias, ALU.add).then_inc(sem("lin_taken"), 1)
                dve.wait_ge(sem("lin_taken"), 3 * T + t + 1)
                dve.sem_inc(sem("rows_ready"), 1)

            layer_norm(2, x_sb, rows, "normed", after=rows_out, have_stats=True)
            dve.sem_inc(sem("self_taken"), 1)
            dve.wait_ge(sem("rows_ready"), 2 * T)
            for l in range(3):
                dve.wait_ge(sem("normed"), (3 + l) * T)
                link(V.memset(accF[:, :], 0.0))
                dve.wait_ge(sem("bhid_used"), 1) if l == 0 else dve.wait_ge(sem("bhid_loaded"), 16 * (l + 1))
                if l == 1:
                    dve.wait_ge(sem("kn_sqrt"), 1)
                    link(V.tensor_scalar(kn[:, 2:4], kn[:, 2:4], 1e-12, None, ALU.max))
                    link(V.reciprocal(kn[:, 0:2], kn[:, 2:4]))
                    link(V.tensor_scalar(kn[:, 0:2], kn[:, 0:2], float(N) ** -0.5, None, ALU.mult))
                    for k in range(KD):
                        V.tensor_scalar(kvs[:, k, :], kv[:, k, :], kn[:, k:k + 1], None, ALU.mult)\
                            .then_inc(sem("kv_scaled"), 1)
                if l == 2:
                    dve.wait_ge(sem("row_spread"), 1)
                    dve.wait_ge(sem("n_mixed_taken"), T + 1)
                    link(V.tensor_tensor(x_sb[:, :, :], x_sb[:, :, :],
                                         banks[0][:, 0:D].unsqueeze(1).to_broadcast([P, T, D]), ALU.add))
                layer_sums(l)
                if l == 0:
                    dve.wait_ge(sem("kv_closed"), 1)
                    for k in range(KD):
                        V.tensor_copy(kv[:, k, :], banks[k][:, 0:D]).then_inc(sem("kv_saved"), 1)
                        V.tensor_copy(kn[:, k:k + 1], banks[k][:, D:AW]).then_inc(sem("kv_saved"), 1)
                    dve.wait_ge(sem("kv_saved"), 2 * KD)
                    dve.sem_inc(sem("kn_ready"), 1)
                    link(V.tensor_scalar(invdeg, acc[:, 0:T, D], 1.0, None, ALU.max))
                    link(V.reciprocal(invdeg, invdeg))
                for t in range(T + 5):
                    if t < T:
                        V.scalar_tensor_tensor(rows[:, t, :], acc[:, t, 0:D], invdeg[:, t:t + 1], vals[:, t, :],
                                               ALU.mult, ALU.add).then_inc(sem("normed"), 1)
                    if l == 2 and 4 <= t < T + 4:
                        dve.wait_ge(sem("lin_done"), 6 * T + t - 3)
                        V.tensor_tensor(x_sb[:, t - 4, :], x_sb[:, t - 4, :], banks[4 + t % 2][:, 0:D], ALU.add)\
                            .then_inc(sem("lin_taken"), 1)
                    if l == 2 and t >= 5:
                        dve.wait_ge(sem("lin_taken"), 6 * T + t - 4)
                        last = V.bn_stats(stats[:, t - 5, :], x_sb[:, t - 5, :])
            link(last)
            dve.wait_ge(sem("lin_taken"), 7 * T)
            dve.wait_ge(sem("tr_done"), 6 * T)
            layer_norm(3, x_sb, rows, "normed", have_stats=True)
            dve.wait_ge(sem("col_sums"), 1)
            for k in range(KD):
                V.tensor_scalar(ksum[:, k:k + 1], banks[6 + k][:, 0:1], 1.0 / N, None, ALU.mult).then_inc(sem("mean_ready"), 1)
            lg, e8, p8 = top[0:1, 0:8], top[0:1, 8:16], top[0:1, 16:24]
            s1, s2, s3, v8 = top[0:1, 24:25], top[0:1, 25:26], top[0:1, 32:40], top[0:1, 40:48]
            dve.wait_ge(sem("route_done"), 1)
            dve.wait_ge(sem("wr_loaded"), 32)
            link(V.tensor_tensor(lg, banks[7][0:1, 0:EX1], rowb[0:1, 512:520], ALU.add))

            def softmax8(k):
                link(V.tensor_reduce(s1, lg, AX, ALU.max))
                V.tensor_scalar(e8, lg, s1, None, ALU.subtract).then_inc(sem("rt_exp"), 1)
                dve.wait_ge(sem("rt_exp_done"), k)
                link(V.tensor_reduce(s1, p8, AX, ALU.add))
                link(V.reciprocal(s2, s1))
                link(V.tensor_scalar(p8, p8, s2, None, ALU.mult))

            softmax8(1)
            link(V.tensor_scalar(s3, p8, float(N), None, ALU.mult))
            link(V.tensor_scalar(v8, s3, CAPACITY, None, ALU.is_gt))
            link(V.reciprocal(s3, s3))
            link(V.tensor_scalar(s3, s3, CAPACITY, -1.0, ALU.mult, ALU.add))
            link(V.tensor_tensor(s3, s3, v8, ALU.mult))
            link(V.tensor_scalar(s3, s3, 1.0, None, ALU.add))
            link(V.tensor_tensor(lg, p8, s3, ALU.mult))
            softmax8(2)
            link(V.max(out=v8, in_=p8))
            link(V.max_index(out=eidx[0:1, 8:16].bitcast(U32), in_max=v8, in_values=p8))
            link(V.tensor_copy(top[0:1, 56:64], eidx[0:1, 8:16].bitcast(U32)))
            V.tensor_copy(eidx[0:1, 0:8], top[0:1, 56:64]).then_inc(sem("experts_chosen"), 1)
            V.tensor_scalar(top[0:1, 48:50], v8[:, 0:2], v8[:, 0:1], None, ALU.subtract).then_inc(sem("rt_exp"), 1)
            dve.wait_ge(sem("rt_exp_done"), 3)
            link(V.tensor_reduce(s1, top[0:1, 50:52], AX, ALU.add))
            link(V.reciprocal(s2, s1))
            V.tensor_scalar(top[0:1, 52:54], top[0:1, 50:52], s2, None, ALU.mult).then_inc(sem("gates_ready"), 1)
            dve.wait_ge(sem("row_spread"), 2)
            link(V.tensor_copy(kinv, banks[7][:, 16:18]))
            dve.wait_ge(sem("w_ffn1_out"), 96)
            for k in range(2):
                link(V.tensor_scalar(rowb[0:1, k * D:(k + 1) * D], rowb[0:1, k * D:(k + 1) * D], kinv[0:1, k:k + 1],
                                     None, ALU.mult))
            link(V.tensor_tensor(rowb[0:1, 0:D], rowb[0:1, 0:D], rowb[0:1, D:2 * D], ALU.add))
            for j in range(J1):
                V.tensor_scalar(W2c[:, j, :], W2c[:, j, :], kinv[:, j * 2 // J1:j * 2 // J1 + 1], None, ALU.mult)\
                    .then_inc(sem("w2_scaled"), 1)
            for c in range(9):
                ts = range(3 * c, min(3 * c + 3, T))
                a, b = ts[0], ts[-1] + 1
                if c == 0:
                    dve.wait_ge(sem("row_spread"), 3)
                link(V.tensor_tensor(rows[:, a:b, :], rows[:, a:b, :],
                                     banks[6][:, 0:D].unsqueeze(1).to_broadcast([P, b - a, D]), ALU.add))
                for t in ts:
                    dve.wait_ge(sem("y1_done"), t + 1)
                    V.tensor_tensor(rows[:, t, :], rows[:, t, :], banks[4 + t % 2][:, 0:D], ALU.add)\
                        .then_inc(sem("y1_taken"), 1)
                dve.wait_ge(sem("y1_taken"), b)
                for t in ts:
                    last = V.bn_stats(stats[:, t, :], rows[:, t, :])
                link(last)
                for t in ts:
                    last = V.bn_aggr(mv[:, t, :], stats[:, t, :])
                link(last)
                link(V.tensor_scalar(ln[:, 0, a:b], mv[:, a:b, 1], EPS, None, ALU.add))
                bits = ln[:, 2, a:b].bitcast(I32)
                link(V.tensor_scalar(bits, ln[:, 0, a:b].bitcast(I32), 1, None, ALU.logical_shift_right))
                link(V.tensor_scalar(bits, bits, -1.0, float(0x5f3759df), ALU.mult, ALU.add))
                for _ in range(3):
                    newton(ln[:, 2, a:b], ln[:, 0, a:b], ln[:, 3, a:b])
                for t in ts:
                    last = V.tensor_scalar(vals[:, t, :], rows[:, t, :], mv[:, t, 0:1], ln[:, 2, t:t + 1],
                                           ALU.subtract, ALU.mult)
                link(last)
                v = vals[:, a:b, :]
                link(V.tensor_tensor(v, v, bcast[:, :].unsqueeze(1).to_broadcast([P, b - a, D]), ALU.mult))
                link(V.tensor_tensor(v, v, wB[:, 0:D].unsqueeze(1).to_broadcast([P, b - a, D]), ALU.add))
                V.tensor_tensor(v, v, x_sb[:, a:b, :], ALU.add).then_inc(sem("out_ready"), 1)

        @block.tensor
        def _(pe):
            mm, tr = nc.tensor.matmul, nc.tensor.transpose

            def transpose(s, t):
                pe.wait_ge(sem("normed"), s * T + t + 1)
                if s * T + t >= 4:
                    pe.wait_ge(sem("tr_taken"), s * T + max(t - 3, 0))
                for k in range(KD):
                    last = tr(banks[t % 4][:, k * P:(k + 1) * P], rows[:, t, k * P:(k + 1) * P], ident[:, :])
                last.then_inc(sem("tr_done"), 1)

            def transposes(s):
                for t in range(T):
                    transpose(s, t)

            def transposes_and_linear(s, s2, source, W, n, bias=None):
                for t in range(T + 2):
                    if t < T:
                        transpose(s, t)
                    if t >= 2:
                        pe.wait_ge(sem("tr_taken"), s * T + t - 1)
                        linear_tile(s2, t - 2, source, W, n, bias)

            def linear_tile(s, t, source, W, n, bias=None):
                pe.wait_ge(sem("lin_taken"), s * T + max(t - 1, 0)) if s or t >= 2 else None
                o = banks[4 + t % 2][:, 0:n]
                if bias is not None:
                    mm(o, ones[0:1, :], bias, start=True, stop=False)
                for k in range(KD):
                    last = mm(o, source[:, k, t * P:(t + 1) * P], W[:, k, 0:n],
                              start=k == 0 and bias is None, stop=k == KD - 1)
                last.then_inc(sem("lin_done"), 1)

            def linear(s, source, W, n, bias=None):
                for t in range(T):
                    linear_tile(s, t, source, W, n, bias)

            def linearT(first, chunks, W):
                for e in range(KD):
                    for c, (a, n) in enumerate(chunks):
                        i = e * len(chunks) + c
                        if first + i >= 2:
                            pe.wait_ge(sem("lt_taken"), first + i - 1)
                        for k in range(KD):
                            last = mm(banks[2 + i % 2][:, 0:n], W[:, k, e * P:(e + 1) * P], xT[:, k, a:a + n],
                                      start=k == 0, stop=k == KD - 1)
                        last.then_inc(sem("lt_done"), 1)

            def bin_counts(nb, k):
                pe.wait_ge(sem("edge_rowtot"), k + 1)
                mm(banks[7][:, 0:nb], tri[:, :], rowtot[:, 0:nb], start=True, stop=True)
                mm(banks[7][:, 32:32 + nb], ones[:, :], rowtot[:, 0:nb], start=True, stop=True)\
                    .then_inc(sem("bin_counts"), 1)

            pe.wait_ge(sem("consts"), 8)
            bin_counts(T, 0)
            transposes(0)
            pe.wait_ge(sem("w_block0"), 11 * 16)
            pe.wait_ge(sem("tr_taken"), T)
            linear(0, xT, W0V, 2 * D)
            linearT(0, CH, Wk)
            pe.wait_ge(sem("exp_ready"), KD)
            pe.wait_ge(sem("lin_taken"), T)
            for t in range(T + 1):
                if t < T:
                    if t >= 2:
                        pe.wait_ge(sem("et_taken"), t - 1)
                    for k in range(KD):
                        last = tr(banks[t % 2][0:tw(t), k * P:(k + 1) * P], hT[:, k, t * P:t * P + tw(t)], ident[:, :])
                    last.then_inc(sem("et_done"), 1)
                if t >= 1:
                    u = t - 1
                    pe.wait_ge(sem("et_taken"), u + 1)
                    for k in range(KD):
                        last = mm(banks[4 + k][:, 0:D], xt[0:tw(u), u % 2, k, :], vals[0:tw(u), u, :],
                                  start=u == 0, stop=u == T - 1)
                    last.then_inc(sem("lam_done"), 1)
            pe.wait_ge(sem("et_taken"), T)
            for k in range(KD):
                for j in range(KD):
                    last = tr(banks[k][:, j * P:(j + 1) * P], Wq[:, j, k * P:(k + 1) * P], ident[:, :])
                last.then_inc(sem("wqT_done"), 1)
            pe.wait_ge(sem("wqT_taken"), KD)
            pe.wait_ge(sem("bn_ready"), KD)
            pe.wait_ge(sem("lt_taken"), KD * len(CH))
            for j in range(KD):
                for k in range(KD):
                    last = mm(banks[2 + j][:, 0:D], WqT[:, k, j * P:(j + 1) * P], bn[:, k, :],
                              start=k == 0, stop=k == KD - 1)
                last.then_inc(sem("mx_done"), 1)
            for k in range(KD):
                last = mm(banks[6][0:1, 0:D], colb[:, 2 + k:3 + k], bn[:, k, :], start=k == 0, stop=k == KD - 1)
            last.then_inc(sem("mx_done"), 1)
            for k in range(KD):
                last = tr(banks[0][:, k * EX:(k + 1) * EX], rw[:, k * P:(k + 1) * P], ident[0:EX, 0:EX])
            last.then_inc(sem("rwT_done"), 1)
            pe.wait_ge(sem("mx_taken"), KD + 1)
            linear(1, xT, Mx, D, rowb[0:1, 256:512])

            def product(a, it, u):
                tokens = 0 if a == 0 else len(range(u % RING, T, RING))
                pe.wait_ge(sem(f"gathered{u % RING}"),
                           it * (16 * U // RING) + (16 * (a * NT // RING + u // RING + 1 + tokens)))
                if u % AHEAD == 0:
                    pe.wait_ge(sem("row_matrix"), it * (U // AHEAD) + (a * (NT // AHEAD + 1) + u // AHEAD + 1))
                pe.wait_ge(sem("summed"), it * U + (a * NT + u + 1))
                mm(banks[4 + u % SLOTS][:, 0:AW], oh[:, u % MRING, :], g[:, u % RING, :],
                   start=True, stop=True).then_inc(sem("product"), 1)

            pe.wait_ge(sem("lin_taken"), 2 * T)
            pe.sem_inc(sem("product"), U)
            pe.sem_inc(sem("summed"), SLOTS)
            pe.wait_ge(sem("g_ones"), 1)
            with pe.Fori(0, NT // U) as it:
                for u in range(U):
                    product(0, it, u)
            pe.wait_ge(sem("rwT_taken"), 1)
            transposes_and_linear(1, 2, xT, rwT, EX)
            bin_counts(EX, 1)
            pe.sem_inc(sem("f_h_done"), 2)
            pe.sem_inc(sem("f_o_done"), 2)
            pe.wait_ge(sem("lin_taken"), 3 * T)
            def f_transpose(s, loaded):
                pe.wait_ge(sem(f"f_x_loaded{s}"), loaded)
                for k in range(KD):
                    last = tr(banks[s % 2][:, k * P:(k + 1) * P], f_x[:, s, k * P:(k + 1) * P], ident[:, :])
                last.then_inc(sem("f_xt_done"), 1)

            def f_hidden(n, s, loaded):
                pe.wait_ge(sem(f"f_loaded{s % 4}"), loaded)
                pe.wait_ge(sem("f_xt_taken"), n + 1)
                pe.wait_ge(sem("f_selected"), n + 1)
                o = banks[2 + s % 2][0:H0, 0:P]
                mm(o, f_b1, f_sel[:, s % 4, :], start=True, stop=False)
                for k in range(KD):
                    last = mm(o, f_w1[:, s % 4, k, :], f_xT[:, s % 2, k, :], start=False, stop=k == KD - 1)
                last.then_inc(sem("f_h_done"), 1)

            def f_out(n, s):
                pe.wait_ge(sem("f_h_taken"), n + 1)
                pe.wait_ge(sem("f_y_ready"), n + 1)
                o = banks[4 + s % 2][:, 0:D]
                mm(o, f_sel[:, s % 4, :], f_b2, start=True, stop=False)
                mm(o, f_h[:, s % 2, :], f_w2[:, s, :], start=False, stop=True).then_inc(sem("f_o_done"), 1)

            pe.wait_ge(sem("f_parts"), 1)
            f_transpose(0, 16)
            f_transpose(1, 16)
            f_hidden(0, 0, 32)
            with pe.Fori(0, FT // 8 - 1) as it:
                for s in range(8):
                    f_transpose((s + 2) % 4, it * 32 + 16 * ((s + 2) // 4 + 1))
                    f_hidden(it * 8 + (s + 1), (s + 1) % 8, it * 64 + 32 * ((s + 1) // 4 + 1))
                    f_out(it * 8 + s, s)
            for n in range(FT - 8, FT):
                if n + 2 < FT:
                    f_transpose((n + 2) % 4, 16 * ((n + 2) // 4 + 1))
                if n + 1 < FT:
                    f_hidden(n + 1, (n + 1) % 8, 32 * ((n + 1) // 4 + 1))
                f_out(n, n % 8)
            pe.wait_ge(sem("w_gnn1"), 10 * 16)
            for w, W in enumerate((Wio[:, 0], Wqkv[:, :, 2 * D:3 * D])):
                if w == 1:
                    pe.wait_ge(sem("w_mix1"), 5 * 16)
                    pe.wait_ge(sem("WT_taken"), KD)
                for k in range(KD):
                    for j in range(KD):
                        last = tr(banks[k][:, j * P:(j + 1) * P], W[:, j, k * P:(k + 1) * P], ident[:, :])
                last.then_inc(sem("WT_done"), 1)
            pe.wait_ge(sem("WT_taken"), 2 * KD)
            pe.wait_ge(sem("f_y_ready"), FT + 2)
            for w, (W, n) in enumerate(((Was[:, 0], 2 * D), (Wo1, D))):
                for j in range(KD):
                    for k in range(KD):
                        last = mm(banks[2 + 2 * w + j][:, 0:n], WT[:, w, k, j * P:(j + 1) * P], W[:, k, 0:n],
                                  start=k == 0, stop=k == KD - 1)
                last.then_inc(sem("fold_done"), 1)
            pe.wait_ge(sem("b_in_ready"), KD)
            for k in range(KD):
                last = mm(banks[6][:, :], b_in[:, k, :], Was[:, 0, k, :], start=k == 0, stop=k == KD - 1)
            last.then_inc(sem("fold_done"), 1)
            mm(banks[7][0:1, 0:D], ones[0:1, 0:1], rowb[0:1, 768:1024], start=True, stop=False)
            mm(banks[7][0:1, 0:D], ones[0:1, 0:1], rowb[0:1, 1024:1280], start=False, stop=False)
            for k in range(KD):
                last = mm(banks[7][0:1, 0:D], colb[:, 10 + k:11 + k], Wo1[:, k, :], start=False, stop=k == KD - 1)
            last.then_inc(sem("fold_done"), 1)
            pe.wait_ge(sem("fold_taken"), 2 * KD + 1)
            pe.wait_ge(sem("bhid_used"), 1)
            transposes_and_linear(2, 3, xT, Was[:, 0], D)

            def beside(l, k, u, n):
                if l == 0 and u == 0:
                    pe.wait_ge(sem("m_x"), k + 1)
                    mm(banks[2][:, :], ones[0:1, :], rowb[0:1, D:3 * D], start=True, stop=False)
                    for c in range(KD):
                        last = mm(banks[2][:, :], s_x[:, c, :], Wqkv[:, c, D:3 * D], start=False, stop=c == KD - 1)
                    last.then_inc(sem("m_proj"), 1)
                if l == 0 and u == 2:
                    pe.wait_ge(sem("self_taken"), k + 1)
                    for c in range(KD):
                        last = mm(banks[3][:, 0:D], s_x[:, c, :], Wvo[:, c, :], start=c == 0, stop=c == KD - 1)
                    last.then_inc(sem("m_out"), 1)
                    for c in range(KD):
                        last = mm(banks[3][:, D:2 * D], s_x[:, c, :], Wself[:, 0, c, :], start=c == 0, stop=c == KD - 1)
                    last.then_inc(sem("self_done"), 1)
                if l == 0 and u == 12:
                    pe.wait_ge(sem("m_k4"), k + 1)
                    for c in range(KD):
                        mm(banks[c][:, 0:D], s_k2[0:n, c * P:(c + 1) * P], s_v[0:n, :], start=False, stop=False)
                        last = mm(banks[c][:, D:AW], s_k4[0:n, c * P:(c + 1) * P], ones[0:n, 0:1],
                                  start=False, stop=False)
                    last.then_inc(sem("m_kv_done"), 1)
                if l == 1 and u == 0:
                    pe.wait_ge(sem("n_x"), k + 1)
                    mm(banks[2][:, 0:D], ones[0:1, :], rowb[0:1, 0:D], start=True, stop=False)
                    for c in range(KD):
                        last = mm(banks[2][:, 0:D], s_x[:, c, :], Wqkv[:, c, 0:D], start=False, stop=c == KD - 1)
                    last.then_inc(sem("n_proj"), 1)
                if l >= 1 and u == 2:
                    pe.wait_ge(sem("self_x"), k + ((l - 1) * T + 1))
                    for c in range(KD):
                        last = mm(banks[3][:, D:2 * D], s_h[:, c, :], Wself[:, l, c, :], start=c == 0, stop=c == KD - 1)
                    last.then_inc(sem("self_done"), 1)
                if l == 1 and u == 6:
                    pe.wait_ge(sem("n_square"), k + 1)
                    for c in range(KD):
                        last = tr(banks[0][:, c * P:(c + 1) * P], s_q2[:, c * P:(c + 1) * P], ident[:, :])
                    last.then_inc(sem("n_qT"), 1)
                if l == 1 and u == 9:
                    pe.wait_ge(sem("n_qT_taken"), k + 1)
                    pe.wait_ge(sem("n_mixed_taken"), k + 1)
                    for c in range(KD):
                        last = mm(banks[1][:, 0:D], s_q2T[:, c, :], kv[:, c, :], start=c == 0, stop=c == KD - 1)
                    last.then_inc(sem("n_mixed"), 1)

            def layer_products(l):
                pe.wait_ge(sem("g_ones"), l + 2)
                last = NT // U - 1
                with pe.Fori(0, last) as it:
                    for u in range(U):
                        beside(l, it * 2 + u // 16, u % 16, P)
                        product(l + 1, it, u)
                for u in range(U):
                    if u < 16:
                        beside(l, last * 2, u, TAIL)
                    product(l + 1, last, u)

            pe.wait_ge(sem("zero_row"), 1)
            pe.wait_ge(sem("tr_taken"), 3 * T)
            for c in range(KD):
                mm(banks[c][:, 0:AW], ones[64:65, :], zero_row, start=True, stop=False)
            pe.sem_inc(sem("m_kv_done"), 1)
            pe.sem_inc(sem("n_scale"), 1)
            pe.sem_inc(sem("n_mixed"), 1)
            pe.sem_inc(sem("n_mixed_taken"), 1)
            pe.wait_ge(sem("lin_taken"), 4 * T)
            for l in range(3):
                if l == 1:
                    pe.wait_ge(sem("kv_scaled"), KD)
                    for j in range(KD):
                        for k in range(KD):
                            last = tr(banks[j][:, k * P:(k + 1) * P], kvs[:, k, j * P:(j + 1) * P], ident[:, :])
                    last.then_inc(sem("kvT_done"), 1)
                    pe.wait_ge(sem("kvT_taken"), KD)
                    for c in range(KD):
                        for j in range(KD):
                            last = mm(banks[2 + c][:, 0:D], kvT[:, j, c * P:(c + 1) * P], Wo1[:, j, :],
                                      start=j == 0, stop=j == KD - 1)
                    last.then_inc(sem("m2_done"), 1)
                    pe.wait_ge(sem("m2_taken"), KD)
                if l == 2:
                    mm(banks[0][:, 0:D], ones[0:1, :], rowb[0:1, 768:1024], start=True, stop=True)\
                        .then_inc(sem("row_spread"), 1)
                layer_products(l)
                if l == 0:
                    for c in range(KD):
                        last = mm(banks[c][:, 0:AW], ones[64:65, :], zero_row, start=False, stop=True)
                    last.then_inc(sem("kv_closed"), 1)
                    pe.wait_ge(sem("kv_saved"), 2 * KD)
                if l < 2:
                    transposes_and_linear(3 + l, 4 + l, hT, Was[:, l + 1], D)
                    pe.wait_ge(sem("lin_taken"), (5 + l) * T)
                else:
                    transposes_and_linear(5, 6, hT, Wio[:, 1], D)
            for t in range(T):
                transpose(6, t)
                for k in range(KD):
                    last = mm(banks[6 + k][:, 0:1], rows[0:tw(t), t, k * P:(k + 1) * P], ones[0:tw(t), 0:1],
                              start=t == 0, stop=t == T - 1)
            last.then_inc(sem("col_sums"), 1)
            pe.wait_ge(sem("mean_ready"), KD)
            pe.wait_ge(sem("wr_loaded"), 32)
            for k in range(KD):
                last = mm(banks[7][0:1, 0:EX1], ksum[:, k:k + 1], top[:, 64 + 8 * k:72 + 8 * k], start=k == 0, stop=k == KD - 1)
            last.then_inc(sem("route_done"), 1)
            pe.wait_ge(sem("gates_ready"), 1)
            mm(banks[7][:, 16:18], ones[0:1, :], top[0:1, 52:54], start=True, stop=True).then_inc(sem("row_spread"), 1)
            pe.wait_ge(sem("w_ffn1_in"), 64)
            pe.wait_ge(sem("lin_taken"), 7 * T)
            i = 0
            for c in range(9):
                n = 384 if c < 8 else P
                for j in range(J1):
                    if i >= 4:
                        pe.wait_ge(sem("h1_taken"), i - 3)
                    for k in range(KD):
                        last = mm(banks[i % 4][:, 0:n], W1c[:, j * 2 // J1, k, (j % (J1 // 2)) * P:(j % (J1 // 2) + 1) * P],
                                  xT[:, k, c * 384:c * 384 + n], start=k == 0, stop=k == KD - 1)
                    last.then_inc(sem("h1_done"), 1)
                    i += 1
                pe.wait_ge(sem("h1_taken"), i)
                if c == 0:
                    pe.wait_ge(sem("w2_scaled"), J1)
                    mm(banks[6][:, 0:D], ones[0:1, :], rowb[0:1, 0:D], start=True, stop=True).then_inc(sem("row_spread"), 1)
                for s in range(n // P):
                    t = 3 * c + s
                    if t >= 2:
                        pe.wait_ge(sem("y1_taken"), t - 1)
                    o = banks[4 + t % 2][:, 0:D]
                    for j in range(J1):
                        last = mm(o, gel[:, c % 2, j, s * P:(s + 1) * P], W2c[:, j, :], start=j == 0, stop=j == J1 - 1)
                    last.then_inc(sem("y1_done"), 1)


_INS = ['x', 'src', 'dst', 'edge_weight', 'L0_gnn_weight', 'L0_mix_W_qk', 'L0_mix_b_qk', 'L0_mix_W_v', 'L0_mix_b_v',
        'L0_mix_gamma', 'L0_mix_beta', 'L0_ffn_router_w', 'L0_ffn_router_b', 'L0_ffn_W1', 'L0_ffn_b1', 'L0_ffn_W2',
        'L0_ffn_b2', 'L1_gnn_W_in', 'L1_gnn_b_in', 'L1_gnn_W_agg', 'L1_gnn_W_self', 'L1_gnn_b_hid', 'L1_gnn_W_out',
        'L1_gnn_b_out', 'L1_mix_W_qkv', 'L1_mix_b_qkv', 'L1_mix_W_out', 'L1_mix_b_out', 'L1_ffn_Wr', 'L1_ffn_br',
        'L1_ffn_W1', 'L1_ffn_b1', 'L1_ffn_W2', 'L1_ffn_b2', 'L1_ffn_gamma', 'L1_ffn_beta']


def kernel(**inputs):
    import numpy as _np
    import concourse.bacc as _bacc
    from concourse import mybir as _mybir
    from concourse.bass_utils import run_bass_kernel_spmd as _run

    nc = _bacc.Bacc("TRN2", target_bir_lowering=False, num_devices=1)
    arrays, args = {}, []
    for name in _INS:
        a = _np.ascontiguousarray(inputs[name])
        arrays[f"in_{name}"] = a
        args.append(nc.dram_tensor(f"in_{name}", a.shape, _mybir.dt.from_np(a.dtype), kind="ExternalInput").ap())
    args.append(nc.dram_tensor("out_0", (N, D), F32, kind="ExternalOutput").ap())
    gps_kernel(nc, *args)
    r = _run(nc, [arrays], core_ids=[0])
    return r.results[0]["out_0"]
```
